# Optimizing a Trainium2 kernel written in Bass

```python
import numpy as np
import jax
import jax.numpy as jnp

def _softmax(x, axis=-1):
    return jax.nn.softmax(x, axis=axis)

def _gelu(x):
    return jax.nn.gelu(x, approximate=True)

def _silu(x):
    return jax.nn.silu(x)

def _sigmoid(x):
    return jax.nn.sigmoid(x)

def _layernorm(x, axis=-1, eps=1e-05):
    m = jnp.mean(x, axis=axis, keepdims=True)
    v = jnp.var(x, axis=axis, keepdims=True)
    return (x - m) / jnp.sqrt(v + eps)

def _scatter_add(tgt, idx, src, axis=0):
    return tgt.at[idx].add(src)

def _segment_sum(src, seg, n):
    return jax.ops.segment_sum(src, seg, n)
kernel_name = 'mk_gnn_preln_d2_gnn_r8_a943b3'

def setup_inputs(seed: int=0):
    np.random.seed(seed)
    _w = jnp.asarray

    def _rec_inputs():
        import jax
        import jax.numpy as jnp
        _gk = jax.random.key(seed)
        x = -6.415e-05 + 1 * jax.random.normal(jax.random.fold_in(_gk, 1), (1250, 512), jnp.float32)
        src = jax.random.randint(jax.random.fold_in(_gk, 2), (20000,), 0, 1250, jnp.int32)
        dst = jnp.minimum((1250 * jax.random.uniform(jax.random.fold_in(_gk, 3), (20000,)) ** 2.0).astype(jnp.int32), 9999)
        _o = jnp.argsort(dst, stable=True)
        src = src[_o]
        dst = dst[_o]
        edge_attr_64 = 0.000279952 + 1.00013 * jax.random.normal(jax.random.fold_in(_gk, 13), (20000, 64), jnp.float32)
        return (x, src, dst, edge_attr_64)
    x, src, dst, edge_attr_64 = _rec_inputs()

    def _L0_gnn_setup():
        import jax, jax.numpy as jnp
        import numpy as np
        N_NODES = 2500
        N_EDGES = 40000
        HIDDEN = 512
        EDGE_DIM = 64
        LN_EPS = 1e-05

        def mish(x):
            return x * jnp.tanh(jax.nn.softplus(x))
        key = jax.random.key(seed)
        ks = jax.random.split(key, 8)
        s = lambda fan_in: 1.0 / np.sqrt(fan_in)
        return {'x': jax.random.normal(ks[0], (N_NODES, HIDDEN), dtype=jnp.float32), 'edge_index': jax.random.randint(ks[1], (2, N_EDGES), 0, N_NODES, dtype=jnp.int64), 'edge_attr': jax.random.normal(ks[2], (N_EDGES, EDGE_DIM), dtype=jnp.float32), 'W1': jax.random.normal(ks[3], (2 * HIDDEN + EDGE_DIM, HIDDEN), dtype=jnp.float32) * s(2 * HIDDEN + EDGE_DIM), 'b1': jnp.zeros((HIDDEN,), dtype=jnp.float32), 'W2': jax.random.normal(ks[4], (HIDDEN, HIDDEN), dtype=jnp.float32) * s(HIDDEN), 'b2': jnp.zeros((HIDDEN,), dtype=jnp.float32), 'W3': jax.random.normal(ks[5], (2 * HIDDEN, HIDDEN), dtype=jnp.float32) * s(2 * HIDDEN), 'b3': jnp.zeros((HIDDEN,), dtype=jnp.float32), 'W4': jax.random.normal(ks[6], (HIDDEN, HIDDEN), dtype=jnp.float32) * s(HIDDEN), 'b4': jnp.zeros((HIDDEN,), dtype=jnp.float32), 'gamma': jnp.ones((HIDDEN,), dtype=jnp.float32), 'beta': jnp.zeros((HIDDEN,), dtype=jnp.float32)}
    _L0_gnn_all = _L0_gnn_setup()
    _L0_gnn_in = {k: v for k, v in _L0_gnn_all.items() if k in ('W1', 'b1', 'W2', 'b2', 'W3', 'b3', 'W4', 'b4', 'gamma', 'beta')}
    del _L0_gnn_all

    def _L1_gnn_setup():
        import jax, jax.numpy as jnp
        import numpy as np
        N_NODES = 1250
        N_EDGES = 20000
        IN_DIM = 512
        OUT_DIM = 512
        LN_EPS = 1e-05
        key = jax.random.key(seed)
        k_x, k_src, k_ws, k_wn = jax.random.split(key, 4)
        x = jax.random.normal(k_x, (N_NODES, IN_DIM), dtype=jnp.float32)
        edge_src = jax.random.randint(k_src, (N_EDGES,), 0, N_NODES, dtype=jnp.int32)
        edge_dst = jnp.repeat(jnp.arange(N_NODES, dtype=jnp.int32), N_EDGES // N_NODES)
        deg = jnp.full((N_NODES,), float(N_EDGES // N_NODES), dtype=jnp.float32)
        scale = 1.0 / np.sqrt(IN_DIM)
        W_self = jax.random.normal(k_ws, (OUT_DIM, IN_DIM), dtype=jnp.float32) * scale
        W_neigh = jax.random.normal(k_wn, (OUT_DIM, IN_DIM), dtype=jnp.float32) * scale
        bias = jnp.zeros((OUT_DIM,), dtype=jnp.float32)
        gamma = jnp.ones((OUT_DIM,), dtype=jnp.float32)
        beta = jnp.zeros((OUT_DIM,), dtype=jnp.float32)
        return {'x': x, 'edge_src': edge_src, 'edge_dst': edge_dst, 'deg': deg, 'W_self': W_self, 'W_neigh': W_neigh, 'bias': bias, 'gamma': gamma, 'beta': beta}
    _L1_gnn_all = _L1_gnn_setup()
    _L1_gnn_in = {k: v for k, v in _L1_gnn_all.items() if k in ('W_self', 'W_neigh', 'bias', 'gamma', 'beta')}
    del _L1_gnn_all
    return {'x': x, 'src': src, 'dst': dst, 'edge_attr_64': edge_attr_64, 'L0_gnn_W1': _L0_gnn_in['W1'], 'L0_gnn_b1': _L0_gnn_in['b1'], 'L0_gnn_W2': _L0_gnn_in['W2'], 'L0_gnn_b2': _L0_gnn_in['b2'], 'L0_gnn_W3': _L0_gnn_in['W3'], 'L0_gnn_b3': _L0_gnn_in['b3'], 'L0_gnn_W4': _L0_gnn_in['W4'], 'L0_gnn_b4': _L0_gnn_in['b4'], 'L0_gnn_gamma': _L0_gnn_in['gamma'], 'L0_gnn_beta': _L0_gnn_in['beta'], 'L1_gnn_W_self': _L1_gnn_in['W_self'], 'L1_gnn_W_neigh': _L1_gnn_in['W_neigh'], 'L1_gnn_bias': _L1_gnn_in['bias'], 'L1_gnn_gamma': _L1_gnn_in['gamma'], 'L1_gnn_beta': _L1_gnn_in['beta']}

def reference(x, src, dst, edge_attr_64, L0_gnn_W1, L0_gnn_b1, L0_gnn_W2, L0_gnn_b2, L0_gnn_W3, L0_gnn_b3, L0_gnn_W4, L0_gnn_b4, L0_gnn_gamma, L0_gnn_beta, L1_gnn_W_self, L1_gnn_W_neigh, L1_gnn_bias, L1_gnn_gamma, L1_gnn_beta):
    import jax
    import jax.numpy as jnp

    def _L0_gnn_ref(x, edge_index, edge_attr, W1, b1, W2, b2, W3, b3, W4, b4, gamma, beta):
        import jax, jax.numpy as jnp
        import numpy as np
        N_NODES = 2500
        N_EDGES = 40000
        HIDDEN = 512
        EDGE_DIM = 64
        LN_EPS = 1e-05

        def mish(x):
            return x * jnp.tanh(jax.nn.softplus(x))
        src, dst = (edge_index[0], edge_index[1])
        edge_feat = jnp.concatenate([x[src], x[dst], edge_attr], axis=-1)
        h = mish(edge_feat @ W1 + b1)
        messages = mish(h @ W2 + b2)
        agg = jax.ops.segment_sum(messages, dst, num_segments=x.shape[0])
        u = mish(jnp.concatenate([x, agg], axis=-1) @ W3 + b3)
        out = u @ W4 + b4
        y = x + out
        mu = jnp.mean(y, axis=-1, keepdims=True)
        var = jnp.mean(jnp.square(y - mu), axis=-1, keepdims=True)
        return (y - mu) * jax.lax.rsqrt(var + LN_EPS) * gamma + beta

    def _L1_gnn_ref(x, edge_src, edge_dst, deg, W_self, W_neigh, bias, gamma, beta):
        import jax, jax.numpy as jnp
        import numpy as np
        N_NODES = 1250
        N_EDGES = 20000
        IN_DIM = 512
        OUT_DIM = 512
        LN_EPS = 1e-05
        n = x.shape[0]
        h_self = jnp.einsum('nd,od->no', x, W_self)
        neigh_sum = jax.ops.segment_sum(x[edge_src], edge_dst, num_segments=n)
        neigh_mean = neigh_sum / jnp.maximum(deg, 1.0)[:, None]
        h_neigh = jnp.einsum('nd,od->no', neigh_mean, W_neigh)
        h = h_self + h_neigh + bias
        mu = jnp.mean(h, axis=-1, keepdims=True)
        var = jnp.mean(jnp.square(h - mu), axis=-1, keepdims=True)
        h = (h - mu) * jax.lax.rsqrt(var + LN_EPS)
        return h * gamma + beta
    edge_index = jnp.stack([src, dst])
    deg = jnp.maximum(jax.ops.segment_sum(jnp.ones(dst.shape, jnp.float32), dst, num_segments=1250), 1.0)
    h = jnp.maximum(_layernorm(x, axis=-1), 0.0)
    x = x + _L0_gnn_ref(h, edge_index, edge_attr_64, L0_gnn_W1, L0_gnn_b1, L0_gnn_W2, L0_gnn_b2, L0_gnn_W3, L0_gnn_b3, L0_gnn_W4, L0_gnn_b4, L0_gnn_gamma, L0_gnn_beta)
    h = jnp.maximum(_layernorm(x, axis=-1), 0.0)
    x = x + _L1_gnn_ref(h, src, dst, deg, L1_gnn_W_self, L1_gnn_W_neigh, L1_gnn_bias, L1_gnn_gamma, L1_gnn_beta)
    return x

_drawn_inputs = setup_inputs


def setup_inputs(seed=0):
    import zlib

    import numpy as np

    out = dict(_drawn_inputs(seed))
    spreads = {'L0_gnn_b1': (0.0, 0.1),
     'L0_gnn_b2': (0.0, 0.1),
     'L0_gnn_b3': (0.0, 0.273),
     'L0_gnn_b4': (0.0, 0.1),
     'L0_gnn_gamma': (1.0, 0.2),
     'L0_gnn_beta': (0.0, 0.1),
     'L1_gnn_bias': (0.0, 0.1),
     'L1_gnn_gamma': (1.0, 0.2),
     'L1_gnn_beta': (0.0, 0.1)}
    factors = {}
    for name, (base, spread) in spreads.items():
        noise = np.random.default_rng([zlib.crc32(name.encode()), seed]).standard_normal(out[name].shape)
        drawn = base * np.exp(spread * noise) if base else spread * noise
        out[name] = jnp.asarray(drawn.astype(out[name].dtype))
    for name, factor in factors.items():
        out[name] = (out[name] * factor).astype(out[name].dtype)
    return out
```

```python
from contextlib import ExitStack

import numpy as np

import concourse.bass as bass
from concourse import mybir

F32 = mybir.dt.float32
F32R = mybir.dt.float32r
I32 = mybir.dt.int32
ALU = mybir.AluOpType
ACT = mybir.ActivationFunctionType
AX = mybir.AxisListType

P = 128
D = 512
C = D // P
DE = 64
N_NODES = 1250
N_EDGES = 20000
NT = -(-N_NODES // P)
NP = NT * P
NG = NT // 2
ET = -(-N_EDGES // P)
ET += ET % 2
EP = ET * P
PAIRS = ET // 2
GW = 2 * P
LAST_BASE = NP - P
EPS = 1e-5
EXP_CAP = float(2.0 ** 30)
Z_CAP = 20.0
LN2 = float(np.log(2.0))
SET_NAME = "natural_log_exp_and_others"
W_ORDER = ["W1a", "W1b", "W3a", "W2", "W3b", "W4", "Ws", "Wn"]
W_SLOT = {"W1a": 0, "W1b": 1, "W3a": 2, "W2": 3, "W3b": 0, "W4": 1, "Ws": 2, "Wn": 3}


def build(nc, x, src_t, dst_t, dst_r, ea_t, ident_d, iota_d, w, v, out):
    assert NT % 2 == 0 and PAIRS % 2 == 1 and PAIRS >= 7

    def scratch(name, shape, dt=F32):
        return nc.dram_tensor(name, shape, dt, kind="Internal").ap()

    tab_a = scratch("tab_a", [NP, D])
    tab_b = scratch("tab_b", [NP, D])
    tab_h = scratch("tab_h", [NP, D])
    tab_h2 = scratch("tab_h2", [NP, D])
    base_d = scratch("base_d", [1, ET], I32)
    span_d = scratch("span_d", [1, ET], I32)

    ctx = ExitStack()
    with ctx:
        top = [-(-nc.sbuf_base // 64) * 64]

        def sb(name, shape, dt=F32):
            size = int(np.prod(shape[1:])) * 4
            t = nc.alloc_sbuf_tensor_at(name, shape, dt, offset=top[0])
            top[0] += -(-size // 64) * 64
            assert top[0] <= nc.sbuf_usable_end, (name, top[0])
            return t

        def sem(name):
            return ctx.enter_context(nc.semaphore(name))

        w_hi = [sb(f"w_hi{i}", [P, C, D], F32R) for i in range(4)]
        w_lo = [sb(f"w_lo{i}", [P, C, D], F32R) for i in range(4)]
        w_raw = [sb(f"w_raw{i}", [P, C, D]) for i in range(2)]
        w1c_hi = sb("w1c_hi", [P, D], F32R)
        w1c_lo = sb("w1c_lo", [P, D], F32R)
        aggT = sb("aggT", [P, C + 1, NP])
        keep = sb("keep", [P, NG, 4 * GW])
        vec = {k: sb(f"vec_{k}", [P, D]) for k in ("b4", "gamma0", "beta0", "bias1", "gamma1", "beta1")}
        b3col = sb("b3col", [P, C])
        b2rows = sb("b2rows", [P, D], F32R)
        ones_r = sb("ones_r", [P, P], F32R)
        ones_f = sb("ones_f", [P, P])
        ident = sb("ident", [P, P])
        iota = sb("iota", [P, P])
        windows = sb("windows", [P, NT])
        src_i = sb("src_i", [P, ET], I32)
        dst_i = sb("dst_i", [P, ET], I32)
        dst_f = sb("dst_f", [P, ET])
        dst_rel = sb("dst_rel", [P, ET])
        base_b = sb("base_b", [P, ET], I32)
        span_row = sb("span_row", [1, ET], I32)
        span_max = sb("span_max", [1, 1], I32)
        phase = top[0]

        w1c_raw = sb("w1c_raw", [P, D])
        b2raw = sb("b2raw", [P, D])
        b1b = sb("b1b", [P, D])
        xin = [sb(f"xin{j}", [P, D]) for j in range(2)]
        hout = [sb(f"hout{j}", [P, D]) for j in range(2)]
        hT_hi = sb("hT_hi", [P, C, GW], F32R)
        hT_lo = sb("hT_lo", [P, C, GW], F32R)
        a_sb = [sb(f"a_sb{j}", [P, D]) for j in range(2)]
        b_sb = [sb(f"b_sb{j}", [P, D]) for j in range(2)]
        dr = sb("dr", [PAIRS, 2, P], I32)
        dr_min = sb("dr_min", [PAIRS, 2])
        dr_max = sb("dr_max", [PAIRS, 2])
        dr_base = sb("dr_base", [PAIRS, 2], I32)
        dr_span = sb("dr_span", [PAIRS, 2], I32)
        bn0 = sb("bn0", [P, 2, 6])
        mv0 = sb("mv0", [P, 2, 2])
        rs0 = sb("rs0", [P, 2, 4])

        top[0] = phase
        ga = [[sb(f"ga{q}{j}", [P, D]) for j in range(2)] for q in range(2)]
        gb = [[sb(f"gb{q}{j}", [P, D]) for j in range(2)] for q in range(2)]
        idx_a = [[sb(f"idx_a{q}{j}", [P, 1], I32) for j in range(2)] for q in range(2)]
        idx_b = [[sb(f"idx_b{q}{j}", [P, 1], I32) for j in range(2)] for q in range(2)]
        r1 = sb("r1", [P, 2, D])
        r2 = sb("r2", [P, 2, D])
        h1f = sb("h1f", [P, 2, D])
        h1_hi = [sb(f"h1_hi{q}", [P, C, GW], F32R) for q in range(2)]
        h1_lo = [sb(f"h1_lo{q}", [P, C, GW], F32R) for q in range(2)]
        msg = [sb(f"msg{q}", [P, 2, D]) for q in range(2)]
        ea_raw = [sb(f"ea_raw{q}", [P, GW]) for q in range(2)]
        ea_st = [sb(f"ea_st{q}", [P, GW], F32R) for q in range(2)]
        onehot = [sb(f"onehot{j}", [P, P]) for j in range(4)]
        end1 = top[0]

        top[0] = phase
        x1 = sb("x1", [P, NT, D])
        g_hi = sb("g_hi", [P, C, GW], F32R)
        g_lo = sb("g_lo", [P, C, GW], F32R)
        z3 = sb("z3", [P, 2, D])
        r3 = sb("r3", [P, 2, D])
        u_hi = sb("u_hi", [P, C, GW], F32R)
        u_lo = sb("u_lo", [P, C, GW], F32R)
        xt = [sb(f"xt{j}", [P, D]) for j in range(2)]
        ht = [sb(f"ht{j}", [P, D]) for j in range(2)]
        h2o = [sb(f"h2o{j}", [P, D]) for j in range(2)]
        bn2 = sb("bn2", [P, 2, 6])
        mv2 = sb("mv2", [P, 2, 2])
        rs2 = sb("rs2", [P, 2, 4])
        gr = [z3[:, 0, :], z3[:, 1, :], r3[:, 0, :], r3[:, 1, :]]
        idx_r = [sb(f"idx_r{j}", [P, 1], I32) for j in range(4)]
        one3 = [sb(f"one3{j}", [P, P]) for j in range(2)]

        psum = ctx.enter_context(nc.psum_tensor("psum", [P, 8, D], F32))

        s_const = sem("const_in")
        s_wraw = [sem(f"w_raw_in{i}") for i in range(2)]
        s_xin = [sem(f"x_in{j}") for j in range(2)]
        s_tabh = [sem(f"h_stored{j}") for j in range(2)]
        s_taba = [sem(f"a_stored{j}") for j in range(2)]
        s_tabb = [sem(f"b_stored{j}") for j in range(2)]
        s_based = sem("base_stored")
        s_basein = sem("base_in")
        s_ga = [[sem(f"a_rows{q}{j}") for j in range(2)] for q in range(2)]
        s_gb = [[sem(f"b_rows{q}{j}") for j in range(2)] for q in range(2)]
        s_ea = [sem(f"edge_attr_in{q}") for q in range(2)]
        s_ht2 = [sem(f"node_rows_in{j}") for j in range(2)]
        s_h2st = [sem(f"h2_stored{j}") for j in range(2)]
        s_gr = [sem(f"h2_rows{j}") for j in range(4)]
        s_out = [sem(f"out_stored{j}") for j in range(2)]
        s_b2clear = sem("b2_rows_cleared")
        s_ones = sem("ones_set")
        s_ones_r = sem("ones_r_set")
        s_apart = sem("apart")
        s_b2 = sem("b2_steps")
        s_whi = sem("w_hi_ready")
        s_wlo = sem("w_lo_ready")
        s_ix = sem("index_steps")
        s_bn = sem("ln0_stats")
        s_mv = sem("ln0_moments")
        s_ln = sem("ln0_log")
        s_rstd = sem("ln0_rstd")
        s_nmr = sem("ln0_shift")
        s_h = sem("h_ready")
        s_hTp = sem("hT_in_psum")
        s_hThi = sem("hT_hi_ready")
        s_hT = sem("hT_ready")
        s_aps = sem("a_in_psum")
        s_bps = sem("b_in_psum")
        s_aev = sem("a_copied")
        s_bev = sem("b_copied")
        s_pps = sem("p_in_psum")
        s_pev = sem("p_copied")
        s_idx = sem("gather_index")
        s_eahi = sem("edge_attr_hi")
        s_east = sem("edge_attr_split")
        s_pre1 = sem("z1_in_psum")
        s_e1, s_c1, s_q1, s_l1, s_x1 = (sem(f"mish1_{k}") for k in ("exp", "cap", "square", "log", "quotient"))
        s_h1 = sem("h1_chunks")
        s_h1hi = sem("h1_hi_ready")
        s_h1s = sem("h1_split")
        s_pre2 = sem("z2_in_psum")
        s_e2, s_c2, s_q2, s_l2, s_x2 = (sem(f"mish2_{k}") for k in ("exp", "cap", "square", "log", "quotient"))
        s_msg = sem("messages")
        s_hot = sem("onehot_ready")
        s_seg = sem("segment_in_psum")
        s_agg = sem("segment_added")
        s_edge_done = sem("agg_complete")
        s_pe_edge = sem("pe_edges_done")
        s_ghi = sem("agg_hi")
        s_gs = sem("agg_split")
        s_z3p = sem("z3_in_psum")
        s_z3 = sem("z3_ready")
        s_e3, s_c3, s_q3, s_l3, s_x3 = (sem(f"mish3_{k}") for k in ("exp", "cap", "square", "log", "quotient"))
        s_u = sem("u_ready")
        s_uhi = sem("u_hi_ready")
        s_us = sem("u_split")
        s_o4 = sem("out4_in_psum")
        s_hb = sem("h_plus_b4")
        s_y = sem("y_ready")
        s_bn2 = sem("ln2_stats")
        s_mv2 = sem("ln2_moments")
        s_ln2 = sem("ln2_log")
        s_rstd2 = sem("ln2_rstd")
        s_t2 = sem("ln2_steps")
        s_xb = sem("x_plus_beta")
        s_x1r = sem("x1_ready")
        s_nmr2 = sem("ln3_shift")
        s_h2 = sem("h2_ready")
        s_h2T = sem("h2T_in_psum")
        s_h2hi = sem("h2T_hi")
        s_h2s = sem("h2T_split")
        s_qps = sem("q_in_psum")
        s_q = sem("q_ready")
        s_idx3 = sem("gather3_index")
        s_hot3 = sem("onehot3_ready")
        s_seg3 = sem("segment3_in_psum")
        s_agg3 = sem("segment3_added")
        s_n3 = sem("neighbours_complete")
        s_zero = sem("aggT_cleared")
        s_zero3 = sem("aggT_cleared_again")
        s_deg = sem("degree_steps")
        s_mean = sem("mean_ready")
        s_mhi = sem("mean_hi")
        s_ms = sem("mean_split")
        s_nps = sem("neigh_in_psum")
        s_h4 = sem("h4_ready")
        s_xb4 = sem("x1_plus_beta")
        s_bn4 = sem("ln4_stats")
        s_mv4 = sem("ln4_moments")
        s_ln4 = sem("ln4_log")
        s_rstd4 = sem("ln4_rstd")
        s_t4 = sem("ln4_steps")
        s_res = sem("result_ready")

        block = ctx.enter_context(nc.Block())
        wk = {k: W_ORDER.index(k) for k in W_ORDER}

        def since(eng, s, value):
            if not isinstance(value, int) or value > 0:
                eng.wait_ge(s, value)

        def over_groups(eng, body):
            body(0)
            with eng.Fori(1, NG) as g:
                body(g)

        def apart(eng):
            eng.sem_inc(s_apart, 1)

        def three_pass(pe, o, a_hi, a_lo, b_hi, b_lo, first, last):
            pe.matmul(o, a_hi, b_hi, start=first, stop=False)
            pe.matmul(o, a_hi, b_lo, start=False, stop=False)
            return pe.matmul(o, a_lo, b_hi, start=False, stop=last)

        @block.sync
        def _(sp):
            def load_w(k):
                if k >= 2:
                    sp.wait_ge(s_wlo, k - 1)
                sp.dma_start(w_raw[k % 2][:], w[W_ORDER[k]].rearrange("(c p) n -> p c n", p=P)
                             ).then_inc(s_wraw[k % 2], 16)

            sp.dma_start(ident[:], ident_d).then_inc(s_const, 16)
            for j in range(2):
                sp.dma_start(xin[j][:], x[j * P:(j + 1) * P, :]).then_inc(s_xin[j], 16)
            load_w(0)
            load_w(1)
            sp.dma_start(dr[:], dst_r.rearrange("(a b) e -> a b e", b=2)).then_inc(s_const, 16)
            sp.dma_start(dst_i[:], dst_t).then_inc(s_const, 16)
            sp.dma_start(src_i[:], src_t).then_inc(s_const, 16)
            sp.dma_start(iota[:], iota_d[:, 0:P].partition_broadcast(P)).then_inc(s_const, 16)
            sp.dma_start(windows[:], iota_d[:, P:].partition_broadcast(P)).then_inc(s_const, 16)
            sp.dma_start(b1b[:], v["b1"].partition_broadcast(P)).then_inc(s_const, 16)
            for k in vec:
                sp.dma_start(vec[k][:], v[k].partition_broadcast(P)).then_inc(s_const, 16)
            for c in range(C):
                sp.dma_start(b3col[:, c:c + 1], v["b3"][0, c * P:(c + 1) * P].rearrange("(p a) -> p a", a=1)
                             ).then_inc(s_const, 16)
            for half in range(2):
                sp.dma_start(w1c_raw[half * DE:(half + 1) * DE, :], w["W1c"]).then_inc(s_const, 16)
            sp.wait_ge(s_b2clear, 1)
            for row in (0, 32):
                sp.dma_start(b2raw[row:row + 1, :], v["b2"]).then_inc(s_const, 16)
            load_w(2)
            load_w(3)

            def stores(g, last):
                for j in range(2):
                    n = 2 * g + j
                    sp.wait_ge(s_h, n + 1)
                    sp.dma_start(tab_h[bass.ds(n * P, P), :], hout[j][:]).then_inc(s_tabh[j], 16)
                    if not last:
                        sp.dma_start(xin[j][:], x[bass.ds((n + 2) * P, P), :]).then_inc(s_xin[j], 16)
                for j in range(2):
                    n = 2 * g + j
                    sp.wait_ge(s_aev, n + 1)
                    sp.dma_start(tab_a[bass.ds(n * P, P), :], a_sb[j][:]).then_inc(s_taba[j], 16)
                    sp.wait_ge(s_bev, n + 1)
                    sp.dma_start(tab_b[bass.ds(n * P, P), :], b_sb[j][:]).then_inc(s_tabb[j], 16)

            sp.wait_ge(s_ix, 5)
            sp.dma_start(base_d.rearrange("o (a b) -> (o a) b", b=2), dr_base[:]).then_inc(s_based, 16)
            sp.dma_start(span_d.rearrange("o (a b) -> (o a) b", b=2), dr_span[:]).then_inc(s_based, 16)
            sp.wait_ge(s_based, 32)
            sp.dma_start(base_b[:], base_d.partition_broadcast(P)).then_inc(s_basein, 16)
            sp.dma_start(span_row[:], span_d).then_inc(s_basein, 16)

            with sp.Fori(0, NG - 1) as g:
                stores(g, False)
            stores(NG - 1, True)

            def load_ea(m, c):
                p = 2 * m + c
                for half in range(2):
                    sp.dma_start(ea_raw[c % 2][half * DE:(half + 1) * DE, :],
                                 ea_t[:, bass.ds(p * GW, GW)]).then_inc(s_ea[c % 2], 16)

            sp.wait_ge(s_pev, NG)
            for j in range(2):
                sp.wait_ge(s_taba[j], 16 * NG)
                sp.wait_ge(s_tabb[j], 16 * NG)
                sp.wait_ge(s_tabh[j], 16 * NG)
            load_ea(0, 0)
            load_ea(0, 1)
            for k in (4, 5, 6):
                load_w(k)
            with sp.Fori(1, (PAIRS - 1) // 2) as m:
                for c in range(2):
                    sp.wait_ge(s_east, 2 * m + c - 1)
                    load_ea(m, c)
            sp.wait_ge(s_east, PAIRS - 2)
            load_ea((PAIRS - 1) // 2, 0)

            load_w(7)
            sp.wait_ge(s_edge_done, 1)
            sp.wait_ge(s_pe_edge, 1)

            def rows_in(g):
                for j in range(2):
                    n = 2 * g + j
                    sp.dma_start(xt[j][:], x[bass.ds(n * P, P), :]).then_inc(s_ht2[j], 16)
                    sp.dma_start(ht[j][:], tab_h[bass.ds(n * P, P), :]).then_inc(s_ht2[j], 16)

            def h2_out(g):
                for j in range(2):
                    n = 2 * g + j
                    sp.wait_ge(s_h2, n + 1)
                    sp.dma_start(tab_h2[bass.ds(n * P, P), :], h2o[j][:]).then_inc(s_h2st[j], 16)

            rows_in(0)
            with sp.Fori(0, NG - 1) as g:
                h2_out(g)
                sp.wait_ge(s_x1r, 2 * g + 2)
                rows_in(g + 1)
            h2_out(NG - 1)

            with sp.Fori(0, NG) as g:
                for j in range(2):
                    n = 2 * g + j
                    sp.wait_ge(s_res, n + 1)
                    sp.dma_start(out[bass.ds(n * P, P), :], ht[j][:]).then_inc(s_out[j], 16)
            for j in range(2):
                sp.wait_ge(s_out[j], 16 * NG)
                sp.wait_ge(s_h2st[j], 16 * NG)

        @block.gpsimd
        def _(pool):
            pool.memset(b2raw[:], 0.0).then_inc(s_b2clear, 1)
            pool.memset(ones_f[:], 1.0).then_inc(s_ones, 1)
            pool.memset(aggT[:], 0.0).then_inc(s_zero, 1)

            def split_w(k):
                slot = W_SLOT[W_ORDER[k]]
                pool.wait_ge(s_whi, k + 1)
                pool.tensor_tensor(w_lo[slot][:], w_raw[k % 2][:], w_hi[slot][:].bitcast(F32),
                                   ALU.subtract).then_inc(s_wlo, 1)

            for k in range(4):
                split_w(k)

            def gather(m, c):
                p = 2 * m + c
                q = c % 2
                for j in range(2):
                    pool.tensor_copy(idx_a[q][j][:], src_i[:, bass.ds(2 * p + j, 1)])
                    pool.tensor_copy(idx_b[q][j][:], dst_i[:, bass.ds(2 * p + j, 1)]).then_inc(s_idx, 1)
                pool.wait_ge(s_idx, 2 * p + 2)
                apart(pool)
                for j in range(2):
                    pool.indirect_dma_start(
                        out=ga[q][j][:], out_offset=None, in_=tab_a,
                        in_offset=bass.IndirectOffsetOnAxis(ap=idx_a[q][j][:], axis=0)).then_inc(s_ga[q][j], 16)
                    pool.indirect_dma_start(
                        out=gb[q][j][:], out_offset=None, in_=tab_b,
                        in_offset=bass.IndirectOffsetOnAxis(ap=idx_b[q][j][:], axis=0)).then_inc(s_gb[q][j], 16)

            for j in range(2):
                pool.wait_ge(s_tabh[j], 16 * NG)
                pool.wait_ge(s_taba[j], 16 * NG)
                pool.wait_ge(s_tabb[j], 16 * NG)
            pool.wait_ge(s_pev, NG)
            gather(0, 0)
            gather(0, 1)
            for k in (4, 5, 6):
                split_w(k)

            def h1_low(m, c):
                p = 2 * m + c
                pool.wait_ge(s_h1hi, p + 1)
                pool.tensor_tensor(h1_lo[c % 2][:], h1f[:].rearrange("p a b -> p (a b)").rearrange(
                    "p (c e) -> p c e", c=C), h1_hi[c % 2][:].bitcast(F32), ALU.subtract).then_inc(s_h1s, 1)

            def step(m, c, more=True):
                p = 2 * m + c
                if more:
                    pool.wait_ge(s_pre1, p + 1)
                    gather(m, c + 2)
                h1_low(m, c)

            with pool.Fori(0, (PAIRS - 3) // 2) as m:
                step(m, 0)
                step(m, 1)
            step((PAIRS - 3) // 2, 0)
            step((PAIRS - 3) // 2, 1, False)
            step((PAIRS - 1) // 2, 0, False)

            split_w(7)

            with pool.Fori(0, NG) as g:
                for j in range(2):
                    n = 2 * g + j
                    pool.wait_ge(s_ht2[j], 32 * g + 32)
                    pool.tensor_tensor(ht[j][:], ht[j][:], vec["b4"][:], ALU.add).then_inc(s_hb, 1)
                    pool.tensor_tensor(xt[j][:], xt[j][:], vec["beta0"][:], ALU.add).then_inc(s_xb, 1)

            for j in range(2):
                pool.wait_ge(s_h2st[j], 16 * NG)

            def gather3(t, j):
                pool.tensor_copy(idx_r[j][:], src_i[:, bass.ds(t, 1)]).then_inc(s_idx3, 1)
                pool.wait_ge(s_idx3, t + 1)
                apart(pool)
                pool.indirect_dma_start(
                    out=gr[j], out_offset=None, in_=tab_h2,
                    in_offset=bass.IndirectOffsetOnAxis(ap=idx_r[j][:], axis=0)).then_inc(s_gr[j], 16)

            for j in range(4):
                gather3(j, j)
            with pool.Fori(1, ET // 4) as k:
                for j in range(4):
                    pool.wait_ge(s_seg3, 4 * k + j - 3)
                    gather3(4 * k + j, j)
            for j in range(ET % 4):
                t = ET // 4 * 4 + j
                pool.wait_ge(s_seg3, t - 3)
                gather3(t, j)

            with pool.Fori(0, NT) as n:
                pool.tensor_tensor(x1[:, bass.ds(n, 1), :].rearrange("p a d -> p (a d)"),
                                   x1[:, bass.ds(n, 1), :].rearrange("p a d -> p (a d)"),
                                   vec["beta1"][:], ALU.add).then_inc(s_xb4, 1)

        @block.scalar
        def _(act):
            act.preload_act_table_set(SET_NAME)

            def nodes0(g):
                for j in range(2):
                    n = 2 * g + j
                    act.wait_ge(s_mv, n + 1)
                    act.activation(rs0[:, j, 0:1], mv0[:, j, 1:2], ACT.Ln, bias=EPS).then_inc(s_ln, 1)
                    act.wait_ge(s_ln, n + 1)
                    act.activation(rs0[:, j, 1:2], rs0[:, j, 0:1], ACT.Exp, scale=-0.5).then_inc(s_rstd, 1)
                    act.wait_ge(s_nmr, n + 1)
                    since(act, s_tabh[j], 16 * g)
                    act.activation(hout[j][:], xin[j][:], ACT.Relu, bias=rs0[:, j, 2:3],
                                   scale=rs0[:, j, 1:2]).then_inc(s_h, 1)
                for j in range(2):
                    n = 2 * g + j
                    act.wait_ge(s_aps, n + 1)
                    since(act, s_taba[j], 16 * g)
                    act.activation(a_sb[j][:], psum[:, 2 + j, :], ACT.Copy).then_inc(s_aev, 1)
                act.wait_ge(s_pps, g + 1)
                for c in range(C):
                    ins = act.activation(keep[:, bass.ds(g, 1), c * GW:(c + 1) * GW].rearrange("p a d -> p (a d)"),
                                         psum[:, 6 + c // 2, (c % 2) * GW:(c % 2 + 1) * GW],
                                         ACT.Identity, bias=b3col[:, c:c + 1])
                ins.then_inc(s_pev, 1)

            over_groups(act, nodes0)

            def e1(m, c):
                act.wait_ge(s_pre1, 2 * m + c + 1)
                act.activation(r1[:], psum[:, 0:2, :], ACT.Exp).then_inc(s_e1, 1)

            def sq1(m, c):
                act.wait_ge(s_c1, 2 * m + c + 1)
                act.activation(r1[:], r1[:], ACT.Square, bias=1.0).then_inc(s_q1, 1)

            def ln1(m, c):
                act.wait_ge(s_q1, 2 * m + c + 1)
                act.activation(r1[:], r1[:], ACT.Ln, bias=1.0).then_inc(s_l1, 1)

            def x1q(m, c):
                act.wait_ge(s_l1, 2 * m + c + 1)
                act.activation(r1[:], r1[:], ACT.Exp, bias=LN2, scale=-1.0).then_inc(s_x1, 1)

            def e2(m, c):
                act.wait_ge(s_pre2, 2 * (2 * m + c) + 2)
                q = c % 2
                act.activation(r2[:], psum[:, 2 + 2 * q:4 + 2 * q, :], ACT.Exp, scale=-1.0).then_inc(s_e2, 1)

            def sq2(m, c):
                act.wait_ge(s_c2, 2 * m + c + 1)
                act.activation(r2[:], r2[:], ACT.Square, bias=1.0).then_inc(s_q2, 1)

            def ln2(m, c):
                act.wait_ge(s_q2, 2 * m + c + 1)
                act.activation(r2[:], r2[:], ACT.Ln, bias=1.0).then_inc(s_l2, 1)

            def x2q(m, c):
                act.wait_ge(s_l2, 2 * m + c + 1)
                act.activation(r2[:], r2[:], ACT.Exp, bias=LN2, scale=-1.0).then_inc(s_x2, 1)

            def step(m, c, first=False, last=False):
                if not last:
                    e1(m, c + 1)
                if not first:
                    x2q(m, c - 1)
                if not last:
                    sq1(m, c + 1)
                    ln1(m, c + 1)
                if not first:
                    act.wait_ge(s_msg, 2 * (2 * m + c))
                e2(m, c)
                if not last:
                    x1q(m, c + 1)
                sq2(m, c)
                ln2(m, c)

            e1(0, 0)
            sq1(0, 0)
            ln1(0, 0)
            x1q(0, 0)
            step(0, 0, first=True)
            with act.Fori(0, (PAIRS - 3) // 2) as m:
                step(m, 1)
                step(m, 2)
            step((PAIRS - 3) // 2, 1)
            step((PAIRS - 3) // 2, 2, last=True)
            x2q((PAIRS - 3) // 2, 2)

            def rstd(n, j, s_m, s_l, s_r, k):
                act.wait_ge(s_m, k)
                act.activation(rs2[:, j, 0:1], mv2[:, j, 1:2], ACT.Ln, bias=EPS).then_inc(s_l, 1)
                act.wait_ge(s_l, k)
                act.activation(rs2[:, j, 1:2], rs2[:, j, 0:1], ACT.Exp, scale=-0.5).then_inc(s_r, 1)

            def nodes2(g):
                act.wait_ge(s_c3, g + 1)
                act.activation(r3[:], r3[:], ACT.Exp).then_inc(s_e3, 1)
                act.wait_ge(s_e3, g + 1)
                act.activation(r3[:], r3[:], ACT.Square, bias=1.0).then_inc(s_q3, 1)
                act.wait_ge(s_q3, g + 1)
                act.activation(r3[:], r3[:], ACT.Ln, bias=1.0).then_inc(s_l3, 1)
                act.wait_ge(s_l3, g + 1)
                act.activation(r3[:], r3[:], ACT.Exp, bias=LN2, scale=-1.0).then_inc(s_x3, 1)
                for j in range(2):
                    n = 2 * g + j
                    rstd(n, j, s_mv2, s_ln2, s_rstd2, 2 * n + 1)
                    rstd(n, j, s_mv2, s_ln2, s_rstd2, 2 * n + 2)
                    act.wait_ge(s_nmr2, n + 1)
                    since(act, s_h2st[j], 16 * g)
                    act.activation(h2o[j][:], x1[:, bass.ds(n, 1), :].rearrange("p a d -> p (a d)"), ACT.Relu,
                                   bias=rs2[:, j, 2:3], scale=rs2[:, j, 1:2]).then_inc(s_h2, 1)

            over_groups(act, nodes2)

            with act.Fori(0, NG) as g:
                for j in range(2):
                    rstd(None, j, s_mv4, s_ln4, s_rstd4, 2 * g + j + 1)

        @block.vector
        def _(dve):
            dve.memset(ones_r[:].bitcast(F32), 1.0).then_inc(s_ones_r, 1)

            def split_w(k):
                slot = W_SLOT[W_ORDER[k]]
                dve.wait_ge(s_wraw[k % 2], 16 * (k // 2 + 1))
                dve.tensor_copy(w_hi[slot][:], w_raw[k % 2][:]).then_inc(s_whi, 1)

            N_CONST = 16 * (1 + 3 + 2 + 1 + len(vec) + C + 2 + 2)

            def ln0(g, j):
                n = 2 * g + j
                dve.wait_ge(s_xin[j], 16 * g + 16)
                apart(dve)
                dve.bn_stats(bn0[:, j, :], xin[j][:]).then_inc(s_bn, 1)
                dve.wait_ge(s_bn, n + 1)
                apart(dve)
                dve.bn_aggr(mv0[:, j, :], bn0[:, j, :]).then_inc(s_mv, 1)
                dve.wait_ge(s_rstd, n + 1)
                dve.wait_ge(s_mv, n + 1)
                dve.tensor_scalar(rs0[:, j, 2:3], mv0[:, j, 0:1], -1.0, rs0[:, j, 1:2],
                                  ALU.mult, ALU.mult).then_inc(s_nmr, 1)

            def node_group(g):
                for j in range(2):
                    ln0(g, j)
                for j in range(2):
                    n = 2 * g + j
                    dve.wait_ge(s_hTp, n + 1)
                    since(dve, s_pps, g)
                    pt = psum[:, j, :].rearrange("p (c e) -> p c e", c=C)
                    dve.tensor_copy(hT_hi[:, :, j * P:(j + 1) * P], pt).then_inc(s_hThi, 1)
                    dve.wait_ge(s_hThi, n + 1)
                    dve.tensor_tensor(hT_lo[:, :, j * P:(j + 1) * P], pt,
                                      hT_hi[:, :, j * P:(j + 1) * P].bitcast(F32), ALU.subtract).then_inc(s_hT, 1)
                for j in range(2):
                    n = 2 * g + j
                    dve.wait_ge(s_bps, n + 1)
                    since(dve, s_tabb[j], 16 * g)
                    dve.tensor_tensor(b_sb[j][:], psum[:, 4 + j, :], b1b[:], ALU.add).then_inc(s_bev, 1)

            split_w(0)
            split_w(1)
            dve.wait_ge(s_const, N_CONST)
            dve.tensor_reduce(dr_min[:], dr[:], AX.X, ALU.min).then_inc(s_ix, 1)
            dve.tensor_reduce(dr_max[:], dr[:], AX.X, ALU.max).then_inc(s_ix, 1)
            dve.wait_ge(s_ix, 2)
            dve.tensor_scalar(dr_min[:], dr_min[:], float(LAST_BASE), None, ALU.min).then_inc(s_ix, 1)
            dve.wait_ge(s_ix, 3)
            dve.tensor_copy(dr_base[:], dr_min[:]).then_inc(s_ix, 1)
            dve.tensor_tensor(dr_span[:], dr_max[:], dr_min[:], ALU.subtract).then_inc(s_ix, 1)
            dve.tensor_copy(w1c_hi[:], w1c_raw[:]).then_inc(s_b2, 1)
            dve.tensor_scalar(b2rows[:], b2raw[:], -1.0, None, ALU.mult).then_inc(s_b2, 1)
            dve.wait_ge(s_b2, 2)
            dve.tensor_tensor(w1c_lo[:], w1c_raw[:], w1c_hi[:].bitcast(F32), ALU.subtract).then_inc(s_b2, 1)
            dve.scalar_tensor_tensor(b2rows[32:64, :], b2raw[32:64, :], -1.0, b2rows[32:64, :].bitcast(F32),
                                     ALU.mult, ALU.subtract).then_inc(s_b2, 1)
            split_w(2)
            split_w(3)
            over_groups(dve, node_group)

            dve.wait_ge(s_basein, 32)
            dve.tensor_reduce(span_max[:], span_row[:], AX.X, ALU.max).then_inc(s_ix, 1)
            dve.tensor_copy(dst_f[:], dst_i[:]).then_inc(s_ix, 1)
            dve.wait_ge(s_ix, 7)
            dve.tensor_tensor(dst_rel[:], dst_f[:], base_b[:], ALU.subtract).then_inc(s_ix, 1)
            dve.wait_ge(s_ix, 8)
            dve.wait_ge(s_pps, NG)

            def ea_split(m, c):
                q = c % 2
                p = 2 * m + c
                dve.wait_ge(s_ea[q], 32 * (m + c // 2) + 32)
                dve.tensor_copy(ea_st[q][:], ea_raw[q][:]).then_inc(s_eahi, 1)
                dve.wait_ge(s_eahi, p + 1)
                dve.tensor_tensor(ea_st[q][DE:P, :], ea_raw[q][DE:P, :], ea_st[q][DE:P, :].bitcast(F32),
                                  ALU.subtract).then_inc(s_east, 1)

            def cap1(m, c):
                dve.wait_ge(s_e1, 2 * m + c + 1)
                dve.tensor_scalar(r1[:], r1[:], EXP_CAP, None, ALU.min).then_inc(s_c1, 1)

            def cap2(m, c):
                dve.wait_ge(s_e2, 2 * m + c + 1)
                dve.tensor_scalar(r2[:], r2[:], EXP_CAP, None, ALU.min).then_inc(s_c2, 1)

            def tail1(m, c, first=False):
                p = 2 * m + c
                dve.wait_ge(s_x1, p + 1)
                since(dve, s_h1s, p)
                for b in range(2):
                    dve.scalar_tensor_tensor(h1f[:, b, :], r1[:, b, :], 1.0, psum[:, b, :],
                                             ALU.subtract, ALU.mult).then_inc(s_h1, 1)
                dve.wait_ge(s_h1, 2 * p + 2)
                if not first:
                    dve.wait_ge(s_pre2, 2 * p - 2)
                dve.tensor_copy(h1_hi[c % 2][:].rearrange("p c e -> p (c e)"),
                                h1f[:].rearrange("p a b -> p (a b)")).then_inc(s_h1hi, 1)

            def tail2(m, c, seg_read=None):
                p = 2 * m + c
                dve.wait_ge(s_x2, p + 1)
                if seg_read is not None:
                    dve.wait_ge(s_seg, seg_read)
                for j in range(2):
                    dve.scalar_tensor_tensor(msg[c % 2][:, j, :], r2[:, j, :], 1.0, psum[:, 2 + 2 * (c % 2) + j, :],
                                             ALU.subtract, ALU.mult).then_inc(s_msg, 1)

            def edges(sorted_tiles):
                visits = 1 if sorted_tiles else NT

                def hots(m, c):
                    p = 2 * m + c
                    for j in range(2):
                        dve.tensor_scalar(onehot[2 * (c % 2) + j][:], iota[:, 0:P],
                                          dst_rel[:, bass.ds(2 * p + j, 1)], None, ALU.is_equal).then_inc(s_hot, 1)

                def add(m, c):
                    p = 2 * m + c
                    for j in range(2):
                        t = 2 * p + j
                        base = dve.value_load(base_b[0:1, bass.ds(t, 1)], min_val=0, max_val=LAST_BASE)
                        dve.wait_ge(s_seg, t + 1)
                        dve.wait_ge(s_agg, t)
                        dst = aggT[:, 0:C, bass.ds(base, P)]
                        dve.tensor_tensor(dst, dst, psum[:, 6 + j, :].rearrange("p (c e) -> p c e", c=C),
                                          ALU.add).then_inc(s_agg, 1)

                def every_window(m, c):
                    p = 2 * m + c
                    for j in range(2):
                        t = 2 * p + j
                        with dve.Fori(0, NT // 2) as k:
                            for b in range(2):
                                nth = t * NT + 2 * k + b
                                dve.wait_ge(s_agg, nth + 1)
                                dve.tensor_scalar(onehot[b][:], iota[:], windows[:, bass.ds(2 * k + b, 1)],
                                                  dst_f[:, bass.ds(t, 1)], ALU.add, ALU.is_equal).then_inc(s_hot, 1)
                                dve.wait_ge(s_seg, nth + 1)
                                dst = aggT[:, 0:C, bass.ds((2 * k + b) * P, P)]
                                dve.tensor_tensor(dst, dst, psum[:, 6 + b, :].rearrange("p (c e) -> p c e", c=C),
                                                  ALU.add).then_inc(s_agg, 1)

                def step(m, c, first=False, second=False, third=False, last=False, ea=True):
                    p = 2 * m + c
                    if not last:
                        cap1(m, c + 1)
                    if not first:
                        tail2(m, c - 1, None if second or third else 2 * visits * (p - 2))
                        if sorted_tiles:
                            hots(m, c - 1)
                    cap2(m, c)
                    if not last:
                        tail1(m, c + 1, first)
                    if not first:
                        (add if sorted_tiles else every_window)(m, c - 1)
                    if ea:
                        ea_split(m, c + 3)

                if not sorted_tiles:
                    dve.sem_inc(s_agg, 1)
                cap1(0, 0)
                tail1(0, 0, first=True)
                step(0, 0, first=True)
                step(0, 1, second=True)
                step(0, 2, third=True)
                with dve.Fori(1, (PAIRS - 5) // 2) as m:
                    step(m, 1)
                    step(m, 2)
                mm = (PAIRS - 5) // 2
                step(mm, 1)
                step(mm, 2, ea=False)
                step(mm, 3, ea=False)
                step(mm, 4, ea=False, last=True)
                tail2(mm, 4, 2 * visits * (PAIRS - 2))
                if sorted_tiles:
                    hots(mm, 4)
                    add(mm, 4)
                else:
                    every_window(mm, 4)
                dve.wait_ge(s_agg, ET * visits + (not sorted_tiles))

            ea_split(0, 0)
            ea_split(0, 1)
            for k in (4, 5, 6):
                split_w(k)
            dve.wait_ge(s_pre1, 1)
            ea_split(0, 2)
            dve.wait_ge(s_zero, 1)
            widest = dve.value_load(span_max[:], min_val=0, max_val=NP)
            with dve.If(widest < P):
                edges(True)
            with dve.Else():
                edges(False)
            split_w(7)
            dve.memset(z3[:, 0, 0:1], 0.0).then_inc(s_edge_done, 1)

            dve.wait_ge(s_edge_done, 1)

            def group2(g):
                since(dve, s_z3p, g)
                src = aggT[:, 0:C, bass.ds(g * GW, GW)]
                dve.tensor_copy(g_hi[:], src).then_inc(s_ghi, 1)
                dve.wait_ge(s_ghi, g + 1)
                dve.tensor_tensor(g_lo[:], src, g_hi[:].bitcast(F32), ALU.subtract).then_inc(s_gs, 1)
                dve.wait_ge(s_z3p, g + 1)
                dve.tensor_tensor(z3[:].rearrange("p a b -> p (a b)"),
                                  keep[:, bass.ds(g, 1), :].rearrange("p a d -> p (a d)"),
                                  psum[:, 0:2, :].rearrange("p a b -> p (a b)"), ALU.add).then_inc(s_z3, 1)
                dve.wait_ge(s_z3, g + 1)
                dve.tensor_scalar(r3[:], z3[:], Z_CAP, None, ALU.min).then_inc(s_c3, 1)
                dve.wait_ge(s_x3, g + 1)
                dve.scalar_tensor_tensor(r3[:], r3[:], 1.0, z3[:], ALU.subtract, ALU.mult).then_inc(s_u, 1)
                dve.wait_ge(s_u, g + 1)
                dve.tensor_copy(u_hi[:].rearrange("p c e -> p (c e)"),
                                r3[:].rearrange("p a b -> p (a b)")).then_inc(s_uhi, 1)
                dve.wait_ge(s_uhi, g + 1)
                dve.tensor_tensor(u_lo[:].rearrange("p c e -> p (c e)"), r3[:].rearrange("p a b -> p (a b)"),
                                  u_hi[:].rearrange("p c e -> p (c e)").bitcast(F32),
                                  ALU.subtract).then_inc(s_us, 1)
                for j in range(2):
                    n = 2 * g + j
                    x1n = x1[:, bass.ds(n, 1), :].rearrange("p a d -> p (a d)")
                    dve.wait_ge(s_o4, n + 1)
                    dve.wait_ge(s_hb, n + 1)
                    dve.tensor_tensor(ht[j][:], ht[j][:], psum[:, 2 + j, :], ALU.subtract).then_inc(s_y, 1)
                    dve.wait_ge(s_y, n + 1)
                    apart(dve)
                    dve.bn_stats(bn2[:, j, :], ht[j][:]).then_inc(s_bn2, 1)
                    dve.wait_ge(s_bn2, 2 * n + 1)
                    apart(dve)
                    dve.bn_aggr(mv2[:, j, :], bn2[:, j, :]).then_inc(s_mv2, 1)
                    dve.wait_ge(s_mv2, 2 * n + 1)
                    dve.wait_ge(s_rstd2, 2 * n + 1)
                    dve.tensor_scalar(ht[j][:], ht[j][:], mv2[:, j, 0:1], rs2[:, j, 1:2],
                                      ALU.subtract, ALU.mult).then_inc(s_t2, 1)
                    dve.wait_ge(s_t2, 2 * n + 1)
                    dve.tensor_tensor(ht[j][:], ht[j][:], vec["gamma0"][:], ALU.mult).then_inc(s_t2, 1)
                    dve.wait_ge(s_t2, 2 * n + 2)
                    dve.wait_ge(s_xb, n + 1)
                    dve.tensor_tensor(x1n, ht[j][:], xt[j][:], ALU.add).then_inc(s_x1r, 1)
                    dve.wait_ge(s_x1r, n + 1)
                    apart(dve)
                    dve.bn_stats(bn2[:, j, :], x1n).then_inc(s_bn2, 1)
                    dve.wait_ge(s_bn2, 2 * n + 2)
                    apart(dve)
                    dve.bn_aggr(mv2[:, j, :], bn2[:, j, :]).then_inc(s_mv2, 1)
                    dve.wait_ge(s_mv2, 2 * n + 2)
                    dve.wait_ge(s_rstd2, 2 * n + 2)
                    dve.tensor_scalar(rs2[:, j, 2:3], mv2[:, j, 0:1], -1.0, rs2[:, j, 1:2],
                                      ALU.mult, ALU.mult).then_inc(s_nmr2, 1)
                for j in range(2):
                    n = 2 * g + j
                    pt = psum[:, 4 + j, :].rearrange("p (c e) -> p c e", c=C)
                    part = slice(j * P, (j + 1) * P)
                    dve.wait_ge(s_h2T, n + 1)
                    dve.tensor_copy(u_hi[:, :, part], pt).then_inc(s_h2hi, 1)
                    dve.wait_ge(s_h2hi, n + 1)
                    dve.tensor_tensor(u_lo[:, :, part], pt, u_hi[:, :, part].bitcast(F32),
                                      ALU.subtract).then_inc(s_h2s, 1)
                for j in range(2):
                    n = 2 * g + j
                    dve.wait_ge(s_qps, n + 1)
                    dve.tensor_tensor(keep[:, bass.ds(g, 1), j * D:(j + 1) * D].rearrange("p a d -> p (a d)"),
                                      psum[:, 6 + j, :], vec["bias1"][:], ALU.add).then_inc(s_q, 1)

            over_groups(dve, group2)

            dve.memset(aggT[:], 0.0).then_inc(s_zero3, 1)
            dve.wait_ge(s_zero3, 1)

            def seg3(b):
                return psum[:, 2 * b:2 * b + 2, :].rearrange("p a b -> p (a b)")[:, 0:(C + 1) * P].rearrange(
                    "p (c e) -> p c e", c=C + 1)

            def neighbours(sorted_tiles):
                if sorted_tiles:
                    def hot(t, j):
                        dve.tensor_scalar(one3[j][:], iota[:, 0:P], dst_rel[:, bass.ds(t, 1)], None,
                                          ALU.is_equal).then_inc(s_hot3, 1)

                    def add(t, j):
                        base = dve.value_load(base_b[0:1, bass.ds(t, 1)], min_val=0, max_val=LAST_BASE)
                        dve.wait_ge(s_seg3, t + 1)
                        dve.wait_ge(s_agg3, t)
                        dst = aggT[:, :, bass.ds(base, P)]
                        dve.tensor_tensor(dst, dst, seg3(j), ALU.add).then_inc(s_agg3, 1)

                    hot(0, 0)
                    hot(1, 1)
                    with dve.Fori(0, ET // 2 - 1) as k:
                        for j in range(2):
                            add(2 * k + j, j)
                            hot(2 * k + 2 + j, j)
                    add(ET - 2, 0)
                    add(ET - 1, 1)
                    dve.wait_ge(s_agg3, ET)
                else:
                    dve.sem_inc(s_agg3, 1)
                    with dve.Fori(0, ET) as t:
                        with dve.Fori(0, NT // 2) as k:
                            for b in range(2):
                                nth = t * NT + 2 * k + b
                                dve.wait_ge(s_agg3, nth + 1)
                                dve.tensor_scalar(one3[b][:], iota[:], windows[:, bass.ds(2 * k + b, 1)],
                                                  dst_f[:, bass.ds(t, 1)], ALU.add, ALU.is_equal).then_inc(s_hot3, 1)
                                dve.wait_ge(s_deg, nth + 1)
                                dst = aggT[:, :, bass.ds((2 * k + b) * P, P)]
                                dve.tensor_tensor(dst, dst, seg3(b), ALU.add).then_inc(s_agg3, 1)
                    dve.wait_ge(s_agg3, ET * NT + 1)

            with dve.If(widest < P):
                neighbours(True)
            with dve.Else():
                neighbours(False)

            deg = aggT[:, C, :]
            dve.wait_ge(s_n3, 1)
            dve.tensor_scalar(deg, deg, 1.0, None, ALU.max).then_inc(s_mean, 1)
            dve.wait_ge(s_mean, 1)
            dve.reciprocal(deg, deg).then_inc(s_mean, 1)
            dve.wait_ge(s_mean, 2)
            for c in range(C):
                dve.tensor_tensor(aggT[:, c, :], aggT[:, c, :], deg, ALU.mult).then_inc(s_mean, 1)
            dve.wait_ge(s_mean, 2 + C)

            def nodes4(g):
                part = aggT[:, 0:C, bass.ds(g * GW, GW)]
                since(dve, s_nps, 2 * g)
                dve.tensor_copy(g_hi[:], part).then_inc(s_mhi, 1)
                dve.wait_ge(s_mhi, g + 1)
                dve.tensor_tensor(g_lo[:], part, g_hi[:].bitcast(F32), ALU.subtract).then_inc(s_ms, 1)
                for j in range(2):
                    n = 2 * g + j
                    dve.wait_ge(s_nps, n + 1)
                    since(dve, s_out[j], 16 * g)
                    dve.tensor_tensor(ht[j][:], psum[:, 4 + j, :],
                                      keep[:, bass.ds(g, 1), j * D:(j + 1) * D].rearrange("p a d -> p (a d)"),
                                      ALU.add).then_inc(s_h4, 1)
                    dve.wait_ge(s_h4, n + 1)
                    apart(dve)
                    dve.bn_stats(bn2[:, j, :], ht[j][:]).then_inc(s_bn4, 1)
                    dve.wait_ge(s_bn4, n + 1)
                    apart(dve)
                    dve.bn_aggr(mv2[:, j, :], bn2[:, j, :]).then_inc(s_mv4, 1)
                    dve.wait_ge(s_mv4, n + 1)
                    dve.wait_ge(s_rstd4, n + 1)
                    dve.tensor_scalar(ht[j][:], ht[j][:], mv2[:, j, 0:1], rs2[:, j, 1:2],
                                      ALU.subtract, ALU.mult).then_inc(s_t4, 1)
                    dve.wait_ge(s_t4, 2 * n + 1)
                    dve.tensor_tensor(ht[j][:], ht[j][:], vec["gamma1"][:], ALU.mult).then_inc(s_t4, 1)
                    dve.wait_ge(s_t4, 2 * n + 2)
                    dve.wait_ge(s_xb4, n + 1)
                    dve.tensor_tensor(ht[j][:], ht[j][:], x1[:, bass.ds(n, 1), :].rearrange("p a d -> p (a d)"),
                                      ALU.add).then_inc(s_res, 1)

            over_groups(dve, nodes4)

        @block.tensor
        def _(pe):
            def square(o, lhs_hi, lhs_lo, name, e0, first=True, last=True):
                slot = W_SLOT[name]
                for c in range(C):
                    cols = slice(e0, e0 + P)
                    mm = three_pass(pe, o, lhs_hi[:, c, cols], lhs_lo[:, c, cols], w_hi[slot][:, c, :],
                                    w_lo[slot][:, c, :], first and c == 0, last and c == C - 1)
                return mm

            def turned(bank, name, rhs_hi, rhs_lo):
                slot = W_SLOT[name]
                for f in range(C):
                    o = psum[:, bank + f // 2, (f % 2) * GW:(f % 2 + 1) * GW]
                    for c in range(C):
                        cols = slice(f * P, (f + 1) * P)
                        mm = three_pass(pe, o, w_hi[slot][:, c, cols], w_lo[slot][:, c, cols], rhs_hi[:, c, :],
                                        rhs_lo[:, c, :], c == 0, c == C - 1)
                return mm

            pe.wait_ge(s_const, 16 * (1 + 3 + 2 + 1 + len(vec) + C + 2 + 2))
            def nodes0(g):
                for j in range(2):
                    n = 2 * g + j
                    pe.wait_ge(s_h, n + 1)
                    since(pe, s_hT, 2 * g)
                    for c in range(C):
                        tr = pe.transpose(psum[:, j, c * P:(c + 1) * P], hout[j][:, c * P:(c + 1) * P], ident[:])
                    tr.then_inc(s_hTp, 1)
                for j in range(2):
                    n = 2 * g + j
                    pe.wait_ge(s_hT, n + 1)
                    pe.wait_ge(s_wlo, 1)
                    since(pe, s_aev, 2 * g)
                    square(psum[:, 2 + j, :], hT_hi, hT_lo, "W1a", j * P).then_inc(s_aps, 1)
                    pe.wait_ge(s_wlo, 2)
                    since(pe, s_bev, 2 * g)
                    square(psum[:, 4 + j, :], hT_hi, hT_lo, "W1b", j * P).then_inc(s_bps, 1)
                pe.wait_ge(s_wlo, 3)
                since(pe, s_pev, g)
                turned(6, "W3a", hT_hi, hT_lo).then_inc(s_pps, 1)

            over_groups(pe, nodes0)

            pe.wait_ge(s_wlo, 4)
            pe.wait_ge(s_b2, 4)
            pe.wait_ge(s_ones, 1)
            pe.wait_ge(s_ones_r, 1)

            def z1(m, c, first=False):
                p = 2 * m + c
                q = c % 2
                use = m + c // 2 + 1
                pe.wait_ge(s_east, p + 1)
                for j in range(2):
                    pe.wait_ge(s_ga[q][j], 16 * use)
                    pe.wait_ge(s_gb[q][j], 16 * use)
                for f in range(C):
                    if not first and f % 2 == 0:
                        pe.wait_ge(s_h1, 2 * p - 1 + f // 2)
                    cols = slice(f * P, (f + 1) * P)
                    at = (f % 2) * GW
                    o = psum[:, f // 2, at:at + GW]
                    pe.matmul(o, w1c_hi[:, cols], ea_st[q][:], start=True, stop=False)
                    pe.matmul(o, w1c_lo[:, cols], ea_st[q][:], start=False, stop=False)
                    for j in range(2):
                        oj = psum[:, f // 2, at + j * P:at + (j + 1) * P]
                        pe.matmul(oj, ga[q][j][:, cols], ident[:], is_transpose=True, start=False, stop=False)
                        mm = pe.matmul(oj, gb[q][j][:, cols], ident[:], is_transpose=True, start=False, stop=j == 1)
                mm.then_inc(s_pre1, 1)

            def z2(m, c, early=False):
                p = 2 * m + c
                q = c % 2
                pe.wait_ge(s_h1s, p + 1)
                if not early:
                    pe.wait_ge(s_msg, 2 * p - 2)
                for j in range(2):
                    o = psum[:, 2 + 2 * q + j, :]
                    pe.matmul(o, ones_r[:], b2rows[:], start=True, stop=False)
                    square(o, h1_hi[q], h1_lo[q], "W2", j * P, first=False).then_inc(s_pre2, 1)

            def edges(sorted_tiles):
                def sums(m, c, first=False):
                    p = 2 * m + c
                    q = c % 2
                    for j in range(2):
                        t = 2 * p + j
                        pe.wait_ge(s_msg, t + 1)
                        pe.wait_ge(s_hot, t + 1)
                        if not first:
                            pe.wait_ge(s_agg, t - 1)
                        for f in range(C):
                            mm = pe.matmul(psum[:, 6 + j, f * P:(f + 1) * P], msg[q][:, j, f * P:(f + 1) * P],
                                           onehot[2 * q + j][:], start=True, stop=True)
                        mm.then_inc(s_seg, 1)

                def every_window(m, c, first=False):
                    p = 2 * m + c
                    q = c % 2
                    for j in range(2):
                        t = 2 * p + j
                        pe.wait_ge(s_msg, t + 1)
                        apart(pe)
                        with pe.Fori(0, NT // 2) as k:
                            for b in range(2):
                                pe.wait_ge(s_hot, t * NT + 2 * k + b + 1)
                                for f in range(C):
                                    mm = pe.matmul(psum[:, 6 + b, f * P:(f + 1) * P],
                                                   msg[q][:, j, f * P:(f + 1) * P], onehot[b][:],
                                                   start=True, stop=True)
                                mm.then_inc(s_seg, 1)

                add_up = sums if sorted_tiles else every_window

                def step(m, c, more=True):
                    z2(m, c)
                    add_up(m, c - 1)
                    if more:
                        z1(m, c + 2)

                z1(0, 1)
                z2(0, 0, early=True)
                z1(0, 2)
                z2(0, 1, early=True)
                add_up(0, 0, first=True)
                z1(0, 3)
                with pe.Fori(1, (PAIRS - 3) // 2) as m:
                    step(m, 0)
                    step(m, 1)
                mm = (PAIRS - 3) // 2
                step(mm, 0)
                step(mm, 1, more=False)
                step(mm, 2, more=False)
                add_up(mm, 2)

            z1(0, 0, first=True)
            pe.wait_ge(s_ix, 6)
            widest = pe.value_load(span_max[:], min_val=0, max_val=NP)
            with pe.If(widest < P):
                edges(True)
            with pe.Else():
                edges(False)
            pe.sem_inc(s_pe_edge, 1)

            pe.wait_ge(s_wlo, 5)
            def nodes2(g):
                pe.wait_ge(s_gs, g + 1)
                since(pe, s_z3, g)
                turned(0, "W3b", g_hi, g_lo).then_inc(s_z3p, 1)
                pe.wait_ge(s_us, g + 1)
                pe.wait_ge(s_wlo, 6)
                for j in range(2):
                    since(pe, s_y, 2 * g)
                    square(psum[:, 2 + j, :], u_hi, u_lo, "W4", j * P).then_inc(s_o4, 1)
                for j in range(2):
                    pe.wait_ge(s_h2, 2 * g + j + 1)
                    since(pe, s_h2s, 2 * g)
                    for c in range(C):
                        tr = pe.transpose(psum[:, 4 + j, c * P:(c + 1) * P], h2o[j][:, c * P:(c + 1) * P], ident[:])
                    tr.then_inc(s_h2T, 1)
                pe.wait_ge(s_wlo, 7)
                for j in range(2):
                    pe.wait_ge(s_h2s, 2 * g + j + 1)
                    since(pe, s_q, 2 * g)
                    square(psum[:, 6 + j, :], u_hi, u_lo, "Ws", j * P).then_inc(s_qps, 1)

            over_groups(pe, nodes2)

            def sum3(j, b):
                for f in range(C):
                    pe.matmul(psum[:, 2 * b, f * P:(f + 1) * P], gr[j][:, f * P:(f + 1) * P], one3[b][:],
                              start=True, stop=True)
                return pe.matmul(psum[:, 2 * b + 1, 0:P], ones_f[:], one3[b][:], start=True, stop=True)

            pe.wait_ge(s_q, NT)

            def tile3(t, j, use, later=True):
                pe.wait_ge(s_gr[j], 16 * use)
                pe.wait_ge(s_hot3, t + 1)
                if later:
                    pe.wait_ge(s_agg3, t - 1)
                sum3(j, j % 2).then_inc(s_seg3, 1)

            def neighbours(sorted_tiles):
                if sorted_tiles:
                    for j in range(4):
                        tile3(j, j, 1, j >= 2)
                    with pe.Fori(1, ET // 4) as k:
                        for j in range(4):
                            tile3(4 * k + j, j, k + 1)
                    for j in range(ET % 4):
                        tile3(ET // 4 * 4 + j, j, ET // 4 + 1)
                else:
                    def windows(t, j, use):
                        pe.wait_ge(s_gr[j], 16 * use)
                        apart(pe)
                        with pe.Fori(0, NT // 2) as k:
                            for b in range(2):
                                pe.wait_ge(s_hot3, t * NT + 2 * k + b + 1)
                                sum3(j, b).then_inc(s_deg, 1)
                        pe.wait_ge(s_deg, t * NT + NT)
                        pe.sem_inc(s_seg3, 1)

                    with pe.Fori(0, ET // 4) as k:
                        for j in range(4):
                            windows(4 * k + j, j, k + 1)
                    for j in range(ET % 4):
                        windows(ET // 4 * 4 + j, j, ET // 4 + 1)

            with pe.If(widest < P):
                neighbours(True)
            with pe.Else():
                neighbours(False)
            pe.sem_inc(s_n3, 1)

            pe.wait_ge(s_wlo, 8)
            def nodes4(g):
                pe.wait_ge(s_ms, g + 1)
                for j in range(2):
                    since(pe, s_h4, 2 * g)
                    square(psum[:, 4 + j, :], g_hi, g_lo, "Wn", j * P).then_inc(s_nps, 1)

            over_groups(pe, nodes4)


def kernel(x, src, dst, edge_attr_64, L0_gnn_W1, L0_gnn_b1, L0_gnn_W2, L0_gnn_b2, L0_gnn_W3, L0_gnn_b3,
           L0_gnn_W4, L0_gnn_b4, L0_gnn_gamma, L0_gnn_beta, L1_gnn_W_self, L1_gnn_W_neigh, L1_gnn_bias,
           L1_gnn_gamma, L1_gnn_beta):
    import concourse.bacc as bacc
    from concourse.bass_utils import run_bass_kernel_spmd

    W1, W3 = np.asarray(L0_gnn_W1), np.asarray(L0_gnn_W3)
    row = lambda a: np.ascontiguousarray(np.asarray(a).reshape(1, -1))
    pad_edges = EP - N_EDGES
    src_p = np.concatenate([np.asarray(src), np.zeros(pad_edges, np.int32)])
    dst_p = np.concatenate([np.asarray(dst), np.full(pad_edges, N_NODES, np.int32)])
    ea = np.concatenate([np.asarray(edge_attr_64), np.zeros((pad_edges, DE), np.float32)])
    arrays = {
        "x": np.concatenate([np.asarray(x), np.zeros((NP - N_NODES, D), np.float32)]),
        "src_t": np.ascontiguousarray(src_p.reshape(ET, P).T),
        "dst_t": np.ascontiguousarray(dst_p.reshape(ET, P).T),
        "dst_r": np.ascontiguousarray(dst_p.reshape(ET, P)),
        "ea_t": np.ascontiguousarray(ea.T),
        "ident_d": np.eye(P, dtype=np.float32),
        "iota_d": np.concatenate([np.arange(P), P * np.arange(NT)]).astype(np.float32).reshape(1, -1),
    }
    weights = {
        "W1a": W1[0:D], "W1b": W1[D:2 * D], "W1c": W1[2 * D:], "W2": L0_gnn_W2, "W3a": W3[0:D], "W3b": W3[D:],
        "W4": L0_gnn_W4, "Ws": np.asarray(L1_gnn_W_self).T, "Wn": np.asarray(L1_gnn_W_neigh).T,
    }
    vectors = {
        "b1": L0_gnn_b1, "b2": L0_gnn_b2, "b3": L0_gnn_b3, "b4": L0_gnn_b4, "gamma0": L0_gnn_gamma,
        "beta0": L0_gnn_beta, "bias1": L1_gnn_bias, "gamma1": L1_gnn_gamma, "beta1": L1_gnn_beta,
    }
    arrays.update({f"w_{k}": np.ascontiguousarray(a) for k, a in weights.items()})
    arrays.update({f"v_{k}": row(a) for k, a in vectors.items()})

    nc = bacc.Bacc("TRN2", target_bir_lowering=False, num_devices=1)
    aps = {k: nc.dram_tensor(k, a.shape, mybir.dt.from_np(a.dtype), kind="ExternalInput").ap()
           for k, a in arrays.items()}
    out = nc.dram_tensor("out", [NP, D], F32, kind="ExternalOutput").ap()
    build(nc, aps["x"], aps["src_t"], aps["dst_t"], aps["dst_r"], aps["ea_t"], aps["ident_d"], aps["iota_d"],
          {k: aps[f"w_{k}"] for k in weights}, {k: aps[f"v_{k}"] for k in vectors}, out)
    result = run_bass_kernel_spmd(nc, [arrays], core_ids=[0])
    return result.results[0]["out"][:N_NODES]
```

```python
from contextlib import ExitStack

import numpy as np

import concourse.bass as bass
from concourse import mybir

F32 = mybir.dt.float32
F32R = mybir.dt.float32r
I32 = mybir.dt.int32
BF16 = mybir.dt.bfloat16
ALU = mybir.AluOpType
ACT = mybir.ActivationFunctionType
AX = mybir.AxisListType

P = 128
D = 512
C = D // P
DE = 64
N_NODES = 1250
N_EDGES = 20000
NT = -(-N_NODES // P)
NP = NT * P
NG = NT // 2
ET = -(-N_EDGES // P)
ET += ET % 2
EP = ET * P
PAIRS = ET // 2
QUADS = -(-ET // 4)
LAST_QUAD = ET - 4 * (QUADS - 1)
GW = 2 * P
LAST_BASE = NP - P
EPS = 1e-5
EXP_CAP = float(2.0 ** 30)
Z_CAP = 20.0
LN2 = float(np.log(2.0))
SET_NAME = "natural_log_exp_and_others"
W_ORDER = ["W1a", "W1b", "W3a", "W2", "W3b", "W4", "Ws", "Wn"]
W_SLOT = {"W1a": 0, "W1b": 1, "W3a": 2, "W2": 3, "W3b": 0, "W4": 1, "Ws": 2, "Wn": 3}


def build(nc, x, src_t, dst_t, dst_r, ea_t, ident_d, iota_d, w, v, out):
    assert NT % 2 == 0 and PAIRS % 2 == 1 and PAIRS >= 7 and QUADS % 2 == 0

    def scratch(name, shape, dt=F32):
        return nc.dram_tensor(name, shape, dt, kind="Internal").ap()

    tab_a = scratch("tab_a", [NP, D])
    tab_b = scratch("tab_b", [NP, D])
    tab_h = scratch("tab_h", [NP, D])
    tab_h2 = scratch("tab_h2", [NP, D])
    base_d = scratch("base_d", [1, QUADS], I32)
    span_d = scratch("span_d", [1, QUADS], I32)

    ctx = ExitStack()
    with ctx:
        top = [-(-nc.sbuf_base // 64) * 64]

        def sb(name, shape, dt=F32):
            size = int(np.prod(shape[1:])) * (2 if dt == BF16 else 4)
            t = nc.alloc_sbuf_tensor_at(name, shape, dt, offset=top[0])
            top[0] += -(-size // 64) * 64
            assert top[0] <= nc.sbuf_usable_end, (name, top[0])
            return t

        def sem(name):
            return ctx.enter_context(nc.semaphore(name))

        w_hi = [sb(f"w_hi{i}", [P, C, D], F32R) for i in range(4)]
        w_lo = [sb(f"w_lo{i}", [P, C, D], F32R) for i in range(4)]
        w_raw = [sb(f"w_raw{i}", [P, C, D]) for i in range(2)]
        w1c_hi = sb("w1c_hi", [P, D], F32R)
        w1c_lo = sb("w1c_lo", [P, D], F32R)
        aggT = sb("aggT", [P, C + 1, NP])
        keep = sb("keep", [P, NG, 4 * GW])
        vec = {k: sb(f"vec_{k}", [P, D]) for k in ("b4", "gamma0", "beta0", "bias1", "gamma1", "beta1")}
        b3col = sb("b3col", [P, C])
        b2rows = sb("b2rows", [P, D], F32R)
        ones_r = sb("ones_r", [P, P], F32R)
        ones_b = sb("ones_b", [P, P], BF16)
        ident = sb("ident", [P, P])
        iota = sb("iota", [P, P])
        windows = sb("windows", [P, NT])
        src_i = sb("src_i", [P, 4 * QUADS], I32)
        dst_i = sb("dst_i", [P, 4 * QUADS], I32)
        dst_f = sb("dst_f", [P, 4 * QUADS])
        dst_rel = sb("dst_rel", [P, 4 * QUADS])
        base_b = sb("base_b", [P, QUADS], I32)
        span_row = sb("span_row", [1, QUADS], I32)
        span_max = sb("span_max", [1, 1], I32)
        phase = top[0]

        w1c_raw = sb("w1c_raw", [P, D])
        b2raw = sb("b2raw", [P, D])
        b1b = sb("b1b", [P, D])
        xin = [sb(f"xin{j}", [P, D]) for j in range(2)]
        hout = [sb(f"hout{j}", [P, D]) for j in range(2)]
        hT_hi = sb("hT_hi", [P, C, GW], F32R)
        hT_lo = sb("hT_lo", [P, C, GW], F32R)
        a_sb = [sb(f"a_sb{j}", [P, D]) for j in range(2)]
        b_sb = [sb(f"b_sb{j}", [P, D]) for j in range(2)]
        dr = sb("dr", [QUADS, 4 * P], I32)
        dr_min = sb("dr_min", [QUADS, 1])
        dr_max = sb("dr_max", [QUADS, 1])
        dr_base = sb("dr_base", [QUADS, 1], I32)
        dr_span = sb("dr_span", [QUADS, 1], I32)
        bn0 = sb("bn0", [P, 2, 6])
        mv0 = sb("mv0", [P, 2, 2])
        rs0 = sb("rs0", [P, 2, 4])

        top[0] = phase
        ga = [sb(f"ga{q}", [P, 2, D]) for q in range(2)]
        gb = [sb(f"gb{q}", [P, 2, D]) for q in range(2)]
        idx_ab = [sb(f"idx_ab{q}", [P, 4], I32) for q in range(2)]
        r1 = sb("r1", [P, 2, D])
        r2 = [sb(f"r2{q}", [P, 2, D]) for q in range(2)]
        h1f = sb("h1f", [P, 2, D])
        h1_hi = [sb(f"h1_hi{q}", [P, C, GW], F32R) for q in range(2)]
        h1_lo = [sb(f"h1_lo{q}", [P, C, GW], F32R) for q in range(2)]
        ea_raw = [sb(f"ea_raw{q}", [P, GW]) for q in range(2)]
        ea_st = [sb(f"ea_st{q}", [P, GW], F32R) for q in range(2)]
        onehot = [sb(f"onehot{j}", [P, P]) for j in range(4)]
        end1 = top[0]

        top[0] = phase
        x1 = sb("x1", [P, NT, D])
        g_hi = sb("g_hi", [P, C, GW], F32R)
        g_lo = sb("g_lo", [P, C, GW], F32R)
        z3 = sb("z3", [P, 2, D])
        r3 = sb("r3", [P, 2, D])
        u_hi = sb("u_hi", [P, C, GW], F32R)
        u_lo = sb("u_lo", [P, C, GW], F32R)
        xt = [sb(f"xt{j}", [P, D]) for j in range(2)]
        ht = [sb(f"ht{j}", [P, D]) for j in range(2)]
        h2o = [sb(f"h2o{j}", [P, D]) for j in range(2)]
        bn2 = sb("bn2", [P, 2, 6])
        mv2 = sb("mv2", [P, 2, 2])
        rs2 = sb("rs2", [P, 2, 4])
        gr = [a[:, j, :] for a in (z3, r3) for j in range(2)]
        gr += [a[:].bitcast(F32).rearrange("p c e -> p (c e)")[:, j * D:(j + 1) * D]
               for a in (g_hi, g_lo) for j in range(2)]
        idx_r = [sb(f"idx_r{h}", [P, 4], I32) for h in range(2)]
        one3 = [sb(f"one3{j}", [P, P]) for j in range(4)]
        count3 = [sb(f"count3{j}", [P, P], BF16) for j in range(4)]

        psum = ctx.enter_context(nc.psum_tensor("psum", [P, 8, D], F32))

        s_const = sem("const_in")
        s_wraw = [sem(f"w_raw_in{i}") for i in range(2)]
        s_xin = [sem(f"x_in{j}") for j in range(2)]
        s_tabh = [sem(f"h_stored{j}") for j in range(2)]
        s_taba = [sem(f"a_stored{j}") for j in range(2)]
        s_tabb = [sem(f"b_stored{j}") for j in range(2)]
        s_based = sem("base_stored")
        s_basein = sem("base_in")
        s_ga = [[sem(f"a_rows{q}{j}") for j in range(2)] for q in range(2)]
        s_gb = [[sem(f"b_rows{q}{j}") for j in range(2)] for q in range(2)]
        s_ea = [sem(f"edge_attr_in{q}") for q in range(2)]
        s_ht2 = [sem(f"node_rows_in{j}") for j in range(2)]
        s_h2st = [sem(f"h2_stored{j}") for j in range(2)]
        s_gr = [sem(f"h2_rows{j}") for j in range(8)]
        s_out = [sem(f"out_stored{j}") for j in range(2)]
        s_b2clear = sem("b2_rows_cleared")
        s_ones = sem("ones_set")
        s_ones_r = sem("ones_r_set")
        s_apart = sem("apart")
        s_b2 = sem("b2_steps")
        s_whi = sem("w_hi_ready")
        s_wlo = sem("w_lo_ready")
        s_ix = sem("index_steps")
        s_bn = sem("ln0_stats")
        s_mv = sem("ln0_moments")
        s_ln = sem("ln0_log")
        s_rstd = sem("ln0_rstd")
        s_nmr = sem("ln0_shift")
        s_h = sem("h_ready")
        s_hTp = sem("hT_in_psum")
        s_hThi = sem("hT_hi_ready")
        s_hT = sem("hT_ready")
        s_aps = sem("a_in_psum")
        s_bps = sem("b_in_psum")
        s_aev = sem("a_copied")
        s_bev = sem("b_copied")
        s_pps = sem("p_in_psum")
        s_pev = sem("p_copied")
        s_idx = sem("gather_index")
        s_eahi = sem("edge_attr_hi")
        s_east = sem("edge_attr_split")
        s_ab = sem("a_plus_b")
        s_pre1 = sem("z1_in_psum")
        s_e1, s_c1, s_q1, s_l1, s_x1 = (sem(f"mish1_{k}") for k in ("exp", "cap", "square", "log", "quotient"))
        s_h1 = sem("h1_chunks")
        s_h1hi = sem("h1_hi_ready")
        s_h1s = sem("h1_split")
        s_pre2 = sem("z2_in_psum")
        s_e2, s_c2, s_q2, s_l2, s_x2 = (sem(f"mish2_{k}") for k in ("exp", "cap", "square", "log", "quotient"))
        s_msg = sem("messages")
        s_hot = sem("onehot_ready")
        s_seg = sem("segment_in_psum")
        s_agg = sem("segment_added")
        s_edge_done = sem("agg_complete")
        s_pe_edge = sem("pe_edges_done")
        s_ghi = sem("agg_hi")
        s_gs = sem("agg_split")
        s_z3p = sem("z3_in_psum")
        s_z3 = sem("z3_ready")
        s_e3, s_c3, s_q3, s_l3, s_x3 = (sem(f"mish3_{k}") for k in ("exp", "cap", "square", "log", "quotient"))
        s_u = sem("u_ready")
        s_uhi = sem("u_hi_ready")
        s_us = sem("u_split")
        s_o4 = sem("out4_in_psum")
        s_hb = sem("h_plus_b4")
        s_y = sem("y_ready")
        s_bn2 = sem("ln2_stats")
        s_mv2 = sem("ln2_moments")
        s_ln2 = sem("ln2_log")
        s_rstd2 = sem("ln2_rstd")
        s_t2 = sem("ln2_steps")
        s_xb = sem("x_plus_beta")
        s_x1r = sem("x1_ready")
        s_nmr2 = sem("ln3_shift")
        s_h2 = sem("h2_ready")
        s_h2T = sem("h2T_in_psum")
        s_h2hi = sem("h2T_hi")
        s_h2s = sem("h2T_split")
        s_qps = sem("q_in_psum")
        s_q = sem("q_ready")
        s_idx3 = sem("gather3_index")
        s_hot3 = sem("onehot3_ready")
        s_seg3 = sem("segment3_in_psum")
        s_agg3 = sem("segment3_added")
        s_n3 = sem("neighbours_complete")
        s_zero = sem("aggT_cleared")
        s_zero3 = sem("aggT_cleared_again")
        s_deg = sem("degree_steps")
        s_mean = sem("mean_ready")
        s_mhi = sem("mean_hi")
        s_ms = sem("mean_split")
        s_nps = sem("neigh_in_psum")
        s_h4 = sem("h4_ready")
        s_xb4 = sem("x1_plus_beta")
        s_bn4 = sem("ln4_stats")
        s_mv4 = sem("ln4_moments")
        s_ln4 = sem("ln4_log")
        s_rstd4 = sem("ln4_rstd")
        s_t4 = sem("ln4_steps")
        s_res = sem("result_ready")

        block = ctx.enter_context(nc.Block())
        wk = {k: W_ORDER.index(k) for k in W_ORDER}

        def since(eng, s, value):
            if not isinstance(value, int) or value > 0:
                eng.wait_ge(s, value)

        def over_groups(eng, body):
            body(0)
            with eng.Fori(1, NG) as g:
                body(g)

        def apart(eng):
            eng.sem_inc(s_apart, 1)

        def three_pass(pe, o, a_hi, a_lo, b_hi, b_lo, first, last):
            pe.matmul(o, a_hi, b_hi, start=first, stop=False)
            pe.matmul(o, a_hi, b_lo, start=False, stop=False)
            return pe.matmul(o, a_lo, b_hi, start=False, stop=last)

        @block.sync
        def _(sp):
            def load_w(k):
                if k >= 2:
                    sp.wait_ge(s_wlo, k - 1)
                sp.dma_start(w_raw[k % 2][:], w[W_ORDER[k]].rearrange("(c p) n -> p c n", p=P)
                             ).then_inc(s_wraw[k % 2], 16)

            sp.dma_start(ident[:], ident_d).then_inc(s_const, 16)
            for j in range(2):
                sp.dma_start(xin[j][:], x[j * P:(j + 1) * P, :]).then_inc(s_xin[j], 16)
            load_w(0)
            load_w(1)
            sp.dma_start(dr[:], dst_r).then_inc(s_const, 16)
            sp.dma_start(dst_i[:], dst_t).then_inc(s_const, 16)
            sp.dma_start(src_i[:], src_t).then_inc(s_const, 16)
            sp.dma_start(iota[:], iota_d[:, 0:P].partition_broadcast(P)).then_inc(s_const, 16)
            sp.dma_start(windows[:], iota_d[:, P:].partition_broadcast(P)).then_inc(s_const, 16)
            sp.dma_start(b1b[:], v["b1"].partition_broadcast(P)).then_inc(s_const, 16)
            for k in vec:
                sp.dma_start(vec[k][:], v[k].partition_broadcast(P)).then_inc(s_const, 16)
            for c in range(C):
                sp.dma_start(b3col[:, c:c + 1], v["b3"][0, c * P:(c + 1) * P].rearrange("(p a) -> p a", a=1)
                             ).then_inc(s_const, 16)
            for half in range(2):
                sp.dma_start(w1c_raw[half * DE:(half + 1) * DE, :], w["W1c"]).then_inc(s_const, 16)
            sp.wait_ge(s_b2clear, 1)
            for row in (0, 32):
                sp.dma_start(b2raw[row:row + 1, :], v["b2"]).then_inc(s_const, 16)
            load_w(2)
            load_w(3)

            def stores(g, last):
                for j in range(2):
                    n = 2 * g + j
                    sp.wait_ge(s_h, n + 1)
                    sp.dma_start(tab_h[bass.ds(n * P, P), :], hout[j][:]).then_inc(s_tabh[j], 16)
                    if not last:
                        sp.dma_start(xin[j][:], x[bass.ds((n + 2) * P, P), :]).then_inc(s_xin[j], 16)
                for j in range(2):
                    n = 2 * g + j
                    sp.wait_ge(s_aev, n + 1)
                    sp.dma_start(tab_a[bass.ds(n * P, P), :], a_sb[j][:]).then_inc(s_taba[j], 16)
                    sp.wait_ge(s_bev, n + 1)
                    sp.dma_start(tab_b[bass.ds(n * P, P), :], b_sb[j][:]).then_inc(s_tabb[j], 16)

            sp.wait_ge(s_ix, 5)
            sp.dma_start(base_d.rearrange("o (a b) -> (o a) b", b=1), dr_base[:]).then_inc(s_based, 16)
            sp.dma_start(span_d.rearrange("o (a b) -> (o a) b", b=1), dr_span[:]).then_inc(s_based, 16)
            sp.wait_ge(s_based, 32)
            sp.dma_start(base_b[:], base_d.partition_broadcast(P)).then_inc(s_basein, 16)
            sp.dma_start(span_row[:], span_d).then_inc(s_basein, 16)

            with sp.Fori(0, NG - 1) as g:
                stores(g, False)
            stores(NG - 1, True)

            def load_ea(m, c):
                p = 2 * m + c
                for half in range(2):
                    sp.dma_start(ea_raw[c % 2][half * DE:(half + 1) * DE, :],
                                 ea_t[:, bass.ds(p * GW, GW)]).then_inc(s_ea[c % 2], 16)

            sp.wait_ge(s_pev, NG)
            for j in range(2):
                sp.wait_ge(s_taba[j], 16 * NG)
                sp.wait_ge(s_tabb[j], 16 * NG)
                sp.wait_ge(s_tabh[j], 16 * NG)
            load_ea(0, 0)
            load_ea(0, 1)
            for k in (4, 5, 6):
                load_w(k)
            with sp.Fori(1, (PAIRS - 1) // 2) as m:
                for c in range(2):
                    sp.wait_ge(s_east, 2 * m + c - 1)
                    load_ea(m, c)
            sp.wait_ge(s_east, PAIRS - 2)
            load_ea((PAIRS - 1) // 2, 0)

            load_w(7)
            sp.wait_ge(s_edge_done, 1)
            sp.wait_ge(s_pe_edge, 1)

            def rows_in(g):
                for j in range(2):
                    n = 2 * g + j
                    sp.dma_start(xt[j][:], x[bass.ds(n * P, P), :]).then_inc(s_ht2[j], 16)
                    sp.dma_start(ht[j][:], tab_h[bass.ds(n * P, P), :]).then_inc(s_ht2[j], 16)

            def h2_out(g):
                for j in range(2):
                    n = 2 * g + j
                    sp.wait_ge(s_h2, n + 1)
                    sp.dma_start(tab_h2[bass.ds(n * P, P), :], h2o[j][:]).then_inc(s_h2st[j], 16)

            rows_in(0)
            with sp.Fori(0, NG - 1) as g:
                h2_out(g)
                sp.wait_ge(s_x1r, 2 * g + 2)
                rows_in(g + 1)
            h2_out(NG - 1)

            with sp.Fori(0, NG) as g:
                for j in range(2):
                    n = 2 * g + j
                    sp.wait_ge(s_res, n + 1)
                    sp.dma_start(out[bass.ds(n * P, P), :], ht[j][:]).then_inc(s_out[j], 16)
            for j in range(2):
                sp.wait_ge(s_out[j], 16 * NG)
                sp.wait_ge(s_h2st[j], 16 * NG)

        @block.gpsimd
        def _(pool):
            pool.memset(b2raw[:], 0.0).then_inc(s_b2clear, 1)
            pool.memset(ones_b[:], 1.0).then_inc(s_ones, 1)
            pool.memset(aggT[:], 0.0).then_inc(s_zero, 1)

            def split_w(k):
                slot = W_SLOT[W_ORDER[k]]
                pool.wait_ge(s_whi, k + 1)
                pool.tensor_tensor(w_lo[slot][:], w_raw[k % 2][:], w_hi[slot][:].bitcast(F32),
                                   ALU.subtract).then_inc(s_wlo, 1)

            for k in range(4):
                split_w(k)

            def gather(m, c):
                p = 2 * m + c
                q = c % 2
                pool.tensor_copy(idx_ab[q][:, 0:2], src_i[:, bass.ds(2 * p, 2)]).then_inc(s_idx, 1)
                pool.tensor_copy(idx_ab[q][:, 2:4], dst_i[:, bass.ds(2 * p, 2)]).then_inc(s_idx, 1)
                pool.wait_ge(s_idx, 2 * p + 2)
                apart(pool)
                for j in range(2):
                    pool.indirect_dma_start(
                        out=ga[q][:, j, :], out_offset=None, in_=tab_a,
                        in_offset=bass.IndirectOffsetOnAxis(ap=idx_ab[q][:, j:j + 1], axis=0)
                    ).then_inc(s_ga[q][j], 16)
                    pool.indirect_dma_start(
                        out=gb[q][:, j, :], out_offset=None, in_=tab_b,
                        in_offset=bass.IndirectOffsetOnAxis(ap=idx_ab[q][:, 2 + j:3 + j], axis=0)
                    ).then_inc(s_gb[q][j], 16)

            for j in range(2):
                pool.wait_ge(s_tabh[j], 16 * NG)
                pool.wait_ge(s_taba[j], 16 * NG)
                pool.wait_ge(s_tabb[j], 16 * NG)
            pool.wait_ge(s_pev, NG)
            gather(0, 0)
            gather(0, 1)
            for k in (4, 5, 6):
                split_w(k)

            def h1_low(m, c):
                p = 2 * m + c
                pool.wait_ge(s_h1hi, p + 1)
                pool.tensor_tensor(h1_lo[c % 2][:], h1f[:].rearrange("p a b -> p (a b)").rearrange(
                    "p (c e) -> p c e", c=C), h1_hi[c % 2][:].bitcast(F32), ALU.subtract).then_inc(s_h1s, 1)

            def step(m, c, more=True):
                p = 2 * m + c
                if more:
                    pool.wait_ge(s_pre1, p + 1)
                    gather(m, c + 2)
                h1_low(m, c)

            with pool.Fori(0, (PAIRS - 3) // 2) as m:
                step(m, 0)
                step(m, 1)
            step((PAIRS - 3) // 2, 0)
            step((PAIRS - 3) // 2, 1, False)
            step((PAIRS - 1) // 2, 0, False)

            split_w(7)

            with pool.Fori(0, NG) as g:
                for j in range(2):
                    n = 2 * g + j
                    pool.wait_ge(s_ht2[j], 32 * g + 32)
                    pool.tensor_tensor(ht[j][:], ht[j][:], vec["b4"][:], ALU.add).then_inc(s_hb, 1)
                    pool.tensor_tensor(xt[j][:], xt[j][:], vec["beta0"][:], ALU.add).then_inc(s_xb, 1)

            for j in range(2):
                pool.wait_ge(s_h2st[j], 16 * NG)

            def gather3(quad, h, count=4, first=False):
                t = 4 * quad
                if not first:
                    pool.wait_ge(s_seg3, t - 4)
                pool.tensor_copy(idx_r[h][:, 0:count], src_i[:, bass.ds(t, count)]).then_inc(s_idx3, 1)
                for j in range(count):
                    if j == 0:
                        pool.wait_ge(s_idx3, quad + 1)
                        apart(pool)
                    pool.indirect_dma_start(
                        out=gr[4 * h + j], out_offset=None, in_=tab_h2,
                        in_offset=bass.IndirectOffsetOnAxis(ap=idx_r[h][:, j:j + 1], axis=0)).then_inc(s_gr[4 * h + j], 16)

            gather3(0, 0, first=True)
            gather3(1, 1, first=True)
            with pool.Fori(1, ET // 8) as k:
                for h in range(2):
                    gather3(2 * k + h, h)
            for quad in range(ET // 8 * 2, -(-ET // 4)):
                gather3(quad, quad % 2, min(4, ET - 4 * quad))

            with pool.Fori(0, NT) as n:
                pool.tensor_tensor(x1[:, bass.ds(n, 1), :].rearrange("p a d -> p (a d)"),
                                   x1[:, bass.ds(n, 1), :].rearrange("p a d -> p (a d)"),
                                   vec["beta1"][:], ALU.add).then_inc(s_xb4, 1)

        @block.scalar
        def _(act):
            act.preload_act_table_set(SET_NAME)

            def nodes0(g):
                for j in range(2):
                    n = 2 * g + j
                    act.wait_ge(s_mv, n + 1)
                    act.activation(rs0[:, j, 0:1], mv0[:, j, 1:2], ACT.Ln, bias=EPS).then_inc(s_ln, 1)
                    act.wait_ge(s_ln, n + 1)
                    act.activation(rs0[:, j, 1:2], rs0[:, j, 0:1], ACT.Exp, scale=-0.5).then_inc(s_rstd, 1)
                    act.wait_ge(s_nmr, n + 1)
                    since(act, s_tabh[j], 16 * g)
                    act.activation(hout[j][:], xin[j][:], ACT.Relu, bias=rs0[:, j, 2:3],
                                   scale=rs0[:, j, 1:2]).then_inc(s_h, 1)
                for j in range(2):
                    n = 2 * g + j
                    act.wait_ge(s_aps, n + 1)
                    since(act, s_taba[j], 16 * g)
                    act.activation(a_sb[j][:], psum[:, 2 + j, :], ACT.Copy).then_inc(s_aev, 1)
                act.wait_ge(s_pps, g + 1)
                for c in range(C):
                    ins = act.activation(keep[:, bass.ds(g, 1), c * GW:(c + 1) * GW].rearrange("p a d -> p (a d)"),
                                         psum[:, 6 + c // 2, (c % 2) * GW:(c % 2 + 1) * GW],
                                         ACT.Identity, bias=b3col[:, c:c + 1])
                ins.then_inc(s_pev, 1)

            over_groups(act, nodes0)

            def e1(m, c):
                act.wait_ge(s_pre1, 2 * m + c + 1)
                act.activation(r1[:], psum[:, 0:2, :], ACT.Exp).then_inc(s_e1, 1)

            def sq1(m, c):
                act.wait_ge(s_c1, 2 * m + c + 1)
                act.activation(r1[:], r1[:], ACT.Square, bias=1.0).then_inc(s_q1, 1)

            def ln1(m, c):
                act.wait_ge(s_q1, 2 * m + c + 1)
                act.activation(r1[:], r1[:], ACT.Ln, bias=1.0).then_inc(s_l1, 1)

            def x1q(m, c):
                act.wait_ge(s_l1, 2 * m + c + 1)
                act.activation(r1[:], r1[:], ACT.Exp, bias=LN2, scale=-1.0).then_inc(s_x1, 1)

            def e2(m, c):
                act.wait_ge(s_pre2, 2 * (2 * m + c) + 2)
                q = c % 2
                act.activation(r2[q][:], psum[:, 2 + 2 * q:4 + 2 * q, :], ACT.Exp, scale=-1.0).then_inc(s_e2, 1)

            def sq2(m, c):
                act.wait_ge(s_c2, 2 * m + c + 1)
                act.activation(r2[c % 2][:], r2[c % 2][:], ACT.Square, bias=1.0).then_inc(s_q2, 1)

            def ln2(m, c):
                act.wait_ge(s_q2, 2 * m + c + 1)
                act.activation(r2[c % 2][:], r2[c % 2][:], ACT.Ln, bias=1.0).then_inc(s_l2, 1)

            def x2q(m, c):
                act.wait_ge(s_l2, 2 * m + c + 1)
                act.activation(r2[c % 2][:], r2[c % 2][:], ACT.Exp, bias=LN2, scale=-1.0).then_inc(s_x2, 1)

            def step(m, c):
                e1(m, c + 1)
                sq2(m, c - 1)
                sq1(m, c + 1)
                ln2(m, c - 1)
                ln1(m, c + 1)
                x1q(m, c + 1)
                x2q(m, c - 1)
                e2(m, c)

            for c in range(2):
                e1(0, c)
                sq1(0, c)
                ln1(0, c)
                x1q(0, c)
            e2(0, 0)
            with act.Fori(0, (PAIRS - 3) // 2) as m:
                step(m, 1)
                step(m, 2)
            mm = (PAIRS - 3) // 2
            step(mm, 1)
            for c in (1, 2):
                sq2(mm, c)
                ln2(mm, c)
                x2q(mm, c)
                if c == 1:
                    e2(mm, 2)

            def rstd(n, j, s_m, s_l, s_r, k):
                act.wait_ge(s_m, k)
                act.activation(rs2[:, j, 0:1], mv2[:, j, 1:2], ACT.Ln, bias=EPS).then_inc(s_l, 1)
                act.wait_ge(s_l, k)
                act.activation(rs2[:, j, 1:2], rs2[:, j, 0:1], ACT.Exp, scale=-0.5).then_inc(s_r, 1)

            def nodes2(g):
                act.wait_ge(s_c3, g + 1)
                act.activation(r3[:], r3[:], ACT.Exp).then_inc(s_e3, 1)
                act.wait_ge(s_e3, g + 1)
                act.activation(r3[:], r3[:], ACT.Square, bias=1.0).then_inc(s_q3, 1)
                act.wait_ge(s_q3, g + 1)
                act.activation(r3[:], r3[:], ACT.Ln, bias=1.0).then_inc(s_l3, 1)
                act.wait_ge(s_l3, g + 1)
                act.activation(r3[:], r3[:], ACT.Exp, bias=LN2, scale=-1.0).then_inc(s_x3, 1)
                for j in range(2):
                    n = 2 * g + j
                    rstd(n, j, s_mv2, s_ln2, s_rstd2, 2 * n + 1)
                    rstd(n, j, s_mv2, s_ln2, s_rstd2, 2 * n + 2)
                    act.wait_ge(s_nmr2, n + 1)
                    since(act, s_h2st[j], 16 * g)
                    act.activation(h2o[j][:], x1[:, bass.ds(n, 1), :].rearrange("p a d -> p (a d)"), ACT.Relu,
                                   bias=rs2[:, j, 2:3], scale=rs2[:, j, 1:2]).then_inc(s_h2, 1)

            over_groups(act, nodes2)

            with act.Fori(0, NG) as g:
                for j in range(2):
                    rstd(None, j, s_mv4, s_ln4, s_rstd4, 2 * g + j + 1)

        @block.vector
        def _(dve):
            dve.memset(ones_r[:].bitcast(F32), 1.0).then_inc(s_ones_r, 1)

            def split_w(k):
                slot = W_SLOT[W_ORDER[k]]
                dve.wait_ge(s_wraw[k % 2], 16 * (k // 2 + 1))
                dve.tensor_copy(w_hi[slot][:], w_raw[k % 2][:]).then_inc(s_whi, 1)

            N_CONST = 16 * (1 + 3 + 2 + 1 + len(vec) + C + 2 + 2)

            def ln0(g, j):
                n = 2 * g + j
                dve.wait_ge(s_xin[j], 16 * g + 16)
                apart(dve)
                dve.bn_stats(bn0[:, j, :], xin[j][:]).then_inc(s_bn, 1)
                dve.wait_ge(s_bn, n + 1)
                apart(dve)
                dve.bn_aggr(mv0[:, j, :], bn0[:, j, :]).then_inc(s_mv, 1)
                dve.wait_ge(s_rstd, n + 1)
                dve.wait_ge(s_mv, n + 1)
                dve.tensor_scalar(rs0[:, j, 2:3], mv0[:, j, 0:1], -1.0, rs0[:, j, 1:2],
                                  ALU.mult, ALU.mult).then_inc(s_nmr, 1)

            def node_group(g):
                for j in range(2):
                    ln0(g, j)
                for j in range(2):
                    n = 2 * g + j
                    dve.wait_ge(s_hTp, n + 1)
                    since(dve, s_pps, g)
                    pt = psum[:, j, :].rearrange("p (c e) -> p c e", c=C)
                    dve.tensor_copy(hT_hi[:, :, j * P:(j + 1) * P], pt).then_inc(s_hThi, 1)
                    dve.wait_ge(s_hThi, n + 1)
                    dve.tensor_tensor(hT_lo[:, :, j * P:(j + 1) * P], pt,
                                      hT_hi[:, :, j * P:(j + 1) * P].bitcast(F32), ALU.subtract).then_inc(s_hT, 1)
                for j in range(2):
                    n = 2 * g + j
                    dve.wait_ge(s_bps, n + 1)
                    since(dve, s_tabb[j], 16 * g)
                    dve.tensor_tensor(b_sb[j][:], psum[:, 4 + j, :], b1b[:], ALU.add).then_inc(s_bev, 1)

            split_w(0)
            split_w(1)
            dve.wait_ge(s_const, N_CONST)
            dve.tensor_reduce(dr_min[:], dr[:], AX.X, ALU.min).then_inc(s_ix, 1)
            dve.tensor_reduce(dr_max[:], dr[:], AX.X, ALU.max).then_inc(s_ix, 1)
            dve.wait_ge(s_ix, 2)
            dve.tensor_scalar(dr_min[:], dr_min[:], float(LAST_BASE), None, ALU.min).then_inc(s_ix, 1)
            dve.wait_ge(s_ix, 3)
            dve.tensor_copy(dr_base[:], dr_min[:]).then_inc(s_ix, 1)
            dve.tensor_tensor(dr_span[:], dr_max[:], dr_min[:], ALU.subtract).then_inc(s_ix, 1)
            dve.tensor_copy(w1c_hi[:], w1c_raw[:]).then_inc(s_b2, 1)
            dve.tensor_scalar(b2rows[:], b2raw[:], -1.0, None, ALU.mult).then_inc(s_b2, 1)
            dve.wait_ge(s_b2, 2)
            dve.tensor_tensor(w1c_lo[:], w1c_raw[:], w1c_hi[:].bitcast(F32), ALU.subtract).then_inc(s_b2, 1)
            dve.scalar_tensor_tensor(b2rows[32:64, :], b2raw[32:64, :], -1.0, b2rows[32:64, :].bitcast(F32),
                                     ALU.mult, ALU.subtract).then_inc(s_b2, 1)
            split_w(2)
            split_w(3)
            over_groups(dve, node_group)

            dve.wait_ge(s_basein, 32)
            dve.tensor_reduce(span_max[:], span_row[:], AX.X, ALU.max).then_inc(s_ix, 1)
            dve.tensor_copy(dst_f[:], dst_i[:]).then_inc(s_ix, 1)
            dve.wait_ge(s_ix, 7)
            for j in range(4):
                of_quad = [a[:].rearrange("p (q b) -> p q b", b=4)[:, :, j] for a in (dst_rel, dst_f)]
                dve.tensor_tensor(of_quad[0], of_quad[1], base_b[:], ALU.subtract).then_inc(s_ix, 1)
            dve.wait_ge(s_ix, 11)
            dve.wait_ge(s_pps, NG)

            def ea_split(m, c):
                q = c % 2
                p = 2 * m + c
                dve.wait_ge(s_ea[q], 32 * (m + c // 2) + 32)
                dve.tensor_copy(ea_st[q][:], ea_raw[q][:]).then_inc(s_eahi, 1)
                dve.wait_ge(s_eahi, p + 1)
                dve.tensor_tensor(ea_st[q][DE:P, :], ea_raw[q][DE:P, :], ea_st[q][DE:P, :].bitcast(F32),
                                  ALU.subtract).then_inc(s_east, 1)

            def ab_sum(m, c):
                q = c % 2
                for j in range(2):
                    dve.wait_ge(s_ga[q][j], 16 * (m + c // 2) + 16)
                    dve.wait_ge(s_gb[q][j], 16 * (m + c // 2) + 16)
                dve.tensor_tensor(ga[q][:], ga[q][:], gb[q][:], ALU.add).then_inc(s_ab, 1)

            def cap1(m, c):
                dve.wait_ge(s_e1, 2 * m + c + 1)
                dve.tensor_scalar(r1[:], r1[:], EXP_CAP, None, ALU.min).then_inc(s_c1, 1)

            def cap2(m, c):
                dve.wait_ge(s_e2, 2 * m + c + 1)
                dve.tensor_scalar(r2[c % 2][:], r2[c % 2][:], EXP_CAP, None, ALU.min).then_inc(s_c2, 1)

            def tail1(m, c):
                p = 2 * m + c
                dve.wait_ge(s_x1, p + 1)
                since(dve, s_h1s, p)
                for b in range(2):
                    dve.scalar_tensor_tensor(h1f[:, b, :], r1[:, b, :], 1.0, psum[:, b, :],
                                             ALU.subtract, ALU.mult).then_inc(s_h1, 1)

            def h1_high(m, c, first=False):
                p = 2 * m + c
                dve.wait_ge(s_h1, 2 * p + 2)
                if not first:
                    dve.wait_ge(s_pre2, 2 * p - 2)
                dve.tensor_copy(h1_hi[c % 2][:].rearrange("p c e -> p (c e)"),
                                h1f[:].rearrange("p a b -> p (a b)")).then_inc(s_h1hi, 1)

            def tail2(m, c):
                q = c % 2
                dve.wait_ge(s_x2, 2 * m + c + 1)
                for j in range(2):
                    dve.scalar_tensor_tensor(r2[q][:, j, :], r2[q][:, j, :], 1.0, psum[:, 2 + 2 * q + j, :],
                                             ALU.subtract, ALU.mult).then_inc(s_msg, 1)

            def edges(sorted_tiles):

                def hots(m, c):
                    p = 2 * m + c
                    for j in range(2):
                        dve.tensor_scalar(onehot[2 * (c % 2) + j][:], iota[:, 0:P],
                                          dst_rel[:, bass.ds(2 * p + j, 1)], None, ALU.is_equal).then_inc(s_hot, 1)

                def add(m, c):
                    p = 2 * m + c
                    base = dve.value_load(base_b[0:1, bass.ds(m + c // 2, 1)], min_val=0, max_val=LAST_BASE)
                    dve.wait_ge(s_seg, p + 1)
                    dve.wait_ge(s_agg, p)
                    dst = aggT[:, 0:C, bass.ds(base, P)]
                    dve.tensor_tensor(dst, dst, psum[:, 6 + c % 2, :].rearrange("p (c e) -> p c e", c=C),
                                      ALU.add).then_inc(s_agg, 1)

                def every_window(m, c):
                    p = 2 * m + c
                    for j in range(2):
                        t = 2 * p + j
                        with dve.Fori(0, NT // 2) as k:
                            for b in range(2):
                                nth = t * NT + 2 * k + b
                                dve.wait_ge(s_agg, nth + 1)
                                dve.tensor_scalar(onehot[b][:], iota[:], windows[:, bass.ds(2 * k + b, 1)],
                                                  dst_f[:, bass.ds(t, 1)], ALU.add, ALU.is_equal).then_inc(s_hot, 1)
                                dve.wait_ge(s_seg, nth + 1)
                                dst = aggT[:, 0:C, bass.ds((2 * k + b) * P, P)]
                                dve.tensor_tensor(dst, dst, psum[:, 6 + b, :].rearrange("p (c e) -> p c e", c=C),
                                                  ALU.add).then_inc(s_agg, 1)

                add_up = add if sorted_tiles else every_window

                def step(m, c, begun=2, last=False, ea=True, ab=True):
                    if not last:
                        cap1(m, c + 1)
                    if begun >= 2:
                        add_up(m, c - 2)
                    if begun >= 1 and sorted_tiles:
                        hots(m, c - 1)
                    if ea:
                        ea_split(m, c + 3)
                    if ab:
                        ab_sum(m, c + 2)
                    if not last:
                        tail1(m, c + 1)
                        h1_high(m, c + 1, begun == 0)
                    if begun >= 1:
                        tail2(m, c - 1)
                    cap2(m, c)

                if not sorted_tiles:
                    dve.sem_inc(s_agg, 1)
                cap1(0, 0)
                tail1(0, 0)
                h1_high(0, 0, first=True)
                for c in range(3):
                    step(0, c, begun=c)
                with dve.Fori(1, (PAIRS - 5) // 2) as m:
                    step(m, 1)
                    step(m, 2)
                mm = (PAIRS - 5) // 2
                step(mm, 1)
                step(mm, 2, ea=False)
                step(mm, 3, ea=False, ab=False)
                step(mm, 4, ea=False, ab=False, last=True)
                tail2(mm, 4)
                if sorted_tiles:
                    hots(mm, 4)
                add_up(mm, 3)
                add_up(mm, 4)
                dve.wait_ge(s_agg, PAIRS if sorted_tiles else ET * NT + 1)

            ea_split(0, 0)
            ea_split(0, 1)
            ab_sum(0, 0)
            ab_sum(0, 1)
            for k in (4, 5, 6):
                split_w(k)
            dve.wait_ge(s_pre1, 1)
            ea_split(0, 2)
            dve.wait_ge(s_zero, 1)
            widest = dve.value_load(span_max[:], min_val=0, max_val=NP)
            with dve.If(widest < P):
                edges(True)
            with dve.Else():
                edges(False)
            split_w(7)
            dve.memset(z3[:, 0, 0:1], 0.0).then_inc(s_edge_done, 1)

            dve.wait_ge(s_edge_done, 1)

            def group2(g):
                since(dve, s_z3p, g)
                src = aggT[:, 0:C, bass.ds(g * GW, GW)]
                dve.tensor_copy(g_hi[:], src).then_inc(s_ghi, 1)
                dve.wait_ge(s_ghi, g + 1)
                dve.tensor_tensor(g_lo[:], src, g_hi[:].bitcast(F32), ALU.subtract).then_inc(s_gs, 1)
                dve.wait_ge(s_z3p, g + 1)
                dve.tensor_tensor(z3[:].rearrange("p a b -> p (a b)"),
                                  keep[:, bass.ds(g, 1), :].rearrange("p a d -> p (a d)"),
                                  psum[:, 0:2, :].rearrange("p a b -> p (a b)"), ALU.add).then_inc(s_z3, 1)
                dve.wait_ge(s_z3, g + 1)
                dve.tensor_scalar(r3[:], z3[:], Z_CAP, None, ALU.min).then_inc(s_c3, 1)
                dve.wait_ge(s_x3, g + 1)
                dve.scalar_tensor_tensor(r3[:], r3[:], 1.0, z3[:], ALU.subtract, ALU.mult).then_inc(s_u, 1)
                dve.wait_ge(s_u, g + 1)
                dve.tensor_copy(u_hi[:].rearrange("p c e -> p (c e)"),
                                r3[:].rearrange("p a b -> p (a b)")).then_inc(s_uhi, 1)
                dve.wait_ge(s_uhi, g + 1)
                dve.tensor_tensor(u_lo[:].rearrange("p c e -> p (c e)"), r3[:].rearrange("p a b -> p (a b)"),
                                  u_hi[:].rearrange("p c e -> p (c e)").bitcast(F32),
                                  ALU.subtract).then_inc(s_us, 1)
                for j in range(2):
                    n = 2 * g + j
                    x1n = x1[:, bass.ds(n, 1), :].rearrange("p a d -> p (a d)")
                    dve.wait_ge(s_o4, n + 1)
                    dve.wait_ge(s_hb, n + 1)
                    dve.tensor_tensor(ht[j][:], ht[j][:], psum[:, 2 + j, :], ALU.subtract).then_inc(s_y, 1)
                    dve.wait_ge(s_y, n + 1)
                    apart(dve)
                    dve.bn_stats(bn2[:, j, :], ht[j][:]).then_inc(s_bn2, 1)
                    dve.wait_ge(s_bn2, 2 * n + 1)
                    apart(dve)
                    dve.bn_aggr(mv2[:, j, :], bn2[:, j, :]).then_inc(s_mv2, 1)
                    dve.wait_ge(s_mv2, 2 * n + 1)
                    dve.wait_ge(s_rstd2, 2 * n + 1)
                    dve.tensor_scalar(ht[j][:], ht[j][:], mv2[:, j, 0:1], rs2[:, j, 1:2],
                                      ALU.subtract, ALU.mult).then_inc(s_t2, 1)
                    dve.wait_ge(s_t2, 2 * n + 1)
                    dve.tensor_tensor(ht[j][:], ht[j][:], vec["gamma0"][:], ALU.mult).then_inc(s_t2, 1)
                    dve.wait_ge(s_t2, 2 * n + 2)
                    dve.wait_ge(s_xb, n + 1)
                    dve.tensor_tensor(x1n, ht[j][:], xt[j][:], ALU.add).then_inc(s_x1r, 1)
                    dve.wait_ge(s_x1r, n + 1)
                    apart(dve)
                    dve.bn_stats(bn2[:, j, :], x1n).then_inc(s_bn2, 1)
                    dve.wait_ge(s_bn2, 2 * n + 2)
                    apart(dve)
                    dve.bn_aggr(mv2[:, j, :], bn2[:, j, :]).then_inc(s_mv2, 1)
                    dve.wait_ge(s_mv2, 2 * n + 2)
                    dve.wait_ge(s_rstd2, 2 * n + 2)
                    dve.tensor_scalar(rs2[:, j, 2:3], mv2[:, j, 0:1], -1.0, rs2[:, j, 1:2],
                                      ALU.mult, ALU.mult).then_inc(s_nmr2, 1)
                for j in range(2):
                    n = 2 * g + j
                    pt = psum[:, 4 + j, :].rearrange("p (c e) -> p c e", c=C)
                    part = slice(j * P, (j + 1) * P)
                    dve.wait_ge(s_h2T, n + 1)
                    dve.tensor_copy(u_hi[:, :, part], pt).then_inc(s_h2hi, 1)
                    dve.wait_ge(s_h2hi, n + 1)
                    dve.tensor_tensor(u_lo[:, :, part], pt, u_hi[:, :, part].bitcast(F32),
                                      ALU.subtract).then_inc(s_h2s, 1)
                for j in range(2):
                    n = 2 * g + j
                    dve.wait_ge(s_qps, n + 1)
                    dve.tensor_tensor(keep[:, bass.ds(g, 1), j * D:(j + 1) * D].rearrange("p a d -> p (a d)"),
                                      psum[:, 6 + j, :], vec["bias1"][:], ALU.add).then_inc(s_q, 1)

            over_groups(dve, group2)

            dve.memset(aggT[:], 0.0).then_inc(s_zero3, 1)
            dve.wait_ge(s_zero3, 1)

            def seg3(b):
                return psum[:, 2 * b:2 * b + 2, :].rearrange("p a b -> p (a b)")[:, 0:(C + 1) * P].rearrange(
                    "p (c e) -> p c e", c=C + 1)

            def hot(t, j):
                for one in (one3, count3):
                    ins = dve.tensor_scalar(one[j][:], iota[:], dst_rel[:, bass.ds(t, 1)], None, ALU.is_equal)
                ins.then_inc(s_hot3, 1)

            def neighbours(sorted_tiles):
                if sorted_tiles:
                    def add(quad, b, count=4, more=4):
                        for j in range(4):
                            if j < more:
                                dve.wait_ge(s_seg3, 4 * quad + j + 1)
                                hot(4 * quad + j + 4, j)
                            if j == 0:
                                base = dve.value_load(base_b[0:1, bass.ds(quad, 1)], min_val=0, max_val=LAST_BASE)
                        dve.wait_ge(s_seg3, 4 * quad + count)
                        dve.wait_ge(s_agg3, quad)
                        dst = aggT[:, :, bass.ds(base, P)]
                        dve.tensor_tensor(dst, dst, seg3(b), ALU.add).then_inc(s_agg3, 1)

                    for j in range(4):
                        hot(j, j)
                    for b in range(2):
                        add(b, b)
                    with dve.Fori(1, (QUADS - 2) // 2) as k:
                        for b in range(2):
                            add(2 * k + b, b)
                    add(QUADS - 2, 0, more=LAST_QUAD)
                    add(QUADS - 1, 1, count=LAST_QUAD, more=0)
                    dve.wait_ge(s_agg3, QUADS)
                else:
                    dve.sem_inc(s_agg3, 1)
                    with dve.Fori(0, ET) as t:
                        with dve.Fori(0, NT // 2) as k:
                            for b in range(2):
                                nth = t * NT + 2 * k + b
                                dve.wait_ge(s_agg3, nth + 1)
                                for one in (one3, count3):
                                    ins = dve.tensor_scalar(one[b][:], iota[:], windows[:, bass.ds(2 * k + b, 1)],
                                                            dst_f[:, bass.ds(t, 1)], ALU.add, ALU.is_equal)
                                ins.then_inc(s_hot3, 1)
                                dve.wait_ge(s_deg, nth + 1)
                                dst = aggT[:, :, bass.ds((2 * k + b) * P, P)]
                                dve.tensor_tensor(dst, dst, seg3(b), ALU.add).then_inc(s_agg3, 1)
                    dve.wait_ge(s_agg3, ET * NT + 1)

            with dve.If(widest < P):
                neighbours(True)
            with dve.Else():
                neighbours(False)

            deg = aggT[:, C, :]
            dve.wait_ge(s_n3, 1)
            dve.tensor_scalar(deg, deg, 1.0, None, ALU.max).then_inc(s_mean, 1)
            dve.wait_ge(s_mean, 1)
            dve.reciprocal(deg, deg).then_inc(s_mean, 1)
            dve.wait_ge(s_mean, 2)
            for c in range(C):
                dve.tensor_tensor(aggT[:, c, :], aggT[:, c, :], deg, ALU.mult).then_inc(s_mean, 1)
            dve.wait_ge(s_mean, 2 + C)

            def nodes4(g):
                part = aggT[:, 0:C, bass.ds(g * GW, GW)]
                since(dve, s_nps, 2 * g)
                dve.tensor_copy(g_hi[:], part).then_inc(s_mhi, 1)
                dve.wait_ge(s_mhi, g + 1)
                dve.tensor_tensor(g_lo[:], part, g_hi[:].bitcast(F32), ALU.subtract).then_inc(s_ms, 1)
                for j in range(2):
                    n = 2 * g + j
                    dve.wait_ge(s_nps, n + 1)
                    since(dve, s_out[j], 16 * g)
                    dve.tensor_tensor(ht[j][:], psum[:, 4 + j, :],
                                      keep[:, bass.ds(g, 1), j * D:(j + 1) * D].rearrange("p a d -> p (a d)"),
                                      ALU.add).then_inc(s_h4, 1)
                    dve.wait_ge(s_h4, n + 1)
                    apart(dve)
                    dve.bn_stats(bn2[:, j, :], ht[j][:]).then_inc(s_bn4, 1)
                    dve.wait_ge(s_bn4, n + 1)
                    apart(dve)
                    dve.bn_aggr(mv2[:, j, :], bn2[:, j, :]).then_inc(s_mv4, 1)
                    dve.wait_ge(s_mv4, n + 1)
                    dve.wait_ge(s_rstd4, n + 1)
                    dve.tensor_scalar(ht[j][:], ht[j][:], mv2[:, j, 0:1], rs2[:, j, 1:2],
                                      ALU.subtract, ALU.mult).then_inc(s_t4, 1)
                    dve.wait_ge(s_t4, 2 * n + 1)
                    dve.tensor_tensor(ht[j][:], ht[j][:], vec["gamma1"][:], ALU.mult).then_inc(s_t4, 1)
                    dve.wait_ge(s_t4, 2 * n + 2)
                    dve.wait_ge(s_xb4, n + 1)
                    dve.tensor_tensor(ht[j][:], ht[j][:], x1[:, bass.ds(n, 1), :].rearrange("p a d -> p (a d)"),
                                      ALU.add).then_inc(s_res, 1)

            over_groups(dve, nodes4)

        @block.tensor
        def _(pe):
            def square(o, lhs_hi, lhs_lo, name, e0, first=True, last=True):
                slot = W_SLOT[name]
                for c in range(C):
                    cols = slice(e0, e0 + P)
                    mm = three_pass(pe, o, lhs_hi[:, c, cols], lhs_lo[:, c, cols], w_hi[slot][:, c, :],
                                    w_lo[slot][:, c, :], first and c == 0, last and c == C - 1)
                return mm

            def turned(bank, name, rhs_hi, rhs_lo):
                slot = W_SLOT[name]
                for f in range(C):
                    o = psum[:, bank + f // 2, (f % 2) * GW:(f % 2 + 1) * GW]
                    for c in range(C):
                        cols = slice(f * P, (f + 1) * P)
                        mm = three_pass(pe, o, w_hi[slot][:, c, cols], w_lo[slot][:, c, cols], rhs_hi[:, c, :],
                                        rhs_lo[:, c, :], c == 0, c == C - 1)
                return mm

            pe.wait_ge(s_const, 16 * (1 + 3 + 2 + 1 + len(vec) + C + 2 + 2))
            def nodes0(g):
                for j in range(2):
                    n = 2 * g + j
                    pe.wait_ge(s_h, n + 1)
                    since(pe, s_hT, 2 * g)
                    for c in range(C):
                        tr = pe.transpose(psum[:, j, c * P:(c + 1) * P], hout[j][:, c * P:(c + 1) * P], ident[:])
                    tr.then_inc(s_hTp, 1)
                for j in range(2):
                    n = 2 * g + j
                    pe.wait_ge(s_hT, n + 1)
                    pe.wait_ge(s_wlo, 1)
                    since(pe, s_aev, 2 * g)
                    square(psum[:, 2 + j, :], hT_hi, hT_lo, "W1a", j * P).then_inc(s_aps, 1)
                    pe.wait_ge(s_wlo, 2)
                    since(pe, s_bev, 2 * g)
                    square(psum[:, 4 + j, :], hT_hi, hT_lo, "W1b", j * P).then_inc(s_bps, 1)
                pe.wait_ge(s_wlo, 3)
                since(pe, s_pev, g)
                turned(6, "W3a", hT_hi, hT_lo).then_inc(s_pps, 1)

            over_groups(pe, nodes0)

            pe.wait_ge(s_wlo, 4)
            pe.wait_ge(s_b2, 4)
            pe.wait_ge(s_ones, 1)
            pe.wait_ge(s_ones_r, 1)

            def z1(m, c, first=False):
                p = 2 * m + c
                q = c % 2
                pe.wait_ge(s_east, p + 1)
                pe.wait_ge(s_ab, p + 1)
                for f in range(C):
                    if not first and f % 2 == 0:
                        pe.wait_ge(s_h1, 2 * p - 1 + f // 2)
                    cols = slice(f * P, (f + 1) * P)
                    at = (f % 2) * GW
                    o = psum[:, f // 2, at:at + GW]
                    pe.matmul(o, w1c_hi[:, cols], ea_st[q][:], start=True, stop=False)
                    pe.matmul(o, w1c_lo[:, cols], ea_st[q][:], start=False, stop=False)
                    for j in range(2):
                        oj = psum[:, f // 2, at + j * P:at + (j + 1) * P]
                        mm = pe.matmul(oj, ga[q][:, j, cols], ident[:], is_transpose=True, start=False, stop=j == 1)
                mm.then_inc(s_pre1, 1)

            def z2(m, c, early=False):
                p = 2 * m + c
                q = c % 2
                slot = W_SLOT["W2"]
                pe.wait_ge(s_h1hi, p + 1)
                if not early:
                    pe.wait_ge(s_msg, 2 * p - 2)
                for j in range(2):
                    o = psum[:, 2 + 2 * q + j, :]
                    pe.matmul(o, ones_r[:], b2rows[:], start=True, stop=False)
                    for k in range(C):
                        for part in (w_hi, w_lo):
                            pe.matmul(o, h1_hi[q][:, k, j * P:(j + 1) * P], part[slot][:, k, :],
                                      start=False, stop=False)
                pe.wait_ge(s_h1s, p + 1)
                for j in range(2):
                    for k in range(C):
                        mm = pe.matmul(psum[:, 2 + 2 * q + j, :], h1_lo[q][:, k, j * P:(j + 1) * P],
                                       w_hi[slot][:, k, :], start=False, stop=k == C - 1)
                    mm.then_inc(s_pre2, 1)

            def edges(sorted_tiles):
                def sums(m, c, first=False):
                    p = 2 * m + c
                    q = c % 2
                    pe.wait_ge(s_msg, 2 * p + 2)
                    pe.wait_ge(s_hot, 2 * p + 2)
                    if not first:
                        pe.wait_ge(s_agg, p - 1)
                    for f in range(C):
                        for j in range(2):
                            mm = pe.matmul(psum[:, 6 + q, f * P:(f + 1) * P], r2[q][:, j, f * P:(f + 1) * P],
                                           onehot[2 * q + j][:], start=j == 0, stop=j == 1)
                    mm.then_inc(s_seg, 1)

                def every_window(m, c, first=False):
                    p = 2 * m + c
                    q = c % 2
                    for j in range(2):
                        t = 2 * p + j
                        pe.wait_ge(s_msg, t + 1)
                        apart(pe)
                        with pe.Fori(0, NT // 2) as k:
                            for b in range(2):
                                pe.wait_ge(s_hot, t * NT + 2 * k + b + 1)
                                for f in range(C):
                                    mm = pe.matmul(psum[:, 6 + b, f * P:(f + 1) * P],
                                                   r2[q][:, j, f * P:(f + 1) * P], onehot[b][:],
                                                   start=True, stop=True)
                                mm.then_inc(s_seg, 1)

                add_up = sums if sorted_tiles else every_window

                def step(m, c, more=True):
                    add_up(m, c - 2)
                    z2(m, c)
                    if more:
                        z1(m, c + 2)

                z1(0, 1)
                z2(0, 0, early=True)
                z1(0, 2)
                z2(0, 1, early=True)
                z1(0, 3)
                add_up(0, 0, first=True)
                z2(0, 2)
                z1(0, 4)
                mm = (PAIRS - 3) // 2
                with pe.Fori(1, mm) as m:
                    step(m, 1)
                    step(m, 2)
                step(mm, 1, more=False)
                step(mm, 2, more=False)
                add_up(mm, 1)
                add_up(mm, 2)

            z1(0, 0, first=True)
            pe.wait_ge(s_ix, 6)
            widest = pe.value_load(span_max[:], min_val=0, max_val=NP)
            with pe.If(widest < P):
                edges(True)
            with pe.Else():
                edges(False)
            pe.sem_inc(s_pe_edge, 1)

            pe.wait_ge(s_wlo, 5)
            def nodes2(g):
                pe.wait_ge(s_gs, g + 1)
                since(pe, s_z3, g)
                turned(0, "W3b", g_hi, g_lo).then_inc(s_z3p, 1)
                pe.wait_ge(s_us, g + 1)
                pe.wait_ge(s_wlo, 6)
                for j in range(2):
                    since(pe, s_y, 2 * g)
                    square(psum[:, 2 + j, :], u_hi, u_lo, "W4", j * P).then_inc(s_o4, 1)
                for j in range(2):
                    pe.wait_ge(s_h2, 2 * g + j + 1)
                    since(pe, s_h2s, 2 * g)
                    for c in range(C):
                        tr = pe.transpose(psum[:, 4 + j, c * P:(c + 1) * P], h2o[j][:, c * P:(c + 1) * P], ident[:])
                    tr.then_inc(s_h2T, 1)
                pe.wait_ge(s_wlo, 7)
                for j in range(2):
                    pe.wait_ge(s_h2s, 2 * g + j + 1)
                    since(pe, s_q, 2 * g)
                    square(psum[:, 6 + j, :], u_hi, u_lo, "Ws", j * P).then_inc(s_qps, 1)

            over_groups(pe, nodes2)

            def sum3(j, hot, b, first=True, last=True):
                for f in range(C):
                    pe.matmul(psum[:, 2 * b, f * P:(f + 1) * P], gr[j][:, f * P:(f + 1) * P], one3[hot][:],
                              start=first and f == 0, stop=last and f == C - 1)
                return pe.matmul(psum[:, 2 * b + 1, 0:P], ones_b[:], count3[hot][:], start=first, stop=last)

            pe.wait_ge(s_q, NT)

            def quad3(use, b, count=4, early=False):
                quad = 2 * use + b
                if not early:
                    pe.wait_ge(s_agg3, quad - 1)
                for j in range(count):
                    pe.wait_ge(s_gr[4 * b + j], 16 * (use + 1))
                    pe.wait_ge(s_hot3, 4 * quad + j + 1)
                    sum3(4 * b + j, j, b, j == 0, j == count - 1).then_inc(s_seg3, 1)

            def neighbours(sorted_tiles):
                if sorted_tiles:
                    for b in range(2):
                        quad3(0, b, early=True)
                    with pe.Fori(1, (QUADS - 2) // 2) as k:
                        for b in range(2):
                            quad3(k, b)
                    quad3((QUADS - 2) // 2, 0)
                    quad3((QUADS - 2) // 2, 1, LAST_QUAD)
                else:
                    def windows(t, j, use):
                        pe.wait_ge(s_gr[j], 16 * use)
                        apart(pe)
                        with pe.Fori(0, NT // 2) as k:
                            for b in range(2):
                                pe.wait_ge(s_hot3, t * NT + 2 * k + b + 1)
                                sum3(j, b, b).then_inc(s_deg, 1)
                        pe.wait_ge(s_deg, t * NT + NT)
                        pe.sem_inc(s_seg3, 1)

                    with pe.Fori(0, ET // 8) as k:
                        for j in range(8):
                            windows(8 * k + j, j, k + 1)
                    for j in range(ET % 8):
                        windows(ET // 8 * 8 + j, j, ET // 8 + 1)

            with pe.If(widest < P):
                neighbours(True)
            with pe.Else():
                neighbours(False)
            pe.sem_inc(s_n3, 1)

            pe.wait_ge(s_wlo, 8)
            def nodes4(g):
                pe.wait_ge(s_ms, g + 1)
                for j in range(2):
                    since(pe, s_h4, 2 * g)
                    square(psum[:, 4 + j, :], g_hi, g_lo, "Wn", j * P).then_inc(s_nps, 1)

            over_groups(pe, nodes4)


def kernel(x, src, dst, edge_attr_64, L0_gnn_W1, L0_gnn_b1, L0_gnn_W2, L0_gnn_b2, L0_gnn_W3, L0_gnn_b3,
           L0_gnn_W4, L0_gnn_b4, L0_gnn_gamma, L0_gnn_beta, L1_gnn_W_self, L1_gnn_W_neigh, L1_gnn_bias,
           L1_gnn_gamma, L1_gnn_beta):
    import concourse.bacc as bacc
    from concourse.bass_utils import run_bass_kernel_spmd

    W1, W3 = np.asarray(L0_gnn_W1), np.asarray(L0_gnn_W3)
    row = lambda a: np.ascontiguousarray(np.asarray(a).reshape(1, -1))
    pad_edges = QUADS * 4 * P - N_EDGES
    src_p = np.concatenate([np.asarray(src), np.zeros(pad_edges, np.int32)])
    dst_p = np.concatenate([np.asarray(dst), np.full(pad_edges, N_NODES, np.int32)])
    ea = np.concatenate([np.asarray(edge_attr_64), np.zeros((EP - N_EDGES, DE), np.float32)])
    arrays = {
        "x": np.concatenate([np.asarray(x), np.zeros((NP - N_NODES, D), np.float32)]),
        "src_t": np.ascontiguousarray(src_p.reshape(4 * QUADS, P).T),
        "dst_t": np.ascontiguousarray(dst_p.reshape(4 * QUADS, P).T),
        "dst_r": np.ascontiguousarray(dst_p.reshape(QUADS, 4 * P)),
        "ea_t": np.ascontiguousarray(ea.T),
        "ident_d": np.eye(P, dtype=np.float32),
        "iota_d": np.concatenate([np.arange(P), P * np.arange(NT)]).astype(np.float32).reshape(1, -1),
    }
    weights = {
        "W1a": W1[0:D], "W1b": W1[D:2 * D], "W1c": W1[2 * D:], "W2": L0_gnn_W2, "W3a": W3[0:D], "W3b": W3[D:],
        "W4": L0_gnn_W4, "Ws": np.asarray(L1_gnn_W_self).T, "Wn": np.asarray(L1_gnn_W_neigh).T,
    }
    vectors = {
        "b1": L0_gnn_b1, "b2": L0_gnn_b2, "b3": L0_gnn_b3, "b4": L0_gnn_b4, "gamma0": L0_gnn_gamma,
        "beta0": L0_gnn_beta, "bias1": L1_gnn_bias, "gamma1": L1_gnn_gamma, "beta1": L1_gnn_beta,
    }
    arrays.update({f"w_{k}": np.ascontiguousarray(a) for k, a in weights.items()})
    arrays.update({f"v_{k}": row(a) for k, a in vectors.items()})

    nc = bacc.Bacc("TRN2", target_bir_lowering=False, num_devices=1)
    aps = {k: nc.dram_tensor(k, a.shape, mybir.dt.from_np(a.dtype), kind="ExternalInput").ap()
           for k, a in arrays.items()}
    out = nc.dram_tensor("out", [NP, D], F32, kind="ExternalOutput").ap()
    build(nc, aps["x"], aps["src_t"], aps["dst_t"], aps["dst_r"], aps["ea_t"], aps["ident_d"], aps["iota_d"],
          {k: aps[f"w_{k}"] for k in weights}, {k: aps[f"v_{k}"] for k in vectors}, out)
    result = run_bass_kernel_spmd(nc, [arrays], core_ids=[0])
    return result.results[0]["out"][:N_NODES]
```

```python
from contextlib import ExitStack

import numpy as np

import concourse.bass as bass
from concourse import mybir

F32 = mybir.dt.float32
F32R = mybir.dt.float32r
I32 = mybir.dt.int32
BF16 = mybir.dt.bfloat16
ALU = mybir.AluOpType
ACT = mybir.ActivationFunctionType
AX = mybir.AxisListType

P = 128
D = 512
C = D // P
DE = 64
N_NODES = 1250
N_EDGES = 20000
NT = -(-N_NODES // P)
NP = NT * P
NG = NT // 2
ET = -(-N_EDGES // P)
ET += ET % 2
EP = ET * P
PAIRS = ET // 2
QUADS = -(-ET // 4)
LAST_QUAD = ET - 4 * (QUADS - 1)
GW = 2 * P
LAST_BASE = NP - P
EPS = 1e-5
EXP_CAP = float(2.0 ** 30)
Z_CAP = 20.0
LN2 = float(np.log(2.0))
SET_NAME = "natural_log_exp_and_others"
W_ORDER = ["W1a", "W3a", "W1b", "W2", "W3b", "W4", "Ws", "Wn"]
W_SLOT = {"W1a": 0, "W1b": 1, "W3a": 2, "W2": 3, "W3b": 0, "W4": 1, "Ws": 2, "Wn": 3}


def build(nc, x, src_t, dst_t, dst_r, ea_t, ident_d, iota_d, w, v, out):
    assert NT % 2 == 0 and PAIRS % 2 == 1 and PAIRS >= 7 and QUADS % 2 == 0

    def scratch(name, shape, dt=F32):
        return nc.dram_tensor(name, shape, dt, kind="Internal").ap()

    tab_a = scratch("tab_a", [NP, D])
    tab_b = scratch("tab_b", [NP, D])
    tab_h = scratch("tab_h", [NP, D])
    tab_h2 = scratch("tab_h2", [NP, D])
    base_d = scratch("base_d", [1, QUADS], I32)
    span_d = scratch("span_d", [1, QUADS], I32)

    ctx = ExitStack()
    with ctx:
        top = [-(-nc.sbuf_base // 64) * 64]

        def sb(name, shape, dt=F32):
            size = int(np.prod(shape[1:])) * (2 if dt == BF16 else 4)
            t = nc.alloc_sbuf_tensor_at(name, shape, dt, offset=top[0])
            top[0] += -(-size // 64) * 64
            assert top[0] <= nc.sbuf_usable_end, (name, top[0])
            return t

        def sem(name):
            return ctx.enter_context(nc.semaphore(name))

        w_hi = [sb(f"w_hi{i}", [P, C, D], F32R) for i in range(4)]
        w_lo = [sb(f"w_lo{i}", [P, C, D], F32R) for i in range(4)]
        w_raw_at = top[0]
        w_raw = [sb(f"w_raw{i}", [P, C, D]) for i in range(2)]
        w1c_hi = sb("w1c_hi", [P, D], F32R)
        w1c_lo = sb("w1c_lo", [P, D], F32R)
        aggT = sb("aggT", [P, C + 1, NP])
        keep = sb("keep", [P, NG, 4 * GW])
        vec = {k: sb(f"vec_{k}", [P, D]) for k in ("b4", "gamma0", "beta0", "bias1", "gamma1", "beta1")}
        b3col = sb("b3col", [P, C])
        b2rows = sb("b2rows", [P, D], F32R)
        ones_r = sb("ones_r", [P, P], F32R)
        ones_b = sb("ones_b", [P, P], BF16)
        ident = sb("ident", [P, P])
        iota = sb("iota", [P, P])
        windows = sb("windows", [P, NT])
        src_i = sb("src_i", [P, 4 * QUADS], I32)
        dst_i = sb("dst_i", [P, 4 * QUADS], I32)
        dst_f = sb("dst_f", [P, 4 * QUADS])
        dst_rel = sb("dst_rel", [P, 4 * QUADS])
        base_b = sb("base_b", [P, QUADS], I32)
        span_row = sb("span_row", [1, QUADS], I32)
        span_max = sb("span_max", [1, 1], I32)
        phase = top[0]

        w1c_raw = sb("w1c_raw", [P, D])
        b2raw = sb("b2raw", [P, D])
        b1b = sb("b1b", [P, D])
        xin = [sb(f"xin{j}", [P, D]) for j in range(2)]
        hout = [sb(f"hout{j}", [P, D]) for j in range(2)]
        hT_hi = sb("hT_hi", [P, C, GW], F32R)
        hT_lo = sb("hT_lo", [P, C, GW], F32R)
        a_sb = [sb(f"a_sb{j}", [P, D]) for j in range(2)]
        b_sb = [sb(f"b_sb{j}", [P, D]) for j in range(2)]
        dr = sb("dr", [QUADS, 4 * P], I32)
        dr_min = sb("dr_min", [QUADS, 1])
        dr_max = sb("dr_max", [QUADS, 1])
        dr_base = sb("dr_base", [QUADS, 1], I32)
        dr_span = sb("dr_span", [QUADS, 1], I32)
        bn0 = sb("bn0", [P, 2, 6])
        mv0 = sb("mv0", [P, 2, 2])
        rs0 = sb("rs0", [P, 2, 4])

        end0 = top[0]
        top[0] = phase
        r1 = sb("r1", [P, 2, D])
        r2 = [sb(f"r2{q}", [P, 2, D]) for q in range(2)]
        h1f = sb("h1f", [P, 2, D])
        h1_hi = [sb(f"h1_hi{q}", [P, C, GW], F32R) for q in range(2)]
        h1_lo = [sb(f"h1_lo{q}", [P, C, GW], F32R) for q in range(2)]
        ea_st = [sb(f"ea_st{q}", [P, GW], F32R) for q in range(2)]
        onehot = [sb(f"onehot{j}", [P, P]) for j in range(4)]
        assert top[0] >= end0
        ea_raw = [sb(f"ea_raw{q}", [P, GW]) for q in range(2)]
        ga = [sb(f"ga{q}", [P, 2, D]) for q in range(2)]
        gb = [sb(f"gb{q}", [P, 2, D]) for q in range(2)]
        idx_ab = [sb(f"idx_ab{q}", [P, 4], I32) for q in range(2)]

        top[0] = phase
        x1 = sb("x1", [P, NT, D])
        g_hi = sb("g_hi", [P, C, GW], F32R)
        g_lo = sb("g_lo", [P, C, GW], F32R)
        z3 = sb("z3", [P, 2, D])
        r3 = sb("r3", [P, 2, D])
        u_hi = sb("u_hi", [P, C, GW], F32R)
        u_lo = sb("u_lo", [P, C, GW], F32R)
        xt = [sb(f"xt{j}", [P, D]) for j in range(2)]
        ht = [sb(f"ht{j}", [P, D]) for j in range(2)]
        h2o = [sb(f"h2o{j}", [P, D]) for j in range(2)]
        degree = sb("degree", [P, NT])
        bn2 = sb("bn2", [P, 2, 6])
        mv2 = sb("mv2", [P, 2, 2])
        rs2 = sb("rs2", [P, 2, 4])
        gr = [a[:, j, :] for a in (z3, r3) for j in range(2)]
        gr += [a[:].bitcast(F32).rearrange("p c e -> p (c e)")[:, j * D:(j + 1) * D]
               for a in (g_hi, g_lo) for j in range(2)]
        idx_r = [sb(f"idx_r{h}", [P, 8], I32) for h in range(2)]
        one3 = [sb(f"one3{j}", [P, P]) for j in range(4)]
        count3 = [sb(f"count3{j}", [P, P], BF16) for j in range(4)]

        h2s = [nc.alloc_sbuf_tensor_at(f"h2s{k}", [P, C, GW], F32R, offset=w_raw_at + k * C * GW * 4)
               for k in range(2)]

        psum = ctx.enter_context(nc.psum_tensor("psum", [P, 8, D], F32))

        s_const = sem("const_in")
        s_ident = sem("ident_in")
        s_vec = sem("vectors_in")
        s_wraw = [sem(f"w_raw_in{i}") for i in range(2)]
        s_xin = [sem(f"x_in{j}") for j in range(2)]
        s_tabh = [sem(f"h_stored{j}") for j in range(2)]
        s_taba = [sem(f"a_stored{j}") for j in range(2)]
        s_tabb = [sem(f"b_stored{j}") for j in range(2)]
        s_based = sem("base_stored")
        s_basein = sem("base_in")
        s_ga = [[sem(f"a_rows{q}{j}") for j in range(2)] for q in range(2)]
        s_gb = [[sem(f"b_rows{q}{j}") for j in range(2)] for q in range(2)]
        s_ea = [sem(f"edge_attr_in{q}") for q in range(2)]
        s_ht2 = [sem(f"node_rows_in{j}") for j in range(2)]
        s_h2st = [sem(f"h2_stored{j}") for j in range(2)]
        s_gr = [sem(f"h2_rows{j}") for j in range(8)]
        s_out = [sem(f"out_stored{j}") for j in range(2)]
        s_b2clear = sem("b2_rows_cleared")
        s_ones = sem("ones_set")
        s_ones_r = sem("ones_r_set")
        s_apart = sem("apart")
        s_b2 = sem("b2_steps")
        s_whi = sem("w_hi_ready")
        s_wlo = sem("w_lo_ready")
        s_wlo_dve = sem("first_w_lo_ready")
        s_ix = sem("index_steps")
        s_bn = sem("ln0_stats")
        s_mv = sem("ln0_moments")
        s_ln = sem("ln0_log")
        s_rstd = sem("ln0_rstd")
        s_nmr = sem("ln0_shift")
        s_h = sem("h_ready")
        s_hTp = sem("hT_in_psum")
        s_hThi = sem("hT_hi_ready")
        s_hT = sem("hT_ready")
        s_aps = sem("a_in_psum")
        s_bps = sem("b_in_psum")
        s_aev = sem("a_copied")
        s_bev = sem("b_copied")
        s_pps = sem("p_in_psum")
        s_pev = sem("p_copied")
        s_idx = sem("gather_index")
        s_eahi = sem("edge_attr_hi")
        s_east = sem("edge_attr_split")
        s_ab = sem("a_plus_b")
        s_pre1 = sem("z1_in_psum")
        s_e1, s_c1, s_q1, s_l1, s_x1 = (sem(f"mish1_{k}") for k in ("exp", "cap", "square", "log", "quotient"))
        s_h1 = sem("h1_chunks")
        s_h1hi = sem("h1_hi_ready")
        s_h1s = sem("h1_split")
        s_pre2 = sem("z2_in_psum")
        s_e2, s_c2, s_q2, s_l2, s_x2 = (sem(f"mish2_{k}") for k in ("exp", "cap", "square", "log", "quotient"))
        s_msg = sem("messages")
        s_hot = sem("onehot_ready")
        s_seg = sem("segment_in_psum")
        s_agg = sem("segment_added")
        s_edge_done = sem("agg_complete")
        s_pe_edge = sem("pe_edges_done")
        s_ghi = sem("agg_hi")
        s_gs = sem("agg_split")
        s_z3p = sem("z3_in_psum")
        s_z3 = sem("z3_ready")
        s_e3, s_c3, s_q3, s_l3, s_x3 = (sem(f"mish3_{k}") for k in ("exp", "cap", "square", "log", "quotient"))
        s_u = sem("u_ready")
        s_uhi = sem("u_hi_ready")
        s_us = sem("u_split")
        s_o4 = sem("out4_in_psum")
        s_hb = sem("h_plus_b4")
        s_y = sem("y_ready")
        s_bn2 = sem("ln2_stats")
        s_mv2 = sem("ln2_moments")
        s_ln2 = sem("ln2_log")
        s_rstd2 = sem("ln2_rstd")
        s_t2 = sem("ln2_steps")
        s_xb = sem("x_plus_beta")
        s_x1r = sem("x1_ready")
        s_nmr2 = sem("ln3_shift")
        s_h2 = sem("h2_ready")
        s_h2T = sem("h2T_in_psum")
        s_h2hi = sem("h2T_hi")
        s_h2s = sem("h2T_split")
        s_qps = sem("q_in_psum")
        s_q = sem("q_ready")
        s_idx3 = sem("gather3_index")
        s_hot3 = sem("onehot3_ready")
        s_seg3 = sem("segment3_in_psum")
        s_agg3 = sem("segment3_added")
        s_n3 = sem("neighbours_complete")
        s_zero = sem("aggT_cleared")
        s_zero3 = sem("aggT_cleared_again")
        s_winsum = sem("windows3_summed")
        s_sum3 = sem("neighbour_sums")
        s_degp = sem("degree_in_psum")
        s_mean = sem("degree_steps4")
        s_mhi = sem("mean_hi")
        s_ms = sem("mean_split")
        s_nps = sem("neigh_in_psum")
        s_h4 = sem("h4_ready")
        s_xb4 = sem("x1_plus_beta")
        s_bn4 = sem("ln4_stats")
        s_mv4 = sem("ln4_moments")
        s_ln4 = sem("ln4_log")
        s_rstd4 = sem("ln4_rstd")
        s_t4 = sem("ln4_steps")
        s_res = sem("result_ready")

        block = ctx.enter_context(nc.Block())
        N_CONST = 16 * (3 + 2 + 1 + C + 2 + 2)
        BY_DVE = 3

        def since(eng, s, value):
            if not isinstance(value, int) or value > 0:
                eng.wait_ge(s, value)

        def one_ahead(eng, body):
            body(0, ahead=2, behind=False)
            with eng.Fori(1, NG - 2) as g:
                body(g, ahead=2, behind=True)
            body(NG - 2, ahead=1, behind=True)
            body(NG - 1, ahead=0, behind=True)

        def over_groups(eng, body):
            body(0)
            with eng.Fori(1, NG) as g:
                body(g)

        def split_done(eng, k):
            k = W_ORDER.index(k) if isinstance(k, str) else k
            if k < BY_DVE:
                eng.wait_ge(s_wlo_dve, k + 1)
            else:
                eng.wait_ge(s_wlo, k + 1 - BY_DVE)

        def apart(eng):
            eng.sem_inc(s_apart, 1)

        def three_pass(pe, o, a_hi, a_lo, b_hi, b_lo, first, last):
            pe.matmul(o, a_hi, b_hi, start=first, stop=False)
            pe.matmul(o, a_hi, b_lo, start=False, stop=False)
            return pe.matmul(o, a_lo, b_hi, start=False, stop=last)

        @block.sync
        def _(sp):
            def load_w(k):
                if k >= 2:
                    split_done(sp, k - 2)
                sp.dma_start(w_raw[k % 2][:], w[W_ORDER[k]].rearrange("(c p) n -> p c n", p=P)
                             ).then_inc(s_wraw[k % 2], 16)

            def load_ea(m, c):
                p = 2 * m + c
                for half in range(2):
                    sp.dma_start(ea_raw[c % 2][half * DE:(half + 1) * DE, :],
                                 ea_t[:, bass.ds(p * GW, GW)]).then_inc(s_ea[c % 2], 16)

            sp.dma_start(xin[0][:], x[0:P, :]).then_inc(s_xin[0], 16)
            sp.dma_start(xin[1][:], x[P:2 * P, :]).then_inc(s_xin[1], 16)
            sp.dma_start(ident[:], ident_d).then_inc(s_ident, 16)
            load_w(0)
            load_w(1)
            for c in range(C):
                sp.dma_start(b3col[:, c:c + 1], v["b3"][0, c * P:(c + 1) * P].rearrange("(p a) -> p a", a=1)
                             ).then_inc(s_const, 16)
            sp.dma_start(b1b[:], v["b1"].partition_broadcast(P)).then_inc(s_const, 16)
            sp.dma_start(dr[:], dst_r).then_inc(s_const, 16)
            sp.dma_start(dst_i[:], dst_t).then_inc(s_const, 16)
            sp.dma_start(src_i[:], src_t).then_inc(s_const, 16)
            sp.dma_start(iota[:], iota_d[:, 0:P].partition_broadcast(P)).then_inc(s_const, 16)
            sp.dma_start(windows[:], iota_d[:, P:].partition_broadcast(P)).then_inc(s_const, 16)
            for half in range(2):
                sp.dma_start(w1c_raw[half * DE:(half + 1) * DE, :], w["W1c"]).then_inc(s_const, 16)
            sp.wait_ge(s_b2clear, 1)
            for row in (0, 32):
                sp.dma_start(b2raw[row:row + 1, :], v["b2"]).then_inc(s_const, 16)
            load_w(2)
            load_w(3)

            def h_out(g, more):
                for j in range(2):
                    n = 2 * g + j
                    sp.wait_ge(s_h, n + 1)
                    sp.dma_start(tab_h[bass.ds(n * P, P), :], hout[j][:]).then_inc(s_tabh[j], 16)
                    if more:
                        sp.dma_start(xin[j][:], x[bass.ds((n + 2) * P, P), :]).then_inc(s_xin[j], 16)

            def tables_out(g, ahead):
                if ahead:
                    h_out(g + 1, ahead == 2)
                for j in range(2):
                    n = 2 * g + j
                    sp.wait_ge(s_aev, n + 1)
                    sp.dma_start(tab_a[bass.ds(n * P, P), :], a_sb[j][:]).then_inc(s_taba[j], 16)
                    sp.wait_ge(s_bev, n + 1)
                    sp.dma_start(tab_b[bass.ds(n * P, P), :], b_sb[j][:]).then_inc(s_tabb[j], 16)

            h_out(0, True)
            sp.wait_ge(s_ix, 5)
            sp.dma_start(base_d.rearrange("o (a b) -> (o a) b", b=1), dr_base[:]).then_inc(s_based, 16)
            sp.dma_start(span_d.rearrange("o (a b) -> (o a) b", b=1), dr_span[:]).then_inc(s_based, 16)
            sp.wait_ge(s_based, 32)
            sp.dma_start(base_b[:], base_d.partition_broadcast(P)).then_inc(s_basein, 16)
            sp.dma_start(span_row[:], span_d).then_inc(s_basein, 16)

            tables_out(0, 2)
            load_w(4)
            load_w(5)
            tables_out(1, 2)
            for k in vec:
                sp.dma_start(vec[k][:], v[k].partition_broadcast(P)).then_inc(s_vec, 16)
            load_ea(0, 0)
            load_ea(0, 1)
            with sp.Fori(2, NG - 2) as g:
                tables_out(g, 2)
            tables_out(NG - 2, 1)
            tables_out(NG - 1, 0)

            with sp.Fori(1, (PAIRS - 1) // 2) as m:
                for c in range(2):
                    sp.wait_ge(s_east, 2 * m + c - 1)
                    load_ea(m, c)
            sp.wait_ge(s_east, PAIRS - 2)
            load_ea((PAIRS - 1) // 2, 0)

            load_w(6)
            load_w(7)
            for j in range(2):
                sp.wait_ge(s_tabh[j], 16 * NG)
            sp.wait_ge(s_edge_done, 1)
            sp.wait_ge(s_pe_edge, 1)

            def rows_in(g):
                for j in range(2):
                    n = 2 * g + j
                    sp.dma_start(xt[j][:], x[bass.ds(n * P, P), :]).then_inc(s_ht2[j], 16)
                    sp.dma_start(ht[j][:], tab_h[bass.ds(n * P, P), :]).then_inc(s_ht2[j], 16)

            def h2_out(g):
                for j in range(2):
                    n = 2 * g + j
                    sp.wait_ge(s_h2, n + 1)
                    sp.dma_start(tab_h2[bass.ds(n * P, P), :], h2o[j][:]).then_inc(s_h2st[j], 16)

            rows_in(0)
            with sp.Fori(0, NG - 1) as g:
                h2_out(g)
                sp.wait_ge(s_x1r, 2 * g + 2)
                rows_in(g + 1)
            h2_out(NG - 1)

            with sp.Fori(0, NG) as g:
                for j in range(2):
                    n = 2 * g + j
                    sp.wait_ge(s_res, n + 1)
                    sp.dma_start(out[bass.ds(n * P, P), :], xt[j][:]).then_inc(s_out[j], 16)
            for j in range(2):
                sp.wait_ge(s_out[j], 16 * NG)
                sp.wait_ge(s_h2st[j], 16 * NG)

        @block.gpsimd
        def _(pool):
            pool.memset(b2raw[:], 0.0).then_inc(s_b2clear, 1)
            pool.memset(ones_b[:], 1.0).then_inc(s_ones, 1)

            def split_w(k):
                slot = W_SLOT[W_ORDER[k]]
                pool.wait_ge(s_whi, k + 1)
                pool.tensor_tensor(w_lo[slot][:], w_raw[k % 2][:], w_hi[slot][:].bitcast(F32),
                                   ALU.subtract).then_inc(s_wlo, 1)

            split_w(3)
            pool.memset(aggT[:], 0.0).then_inc(s_zero, 1)
            pool.wait_ge(s_const, N_CONST)

            def gather(m, c):
                p = 2 * m + c
                q = c % 2
                pool.tensor_copy(idx_ab[q][:, 0:2], src_i[:, bass.ds(2 * p, 2)]).then_inc(s_idx, 1)
                pool.tensor_copy(idx_ab[q][:, 2:4], dst_i[:, bass.ds(2 * p, 2)]).then_inc(s_idx, 1)
                pool.wait_ge(s_idx, 2 * p + 2)
                apart(pool)
                for j in range(2):
                    pool.indirect_dma_start(
                        out=ga[q][:, j, :], out_offset=None, in_=tab_a,
                        in_offset=bass.IndirectOffsetOnAxis(ap=idx_ab[q][:, j:j + 1], axis=0)
                    ).then_inc(s_ga[q][j], 16)
                    pool.indirect_dma_start(
                        out=gb[q][:, j, :], out_offset=None, in_=tab_b,
                        in_offset=bass.IndirectOffsetOnAxis(ap=idx_ab[q][:, 2 + j:3 + j], axis=0)
                    ).then_inc(s_gb[q][j], 16)

            for j in range(2):
                pool.wait_ge(s_tabh[j], 16 * NG)
                pool.wait_ge(s_taba[j], 16 * NG)
                pool.wait_ge(s_tabb[j], 16 * NG)
            gather(0, 0)
            gather(0, 1)

            def h1_low(m, c):
                p = 2 * m + c
                pool.wait_ge(s_h1hi, p + 1)
                pool.tensor_tensor(h1_lo[c % 2][:], h1f[:].rearrange("p a b -> p (a b)").rearrange(
                    "p (c e) -> p c e", c=C), h1_hi[c % 2][:].bitcast(F32), ALU.subtract).then_inc(s_h1s, 1)

            def step(m, c, more=True):
                p = 2 * m + c
                if more:
                    pool.wait_ge(s_pre1, p + 1)
                    gather(m, c + 2)
                h1_low(m, c)

            with pool.Fori(0, (PAIRS - 3) // 2) as m:
                step(m, 0)
                step(m, 1)
            step((PAIRS - 3) // 2, 0)
            split_w(4)
            step((PAIRS - 3) // 2, 1, False)
            split_w(5)
            step((PAIRS - 1) // 2, 0, False)
            pool.wait_ge(s_vec, 16 * len(vec))

            pool.wait_ge(s_edge_done, 1)

            def agg_low(g):
                pool.wait_ge(s_ghi, g + 1)
                apart(pool)
                pool.tensor_tensor(g_lo[:], aggT[:, 0:C, bass.ds(g * GW, GW)], g_hi[:].bitcast(F32),
                                   ALU.subtract).then_inc(s_gs, 1)

            def u_low(g):
                pool.wait_ge(s_uhi, g + 1)
                pool.tensor_tensor(u_lo[:].rearrange("p c e -> p (c e)"), r3[:].rearrange("p a b -> p (a b)"),
                                   u_hi[:].rearrange("p c e -> p (c e)").bitcast(F32),
                                   ALU.subtract).then_inc(s_us, 1)

            def rows(g):
                for j in range(2):
                    pool.wait_ge(s_ht2[j], 32 * g + 32)
                    pool.tensor_tensor(ht[j][:], ht[j][:], vec["b4"][:], ALU.add).then_inc(s_hb, 1)
                    pool.tensor_tensor(xt[j][:], xt[j][:], vec["beta0"][:], ALU.add).then_inc(s_xb, 1)

            agg_low(0)
            rows(0)
            agg_low(1)
            split_w(6)
            u_low(0)
            split_w(7)
            with pool.Fori(2, NG) as g:
                agg_low(g)
                u_low(g - 1)
                rows(g - 1)
            u_low(NG - 1)
            rows(NG - 1)
            pool.wait_ge(s_gs, NG)
            pool.memset(aggT[:], 0.0).then_inc(s_zero3, 1)

            for j in range(2):
                pool.wait_ge(s_h2st[j], 16 * NG)

            def gather3(octet, h, count=8, first=False):
                t = 8 * octet
                for j in range(count):
                    if j % 4 == 0 and not (first and octet == 0):
                        pool.wait_ge(s_seg3, t + j - 4)
                    if j == 0:
                        pool.tensor_copy(idx_r[h][:, 0:count], src_i[:, bass.ds(t, count)]).then_inc(s_idx3, 1)
                        pool.wait_ge(s_idx3, octet + 1)
                    if j % 4 == 0:
                        apart(pool)
                    pool.indirect_dma_start(
                        out=gr[j], out_offset=None, in_=tab_h2,
                        in_offset=bass.IndirectOffsetOnAxis(ap=idx_r[h][:, j:j + 1], axis=0)).then_inc(s_gr[j], 16)

            octets = -(-ET // 8)
            gather3(0, 0, first=True)
            gather3(1, 1)
            with pool.Fori(1, ET // 16) as k:
                for h in range(2):
                    gather3(2 * k + h, h)
            for octet in range(ET // 16 * 2, octets):
                gather3(octet, octet % 2, min(8, ET - 8 * octet))

            def nodes4(g):
                for j in range(2):
                    n = 2 * g + j
                    pool.wait_ge(s_mhi, n + 1)
                    apart(pool)
                    part = g_hi[:, :, j * P:(j + 1) * P]
                    pool.tensor_tensor(g_lo[:, :, j * P:(j + 1) * P], aggT[:, 0:C, bass.ds(n * P, P)],
                                       part.bitcast(F32), ALU.subtract).then_inc(s_ms, 1)
                    x1n = x1[:, bass.ds(n, 1), :].rearrange("p a d -> p (a d)")
                    pool.tensor_tensor(x1n, x1n, vec["beta1"][:], ALU.add).then_inc(s_xb4, 1)

            over_groups(pool, nodes4)

        @block.scalar
        def _(act):
            act.preload_act_table_set(SET_NAME)

            def h_rows(g):
                for j in range(2):
                    n = 2 * g + j
                    act.wait_ge(s_mv, n + 1)
                    act.activation(rs0[:, j, 0:1], mv0[:, j, 1:2], ACT.Ln, bias=EPS).then_inc(s_ln, 1)
                    act.wait_ge(s_ln, n + 1)
                    act.activation(rs0[:, j, 1:2], rs0[:, j, 0:1], ACT.Exp, scale=-0.5).then_inc(s_rstd, 1)
                    act.wait_ge(s_nmr, n + 1)
                    since(act, s_hTp, 2 * g)
                    since(act, s_tabh[j], 16 * g)
                    act.activation(hout[j][:], xin[j][:], ACT.Relu, bias=rs0[:, j, 2:3],
                                   scale=rs0[:, j, 1:2]).then_inc(s_h, 1)

            def a_out(g, j):
                act.wait_ge(s_aps, 2 * g + j + 1)
                since(act, s_taba[j], 16 * g)
                act.activation(a_sb[j][:], psum[:, 2 + j, :], ACT.Copy).then_inc(s_aev, 1)

            def nodes0(g, ahead, behind):
                if ahead:
                    h_rows(g + 1)
                a_out(g, 0)
                if not ahead:
                    a_out(g, 1)
                act.wait_ge(s_pps, g + 1)
                for c in range(C):
                    ins = act.activation(keep[:, bass.ds(g, 1), c * GW:(c + 1) * GW].rearrange("p a d -> p (a d)"),
                                         psum[:, 6 + c // 2, (c % 2) * GW:(c % 2 + 1) * GW],
                                         ACT.Identity, bias=b3col[:, c:c + 1])
                ins.then_inc(s_pev, 1)
                if ahead:
                    a_out(g, 1)

            h_rows(0)
            act.wait_ge(s_const, N_CONST)
            one_ahead(act, nodes0)

            def e1(m, c):
                act.wait_ge(s_pre1, 2 * m + c + 1)
                act.activation(r1[:], psum[:, 0:2, :], ACT.Exp).then_inc(s_e1, 1)

            def sq1(m, c):
                act.wait_ge(s_c1, 2 * m + c + 1)
                act.activation(r1[:], r1[:], ACT.Square, bias=1.0).then_inc(s_q1, 1)

            def ln1(m, c):
                act.wait_ge(s_q1, 2 * m + c + 1)
                act.activation(r1[:], r1[:], ACT.Ln, bias=1.0).then_inc(s_l1, 1)

            def x1q(m, c):
                act.wait_ge(s_l1, 2 * m + c + 1)
                act.activation(r1[:], r1[:], ACT.Exp, bias=LN2, scale=-1.0).then_inc(s_x1, 1)

            def e2(m, c):
                act.wait_ge(s_pre2, 2 * (2 * m + c) + 2)
                q = c % 2
                act.activation(r2[q][:], psum[:, 2 + 2 * q:4 + 2 * q, :], ACT.Exp, scale=-1.0).then_inc(s_e2, 1)

            def sq2(m, c):
                act.wait_ge(s_c2, 2 * m + c + 1)
                act.activation(r2[c % 2][:], r2[c % 2][:], ACT.Square, bias=1.0).then_inc(s_q2, 1)

            def ln2(m, c):
                act.wait_ge(s_q2, 2 * m + c + 1)
                act.activation(r2[c % 2][:], r2[c % 2][:], ACT.Ln, bias=1.0).then_inc(s_l2, 1)

            def x2q(m, c):
                act.wait_ge(s_l2, 2 * m + c + 1)
                act.activation(r2[c % 2][:], r2[c % 2][:], ACT.Exp, bias=LN2, scale=-1.0).then_inc(s_x2, 1)

            def step(m, c):
                e1(m, c + 1)
                sq2(m, c - 1)
                sq1(m, c + 1)
                ln2(m, c - 1)
                ln1(m, c + 1)
                x1q(m, c + 1)
                x2q(m, c - 1)
                e2(m, c)

            for c in range(2):
                e1(0, c)
                sq1(0, c)
                ln1(0, c)
                x1q(0, c)
            e2(0, 0)
            with act.Fori(0, (PAIRS - 3) // 2) as m:
                step(m, 1)
                step(m, 2)
            mm = (PAIRS - 3) // 2
            step(mm, 1)
            for c in (1, 2):
                sq2(mm, c)
                ln2(mm, c)
                x2q(mm, c)
                if c == 1:
                    e2(mm, 2)

            def rstd(j, s_m, s_l, s_r, k):
                act.wait_ge(s_m, k)
                act.activation(rs2[:, j, 0:1], mv2[:, j, 1:2], ACT.Ln, bias=EPS).then_inc(s_l, 1)
                act.wait_ge(s_l, k)
                act.activation(rs2[:, j, 1:2], rs2[:, j, 0:1], ACT.Exp, scale=-0.5).then_inc(s_r, 1)

            def mish3(g):
                act.wait_ge(s_c3, g + 1)
                act.activation(r3[:], r3[:], ACT.Exp).then_inc(s_e3, 1)
                act.wait_ge(s_e3, g + 1)
                act.activation(r3[:], r3[:], ACT.Square, bias=1.0).then_inc(s_q3, 1)
                act.wait_ge(s_q3, g + 1)
                act.activation(r3[:], r3[:], ACT.Ln, bias=1.0).then_inc(s_l3, 1)
                act.wait_ge(s_l3, g + 1)
                act.activation(r3[:], r3[:], ACT.Exp, bias=LN2, scale=-1.0).then_inc(s_x3, 1)

            def u_high(g):
                act.wait_ge(s_u, g + 1)
                since(act, s_o4, 2 * g)
                act.activation(u_hi[:].rearrange("p c e -> p (c e)"), r3[:].rearrange("p a b -> p (a b)"),
                               ACT.Copy).then_inc(s_uhi, 1)

            def h2_high(g):
                split_done(act, "Ws")
                for j in range(2):
                    n = 2 * g + j
                    act.wait_ge(s_h2T, n + 1)
                    since(act, s_qps, 2 * g)
                    act.activation(h2s[0][:, :, j * P:(j + 1) * P],
                                   psum[:, 4 + j, :].rearrange("p (c e) -> p c e", c=C), ACT.Copy
                                   ).then_inc(s_h2hi, 1)

            def nodes2(g, ahead, behind):
                if behind:
                    h2_high(g - 1)
                if ahead:
                    mish3(g + 1)
                for j in range(2):
                    rstd(j, s_mv2, s_ln2, s_rstd2, 4 * g + j + 1)
                if ahead:
                    u_high(g + 1)
                for j in range(2):
                    rstd(j, s_mv2, s_ln2, s_rstd2, 4 * g + j + 3)
                for j in range(2):
                    n = 2 * g + j
                    act.wait_ge(s_nmr2, n + 1)
                    since(act, s_h2st[j], 16 * g)
                    act.activation(h2o[j][:], x1[:, bass.ds(n, 1), :].rearrange("p a d -> p (a d)"), ACT.Relu,
                                   bias=rs2[:, j, 2:3], scale=rs2[:, j, 1:2]).then_inc(s_h2, 1)

            mish3(0)
            u_high(0)
            one_ahead(act, nodes2)
            h2_high(NG - 1)

            def sum_high(g):
                for j in range(2):
                    n = 2 * g + j
                    since(act, s_nps, n - 1 if not isinstance(g, int) or g else 0)
                    act.activation(g_hi[:, :, j * P:(j + 1) * P], aggT[:, 0:C, bass.ds(n * P, P)], ACT.Copy
                                   ).then_inc(s_mhi, 1)

            act.wait_ge(s_sum3, 1)
            sum_high(0)
            with act.Fori(0, NG - 1) as g:
                sum_high(g + 1)
                for j in range(2):
                    rstd(j, s_mv4, s_ln4, s_rstd4, 2 * g + j + 1)
            for j in range(2):
                rstd(j, s_mv4, s_ln4, s_rstd4, 2 * (NG - 1) + j + 1)

        @block.vector
        def _(dve):
            dve.memset(ones_r[:].bitcast(F32), 1.0).then_inc(s_ones_r, 1)

            def split_w(k):
                slot = W_SLOT[W_ORDER[k]]
                dve.wait_ge(s_wraw[k % 2], 16 * (k // 2 + 1))
                dve.tensor_copy(w_hi[slot][:], w_raw[k % 2][:]).then_inc(s_whi, 1)

            def low_w(k):
                slot = W_SLOT[W_ORDER[k]]
                dve.wait_ge(s_whi, k + 1)
                dve.tensor_tensor(w_lo[slot][:], w_raw[k % 2][:], w_hi[slot][:].bitcast(F32),
                                  ALU.subtract).then_inc(s_wlo_dve, 1)

            def ln0(g, j):
                n = 2 * g + j
                dve.wait_ge(s_xin[j], 16 * g + 16)
                apart(dve)
                dve.bn_stats(bn0[:, j, :], xin[j][:]).then_inc(s_bn, 1)
                dve.wait_ge(s_bn, n + 1)
                apart(dve)
                dve.bn_aggr(mv0[:, j, :], bn0[:, j, :]).then_inc(s_mv, 1)
                dve.wait_ge(s_rstd, n + 1)
                dve.wait_ge(s_mv, n + 1)
                dve.tensor_scalar(rs0[:, j, 2:3], mv0[:, j, 0:1], -1.0, rs0[:, j, 1:2],
                                  ALU.mult, ALU.mult).then_inc(s_nmr, 1)

            def hT_parts(g, j):
                n = 2 * g + j
                dve.wait_ge(s_hTp, n + 1)
                pt = psum[:, j, :].rearrange("p (c e) -> p c e", c=C)
                dve.tensor_copy(hT_hi[:, :, j * P:(j + 1) * P], pt).then_inc(s_hThi, 1)
                dve.wait_ge(s_hThi, n + 1)
                dve.tensor_tensor(hT_lo[:, :, j * P:(j + 1) * P], pt,
                                  hT_hi[:, :, j * P:(j + 1) * P].bitcast(F32), ALU.subtract).then_inc(s_hT, 1)

            def constants():
                dve.wait_ge(s_const, N_CONST)
                dve.tensor_reduce(dr_min[:], dr[:], AX.X, ALU.min).then_inc(s_ix, 1)
                dve.tensor_reduce(dr_max[:], dr[:], AX.X, ALU.max).then_inc(s_ix, 1)
                dve.wait_ge(s_ix, 2)
                dve.tensor_scalar(dr_min[:], dr_min[:], float(LAST_BASE), None, ALU.min).then_inc(s_ix, 1)
                dve.wait_ge(s_ix, 3)
                dve.tensor_copy(dr_base[:], dr_min[:]).then_inc(s_ix, 1)
                dve.tensor_tensor(dr_span[:], dr_max[:], dr_min[:], ALU.subtract).then_inc(s_ix, 1)
                dve.tensor_copy(w1c_hi[:], w1c_raw[:]).then_inc(s_b2, 1)
                dve.tensor_scalar(b2rows[:], b2raw[:], -1.0, None, ALU.mult).then_inc(s_b2, 1)
                dve.wait_ge(s_b2, 2)
                dve.tensor_tensor(w1c_lo[:], w1c_raw[:], w1c_hi[:].bitcast(F32), ALU.subtract).then_inc(s_b2, 1)
                dve.scalar_tensor_tensor(b2rows[32:64, :], b2raw[32:64, :], -1.0, b2rows[32:64, :].bitcast(F32),
                                         ALU.mult, ALU.subtract).then_inc(s_b2, 1)
                split_w(3)

            def node_group(g, ahead, behind):
                if ahead:
                    for j in range(2):
                        ln0(g + 1, j)
                if not behind:
                    constants()
                for j in range(2):
                    n = 2 * g + j
                    dve.wait_ge(s_bps, n + 1)
                    if ahead:
                        hT_parts(g + 1, j)
                    since(dve, s_tabb[j], 16 * g)
                    dve.tensor_tensor(b_sb[j][:], psum[:, 4 + j, :], b1b[:], ALU.add).then_inc(s_bev, 1)

            for j in range(2):
                ln0(0, j)
            split_w(0)
            hT_parts(0, 0)
            low_w(0)
            split_w(1)
            hT_parts(0, 1)
            low_w(1)
            split_w(2)
            low_w(2)
            one_ahead(dve, node_group)

            dve.wait_ge(s_basein, 32)
            dve.tensor_reduce(span_max[:], span_row[:], AX.X, ALU.max).then_inc(s_ix, 1)
            dve.tensor_copy(dst_f[:], dst_i[:]).then_inc(s_ix, 1)
            dve.wait_ge(s_ix, 7)
            for j in range(4):
                of_quad = [a[:].rearrange("p (q b) -> p q b", b=4)[:, :, j] for a in (dst_rel, dst_f)]
                dve.tensor_tensor(of_quad[0], of_quad[1], base_b[:], ALU.subtract).then_inc(s_ix, 1)
            dve.wait_ge(s_ix, 11)

            def ea_split(m, c):
                q = c % 2
                p = 2 * m + c
                dve.wait_ge(s_ea[q], 32 * (m + c // 2) + 32)
                dve.tensor_copy(ea_st[q][:], ea_raw[q][:]).then_inc(s_eahi, 1)
                dve.wait_ge(s_eahi, p + 1)
                dve.tensor_tensor(ea_st[q][DE:P, :], ea_raw[q][DE:P, :], ea_st[q][DE:P, :].bitcast(F32),
                                  ALU.subtract).then_inc(s_east, 1)

            def ab_sum(m, c):
                q = c % 2
                for j in range(2):
                    dve.wait_ge(s_ga[q][j], 16 * (m + c // 2) + 16)
                    dve.wait_ge(s_gb[q][j], 16 * (m + c // 2) + 16)
                dve.tensor_tensor(ga[q][:], ga[q][:], gb[q][:], ALU.add).then_inc(s_ab, 1)

            def cap1(m, c):
                dve.wait_ge(s_e1, 2 * m + c + 1)
                dve.tensor_scalar(r1[:], r1[:], EXP_CAP, None, ALU.min).then_inc(s_c1, 1)

            def cap2(m, c):
                dve.wait_ge(s_e2, 2 * m + c + 1)
                dve.tensor_scalar(r2[c % 2][:], r2[c % 2][:], EXP_CAP, None, ALU.min).then_inc(s_c2, 1)

            def tail1(m, c):
                p = 2 * m + c
                dve.wait_ge(s_x1, p + 1)
                since(dve, s_h1s, p)
                for b in range(2):
                    dve.scalar_tensor_tensor(h1f[:, b, :], r1[:, b, :], 1.0, psum[:, b, :],
                                             ALU.subtract, ALU.mult).then_inc(s_h1, 1)

            def h1_high(m, c, first=False):
                p = 2 * m + c
                dve.wait_ge(s_h1, 2 * p + 2)
                if not first:
                    dve.wait_ge(s_pre2, 2 * p - 2)
                dve.tensor_copy(h1_hi[c % 2][:].rearrange("p c e -> p (c e)"),
                                h1f[:].rearrange("p a b -> p (a b)")).then_inc(s_h1hi, 1)

            def tail2(m, c):
                q = c % 2
                dve.wait_ge(s_x2, 2 * m + c + 1)
                for j in range(2):
                    dve.scalar_tensor_tensor(r2[q][:, j, :], r2[q][:, j, :], 1.0, psum[:, 2 + 2 * q + j, :],
                                             ALU.subtract, ALU.mult).then_inc(s_msg, 1)

            def edges(sorted_tiles):

                def hots(m, c):
                    p = 2 * m + c
                    for j in range(2):
                        dve.tensor_scalar(onehot[2 * (c % 2) + j][:], iota[:, 0:P],
                                          dst_rel[:, bass.ds(2 * p + j, 1)], None, ALU.is_equal).then_inc(s_hot, 1)

                def add(m, c):
                    p = 2 * m + c
                    base = dve.value_load(base_b[0:1, bass.ds(m + c // 2, 1)], min_val=0, max_val=LAST_BASE)
                    dve.wait_ge(s_seg, p + 1)
                    dve.wait_ge(s_agg, p)
                    dst = aggT[:, 0:C, bass.ds(base, P)]
                    dve.tensor_tensor(dst, dst, psum[:, 6 + c % 2, :].rearrange("p (c e) -> p c e", c=C),
                                      ALU.add).then_inc(s_agg, 1)

                def every_window(m, c):
                    p = 2 * m + c
                    for j in range(2):
                        t = 2 * p + j
                        with dve.Fori(0, NT // 2) as k:
                            for b in range(2):
                                nth = t * NT + 2 * k + b
                                dve.wait_ge(s_agg, nth + 1)
                                dve.tensor_scalar(onehot[b][:], iota[:], windows[:, bass.ds(2 * k + b, 1)],
                                                  dst_f[:, bass.ds(t, 1)], ALU.add, ALU.is_equal).then_inc(s_hot, 1)
                                dve.wait_ge(s_seg, nth + 1)
                                dst = aggT[:, 0:C, bass.ds((2 * k + b) * P, P)]
                                dve.tensor_tensor(dst, dst, psum[:, 6 + b, :].rearrange("p (c e) -> p c e", c=C),
                                                  ALU.add).then_inc(s_agg, 1)

                add_up = add if sorted_tiles else every_window

                def step(m, c, begun=2, last=False, ea=True, ab=True):
                    if not last:
                        cap1(m, c + 1)
                    if begun >= 2:
                        add_up(m, c - 2)
                    if begun >= 1 and sorted_tiles:
                        hots(m, c - 1)
                    if ea:
                        ea_split(m, c + 3)
                    if ab:
                        ab_sum(m, c + 2)
                    if not last:
                        tail1(m, c + 1)
                    if begun >= 1:
                        tail2(m, c - 1)
                    if not last:
                        h1_high(m, c + 1, begun == 0)
                    cap2(m, c)

                if not sorted_tiles:
                    dve.sem_inc(s_agg, 1)
                cap1(0, 0)
                tail1(0, 0)
                h1_high(0, 0, first=True)
                for c in range(3):
                    step(0, c, begun=c)
                with dve.Fori(1, (PAIRS - 5) // 2) as m:
                    step(m, 1)
                    step(m, 2)
                mm = (PAIRS - 5) // 2
                step(mm, 1)
                split_w(4)
                step(mm, 2, ea=False)
                split_w(5)
                step(mm, 3, ea=False, ab=False)
                step(mm, 4, ea=False, ab=False, last=True)
                tail2(mm, 4)
                if sorted_tiles:
                    hots(mm, 4)
                add_up(mm, 3)
                add_up(mm, 4)
                dve.wait_ge(s_agg, PAIRS if sorted_tiles else ET * NT + 1)

            ea_split(0, 0)
            ea_split(0, 1)
            ab_sum(0, 0)
            ab_sum(0, 1)
            dve.wait_ge(s_pre1, 1)
            ea_split(0, 2)
            dve.wait_ge(s_zero, 1)
            widest = dve.value_load(span_max[:], min_val=0, max_val=NP)
            with dve.If(widest < P):
                edges(True)
            with dve.Else():
                edges(False)
            dve.memset(z3[:, 0, 0:1], 0.0).then_inc(s_edge_done, 1)

            dve.wait_ge(s_edge_done, 1)
            dve.wait_ge(s_vec, 16 * len(vec))

            def agg_high(g):
                since(dve, s_z3p, g)
                dve.tensor_copy(g_hi[:], aggT[:, 0:C, bass.ds(g * GW, GW)]).then_inc(s_ghi, 1)

            def z3_in(g):
                dve.wait_ge(s_z3p, g + 1)
                since(dve, s_u, g)
                dve.tensor_tensor(z3[:].rearrange("p a b -> p (a b)"),
                                  keep[:, bass.ds(g, 1), :].rearrange("p a d -> p (a d)"),
                                  psum[:, 0:2, :].rearrange("p a b -> p (a b)"), ALU.add).then_inc(s_z3, 1)
                dve.wait_ge(s_z3, g + 1)
                since(dve, s_us, g)
                dve.tensor_scalar(r3[:], z3[:], Z_CAP, None, ALU.min).then_inc(s_c3, 1)

            def u_out(g):
                dve.wait_ge(s_x3, g + 1)
                dve.scalar_tensor_tensor(r3[:], r3[:], 1.0, z3[:], ALU.subtract, ALU.mult).then_inc(s_u, 1)

            def h2_low(g):
                for j in range(2):
                    n = 2 * g + j
                    part = slice(j * P, (j + 1) * P)
                    dve.wait_ge(s_h2hi, n + 1)
                    dve.tensor_tensor(h2s[1][:, :, part], psum[:, 4 + j, :].rearrange("p (c e) -> p c e", c=C),
                                      h2s[0][:, :, part].bitcast(F32), ALU.subtract).then_inc(s_h2s, 1)

            def q_out(g):
                for j in range(2):
                    dve.wait_ge(s_qps, 2 * g + j + 1)
                    dve.tensor_tensor(keep[:, bass.ds(g, 1), j * D:(j + 1) * D].rearrange("p a d -> p (a d)"),
                                      psum[:, 6 + j, :], vec["bias1"][:], ALU.add).then_inc(s_q, 1)

            def x1_of(n):
                return x1[:, bass.ds(n, 1), :].rearrange("p a d -> p (a d)")

            def moments(j, rows, k):
                apart(dve)
                dve.bn_stats(bn2[:, j, :], rows).then_inc(s_bn2, 1)
                dve.wait_ge(s_bn2, k + 1)
                apart(dve)
                dve.bn_aggr(mv2[:, j, :], bn2[:, j, :]).then_inc(s_mv2, 1)

            def nodes2(g, ahead, behind):
                if ahead:
                    z3_in(g + 1)
                if ahead == 2:
                    agg_high(g + 2)
                if behind:
                    h2_low(g - 1)
                for j in range(2):
                    n = 2 * g + j
                    dve.wait_ge(s_o4, n + 1)
                    dve.wait_ge(s_hb, n + 1)
                    dve.tensor_tensor(ht[j][:], ht[j][:], psum[:, 2 + j, :], ALU.subtract).then_inc(s_y, 1)
                    dve.wait_ge(s_y, n + 1)
                    moments(j, ht[j][:], 4 * g + j)
                if ahead:
                    u_out(g + 1)
                for j in range(2):
                    dve.wait_ge(s_mv2, 4 * g + j + 1)
                    dve.scalar_tensor_tensor(ht[j][:], ht[j][:], mv2[:, j, 0:1], vec["gamma0"][:],
                                             ALU.subtract, ALU.mult).then_inc(s_t2, 1)
                for j in range(2):
                    n = 2 * g + j
                    dve.wait_ge(s_rstd2, 4 * g + j + 1)
                    dve.wait_ge(s_xb, n + 1)
                    dve.wait_ge(s_t2, n + 1)
                    dve.scalar_tensor_tensor(x1_of(n), ht[j][:], rs2[:, j, 1:2], xt[j][:],
                                             ALU.mult, ALU.add).then_inc(s_x1r, 1)
                    dve.wait_ge(s_x1r, n + 1)
                    moments(j, x1_of(n), 4 * g + 2 + j)
                for j in range(2):
                    dve.wait_ge(s_mv2, 4 * g + 3 + j)
                    dve.wait_ge(s_rstd2, 4 * g + 3 + j)
                    dve.tensor_scalar(rs2[:, j, 2:3], mv2[:, j, 0:1], -1.0, rs2[:, j, 1:2],
                                      ALU.mult, ALU.mult).then_inc(s_nmr2, 1)
                if behind:
                    q_out(g - 1)

            agg_high(0)
            split_w(6)
            agg_high(1)
            z3_in(0)
            u_out(0)
            split_w(7)
            one_ahead(dve, nodes2)
            h2_low(NG - 1)
            q_out(NG - 1)

            dve.wait_ge(s_zero3, 1)

            def seg3(b):
                return psum[:, 2 * b:2 * b + 2, :].rearrange("p a b -> p (a b)")[:, 0:(C + 1) * P].rearrange(
                    "p (c e) -> p c e", c=C + 1)

            def hot(t, j):
                for one in (one3, count3):
                    ins = dve.tensor_scalar(one[j][:], iota[:], dst_rel[:, bass.ds(t, 1)], None, ALU.is_equal)
                ins.then_inc(s_hot3, 1)

            def neighbours(sorted_tiles):
                if sorted_tiles:
                    def add(quad, b, count=4, more=4):
                        for j in range(4):
                            if j < more:
                                dve.wait_ge(s_seg3, 4 * quad + j + 1)
                                hot(4 * quad + j + 4, j)
                            if j == 0:
                                base = dve.value_load(base_b[0:1, bass.ds(quad, 1)], min_val=0, max_val=LAST_BASE)
                        dve.wait_ge(s_seg3, 4 * quad + count)
                        dve.wait_ge(s_agg3, quad)
                        dst = aggT[:, :, bass.ds(base, P)]
                        dve.tensor_tensor(dst, dst, seg3(b), ALU.add).then_inc(s_agg3, 1)

                    for j in range(4):
                        hot(j, j)
                    for b in range(2):
                        add(b, b)
                    with dve.Fori(1, (QUADS - 2) // 2) as k:
                        for b in range(2):
                            add(2 * k + b, b)
                    add(QUADS - 2, 0, more=LAST_QUAD)
                    add(QUADS - 1, 1, count=LAST_QUAD, more=0)
                    dve.wait_ge(s_agg3, QUADS)
                else:
                    dve.sem_inc(s_agg3, 1)
                    with dve.Fori(0, ET) as t:
                        with dve.Fori(0, NT // 2) as k:
                            for b in range(2):
                                nth = t * NT + 2 * k + b
                                dve.wait_ge(s_agg3, nth + 1)
                                for one in (one3, count3):
                                    ins = dve.tensor_scalar(one[b][:], iota[:], windows[:, bass.ds(2 * k + b, 1)],
                                                            dst_f[:, bass.ds(t, 1)], ALU.add, ALU.is_equal)
                                ins.then_inc(s_hot3, 1)
                                dve.wait_ge(s_winsum, nth + 1)
                                dst = aggT[:, :, bass.ds((2 * k + b) * P, P)]
                                dve.tensor_tensor(dst, dst, seg3(b), ALU.add).then_inc(s_agg3, 1)
                    dve.wait_ge(s_agg3, ET * NT + 1)

            with dve.If(widest < P):
                neighbours(True)
            with dve.Else():
                neighbours(False)

            dve.wait_ge(s_n3, 1)
            dve.sem_inc(s_sum3, 1)

            dve.wait_ge(s_degp, 1)
            dve.tensor_scalar(degree[:], psum[:, 0, 0:NT], 1.0, None, ALU.max).then_inc(s_mean, 1)
            dve.wait_ge(s_mean, 1)
            dve.reciprocal(degree[:], degree[:]).then_inc(s_mean, 1)
            dve.wait_ge(s_mean, 2)

            def nodes4(g):
                since(dve, s_res, 2 * g)
                for j in range(2):
                    n = 2 * g + j
                    dve.wait_ge(s_nps, n + 1)
                    dve.scalar_tensor_tensor(ht[j][:], psum[:, 4 + j, :], degree[:, bass.ds(n, 1)],
                                             keep[:, bass.ds(g, 1), j * D:(j + 1) * D].rearrange("p a d -> p (a d)"),
                                             ALU.mult, ALU.add).then_inc(s_h4, 1)
                    dve.wait_ge(s_h4, n + 1)
                    apart(dve)
                    dve.bn_stats(bn2[:, j, :], ht[j][:]).then_inc(s_bn4, 1)
                    dve.wait_ge(s_bn4, n + 1)
                    apart(dve)
                    dve.bn_aggr(mv2[:, j, :], bn2[:, j, :]).then_inc(s_mv4, 1)
                for j in range(2):
                    dve.wait_ge(s_mv4, 2 * g + j + 1)
                    dve.scalar_tensor_tensor(ht[j][:], ht[j][:], mv2[:, j, 0:1], vec["gamma1"][:],
                                             ALU.subtract, ALU.mult).then_inc(s_t4, 1)
                for j in range(2):
                    n = 2 * g + j
                    dve.wait_ge(s_rstd4, n + 1)
                    dve.wait_ge(s_xb4, n + 1)
                    dve.wait_ge(s_t4, n + 1)
                    since(dve, s_out[j], 16 * g)
                    dve.scalar_tensor_tensor(xt[j][:], ht[j][:], rs2[:, j, 1:2], x1_of(n),
                                             ALU.mult, ALU.add).then_inc(s_res, 1)

            over_groups(dve, nodes4)

        @block.tensor
        def _(pe):
            def square(o, lhs_hi, lhs_lo, name, e0, first=True, last=True):
                slot = W_SLOT[name]
                for c in range(C):
                    cols = slice(e0, e0 + P)
                    mm = three_pass(pe, o, lhs_hi[:, c, cols], lhs_lo[:, c, cols], w_hi[slot][:, c, :],
                                    w_lo[slot][:, c, :], first and c == 0, last and c == C - 1)
                return mm

            def turned(bank, name, rhs_hi, rhs_lo):
                slot = W_SLOT[name]
                for f in range(C):
                    o = psum[:, bank + f // 2, (f % 2) * GW:(f % 2 + 1) * GW]
                    for c in range(C):
                        cols = slice(f * P, (f + 1) * P)
                        mm = three_pass(pe, o, w_hi[slot][:, c, cols], w_lo[slot][:, c, cols], rhs_hi[:, c, :],
                                        rhs_lo[:, c, :], c == 0, c == C - 1)
                return mm

            pe.wait_ge(s_ident, 16)

            def h_turned(g):
                for j in range(2):
                    pe.wait_ge(s_h, 2 * g + j + 1)
                    since(pe, s_hT, 2 * g)
                    for c in range(C):
                        tr = pe.transpose(psum[:, j, c * P:(c + 1) * P], hout[j][:, c * P:(c + 1) * P], ident[:])
                    tr.then_inc(s_hTp, 1)

            def a_product(g, j):
                pe.wait_ge(s_hT, 2 * g + j + 1)
                since(pe, s_aev, 2 * g)
                square(psum[:, 2 + j, :], hT_hi, hT_lo, "W1a", j * P).then_inc(s_aps, 1)

            def b_product(g, j):
                since(pe, s_bev, 2 * g)
                square(psum[:, 4 + j, :], hT_hi, hT_lo, "W1b", j * P).then_inc(s_bps, 1)

            def p_product(g):
                pe.wait_ge(s_hT, 2 * g + 2)
                split_done(pe, "W3a")
                since(pe, s_pev, g)
                turned(6, "W3a", hT_hi, hT_lo).then_inc(s_pps, 1)

            def nodes0(g, ahead, behind):
                split_done(pe, "W1a")
                a_product(g, 0)
                if ahead:
                    p_product(g)
                split_done(pe, "W1b")
                b_product(g, 0)
                if ahead:
                    h_turned(g + 1)
                a_product(g, 1)
                b_product(g, 1)
                if not ahead:
                    p_product(g)

            h_turned(0)
            one_ahead(pe, nodes0)

            split_done(pe, "W2")
            pe.wait_ge(s_b2, 4)
            pe.wait_ge(s_ones, 1)
            pe.wait_ge(s_ones_r, 1)

            def z1(m, c, first=False):
                p = 2 * m + c
                q = c % 2
                pe.wait_ge(s_east, p + 1)
                pe.wait_ge(s_ab, p + 1)
                for f in range(C):
                    if not first and f % 2 == 0:
                        pe.wait_ge(s_h1, 2 * p - 1 + f // 2)
                    cols = slice(f * P, (f + 1) * P)
                    at = (f % 2) * GW
                    o = psum[:, f // 2, at:at + GW]
                    pe.matmul(o, w1c_hi[:, cols], ea_st[q][:], start=True, stop=False)
                    pe.matmul(o, w1c_lo[:, cols], ea_st[q][:], start=False, stop=False)
                    for j in range(2):
                        oj = psum[:, f // 2, at + j * P:at + (j + 1) * P]
                        mm = pe.matmul(oj, ga[q][:, j, cols], ident[:], is_transpose=True, start=False, stop=j == 1)
                mm.then_inc(s_pre1, 1)

            def z2(m, c, early=False):
                p = 2 * m + c
                q = c % 2
                slot = W_SLOT["W2"]
                pe.wait_ge(s_h1hi, p + 1)
                if not early:
                    pe.wait_ge(s_msg, 2 * p - 2)
                for j in range(2):
                    o = psum[:, 2 + 2 * q + j, :]
                    pe.matmul(o, ones_r[:], b2rows[:], start=True, stop=False)
                    for k in range(C):
                        for part in (w_hi, w_lo):
                            pe.matmul(o, h1_hi[q][:, k, j * P:(j + 1) * P], part[slot][:, k, :],
                                      start=False, stop=False)
                pe.wait_ge(s_h1s, p + 1)
                for j in range(2):
                    for k in range(C):
                        mm = pe.matmul(psum[:, 2 + 2 * q + j, :], h1_lo[q][:, k, j * P:(j + 1) * P],
                                       w_hi[slot][:, k, :], start=False, stop=k == C - 1)
                    mm.then_inc(s_pre2, 1)

            def edges(sorted_tiles):
                def sums(m, c, first=False):
                    p = 2 * m + c
                    q = c % 2
                    pe.wait_ge(s_msg, 2 * p + 2)
                    pe.wait_ge(s_hot, 2 * p + 2)
                    if not first:
                        pe.wait_ge(s_agg, p - 1)
                    for f in range(C):
                        for j in range(2):
                            mm = pe.matmul(psum[:, 6 + q, f * P:(f + 1) * P], r2[q][:, j, f * P:(f + 1) * P],
                                           onehot[2 * q + j][:], start=j == 0, stop=j == 1)
                    mm.then_inc(s_seg, 1)

                def every_window(m, c, first=False):
                    p = 2 * m + c
                    q = c % 2
                    for j in range(2):
                        t = 2 * p + j
                        pe.wait_ge(s_msg, t + 1)
                        apart(pe)
                        with pe.Fori(0, NT // 2) as k:
                            for b in range(2):
                                pe.wait_ge(s_hot, t * NT + 2 * k + b + 1)
                                for f in range(C):
                                    mm = pe.matmul(psum[:, 6 + b, f * P:(f + 1) * P],
                                                   r2[q][:, j, f * P:(f + 1) * P], onehot[b][:],
                                                   start=True, stop=True)
                                mm.then_inc(s_seg, 1)

                add_up = sums if sorted_tiles else every_window

                def step(m, c, more=True):
                    add_up(m, c - 2)
                    z2(m, c)
                    if more:
                        z1(m, c + 2)

                z1(0, 1)
                z2(0, 0, early=True)
                z1(0, 2)
                z2(0, 1, early=True)
                z1(0, 3)
                add_up(0, 0, first=True)
                z2(0, 2)
                z1(0, 4)
                mm = (PAIRS - 3) // 2
                with pe.Fori(1, mm) as m:
                    step(m, 1)
                    step(m, 2)
                step(mm, 1, more=False)
                step(mm, 2, more=False)
                add_up(mm, 1)
                add_up(mm, 2)

            z1(0, 0, first=True)
            pe.wait_ge(s_ix, 6)
            widest = pe.value_load(span_max[:], min_val=0, max_val=NP)
            with pe.If(widest < P):
                edges(True)
            with pe.Else():
                edges(False)
            pe.sem_inc(s_pe_edge, 1)

            split_done(pe, "W3b")
            def z3_product(g):
                pe.wait_ge(s_gs, g + 1)
                since(pe, s_z3, g)
                turned(0, "W3b", g_hi, g_lo).then_inc(s_z3p, 1)

            def h2_turned(g):
                for j in range(2):
                    pe.wait_ge(s_h2, 2 * g + j + 1)
                    since(pe, s_h2s, 2 * g)
                    for c in range(C):
                        tr = pe.transpose(psum[:, 4 + j, c * P:(c + 1) * P], h2o[j][:, c * P:(c + 1) * P], ident[:])
                    tr.then_inc(s_h2T, 1)

            def q_product(g):
                split_done(pe, "Ws")
                for j in range(2):
                    pe.wait_ge(s_h2s, 2 * g + j + 1)
                    since(pe, s_q, 2 * g)
                    square(psum[:, 6 + j, :], h2s[0], h2s[1], "Ws", j * P).then_inc(s_qps, 1)

            def nodes2(g, ahead, behind):
                if ahead:
                    z3_product(g + 1)
                if behind:
                    h2_turned(g - 1)
                pe.wait_ge(s_us, g + 1)
                split_done(pe, "W4")
                for j in range(2):
                    since(pe, s_y, 2 * g)
                    square(psum[:, 2 + j, :], u_hi, u_lo, "W4", j * P).then_inc(s_o4, 1)
                if behind:
                    q_product(g - 1)

            z3_product(0)
            one_ahead(pe, nodes2)
            h2_turned(NG - 1)
            q_product(NG - 1)

            def sum3(j, hot, b, first=True, last=True):
                for f in range(C):
                    pe.matmul(psum[:, 2 * b, f * P:(f + 1) * P], gr[j][:, f * P:(f + 1) * P], one3[hot][:],
                              start=first and f == 0, stop=last and f == C - 1)
                return pe.matmul(psum[:, 2 * b + 1, 0:P], ones_b[:], count3[hot][:], start=first, stop=last)


            def quad3(use, b, count=4, early=False):
                quad = 2 * use + b
                if not early:
                    pe.wait_ge(s_agg3, quad - 1)
                for j in range(count):
                    pe.wait_ge(s_gr[4 * b + j], 16 * (use + 1))
                    pe.wait_ge(s_hot3, 4 * quad + j + 1)
                    sum3(4 * b + j, j, b, j == 0, j == count - 1).then_inc(s_seg3, 1)

            def neighbours(sorted_tiles):
                if sorted_tiles:
                    for b in range(2):
                        quad3(0, b, early=True)
                    with pe.Fori(1, (QUADS - 2) // 2) as k:
                        for b in range(2):
                            quad3(k, b)
                    quad3((QUADS - 2) // 2, 0)
                    quad3((QUADS - 2) // 2, 1, LAST_QUAD)
                else:
                    def windows(t, j, use):
                        pe.wait_ge(s_gr[j], 16 * use)
                        apart(pe)
                        with pe.Fori(0, NT // 2) as k:
                            for b in range(2):
                                pe.wait_ge(s_hot3, t * NT + 2 * k + b + 1)
                                sum3(j, b, b).then_inc(s_winsum, 1)
                        pe.wait_ge(s_winsum, t * NT + NT)
                        pe.sem_inc(s_seg3, 1)

                    with pe.Fori(0, ET // 8) as k:
                        for j in range(8):
                            windows(8 * k + j, j, k + 1)
                    for j in range(ET % 8):
                        windows(ET // 8 * 8 + j, j, ET // 8 + 1)

            with pe.If(widest < P):
                neighbours(True)
            with pe.Else():
                neighbours(False)
            pe.sem_inc(s_n3, 1)

            pe.wait_ge(s_sum3, 1)
            for n in range(NT):
                mm = pe.matmul(psum[:, 0, n:n + 1], aggT[:, C, n * P:(n + 1) * P], ident[:, 0:1],
                               start=True, stop=True)
            mm.then_inc(s_degp, 1)
            split_done(pe, "Wn")

            def nodes4(g):
                for j in range(2):
                    n = 2 * g + j
                    pe.wait_ge(s_ms, n + 1)
                    since(pe, s_h4, n - 1)
                    square(psum[:, 4 + j, :], g_hi, g_lo, "Wn", j * P).then_inc(s_nps, 1)

            over_groups(pe, nodes4)


def kernel(x, src, dst, edge_attr_64, L0_gnn_W1, L0_gnn_b1, L0_gnn_W2, L0_gnn_b2, L0_gnn_W3, L0_gnn_b3,
           L0_gnn_W4, L0_gnn_b4, L0_gnn_gamma, L0_gnn_beta, L1_gnn_W_self, L1_gnn_W_neigh, L1_gnn_bias,
           L1_gnn_gamma, L1_gnn_beta):
    import concourse.bacc as bacc
    from concourse.bass_utils import run_bass_kernel_spmd

    W1, W3 = np.asarray(L0_gnn_W1), np.asarray(L0_gnn_W3)
    row = lambda a: np.ascontiguousarray(np.asarray(a).reshape(1, -1))
    pad_edges = QUADS * 4 * P - N_EDGES
    src_p = np.concatenate([np.asarray(src), np.zeros(pad_edges, np.int32)])
    dst_p = np.concatenate([np.asarray(dst), np.full(pad_edges, N_NODES, np.int32)])
    ea = np.concatenate([np.asarray(edge_attr_64), np.zeros((EP - N_EDGES, DE), np.float32)])
    arrays = {
        "x": np.concatenate([np.asarray(x), np.zeros((NP - N_NODES, D), np.float32)]),
        "src_t": np.ascontiguousarray(src_p.reshape(4 * QUADS, P).T),
        "dst_t": np.ascontiguousarray(dst_p.reshape(4 * QUADS, P).T),
        "dst_r": np.ascontiguousarray(dst_p.reshape(QUADS, 4 * P)),
        "ea_t": np.ascontiguousarray(ea.T),
        "ident_d": np.eye(P, dtype=np.float32),
        "iota_d": np.concatenate([np.arange(P), P * np.arange(NT)]).astype(np.float32).reshape(1, -1),
    }
    weights = {
        "W1a": W1[0:D], "W1b": W1[D:2 * D], "W1c": W1[2 * D:], "W2": L0_gnn_W2, "W3a": W3[0:D], "W3b": W3[D:],
        "W4": L0_gnn_W4, "Ws": np.asarray(L1_gnn_W_self).T, "Wn": np.asarray(L1_gnn_W_neigh).T,
    }
    vectors = {
        "b1": L0_gnn_b1, "b2": L0_gnn_b2, "b3": L0_gnn_b3, "b4": L0_gnn_b4, "gamma0": L0_gnn_gamma,
        "beta0": L0_gnn_beta, "bias1": L1_gnn_bias, "gamma1": L1_gnn_gamma, "beta1": L1_gnn_beta,
    }
    arrays.update({f"w_{k}": np.ascontiguousarray(a) for k, a in weights.items()})
    arrays.update({f"v_{k}": row(a) for k, a in vectors.items()})

    nc = bacc.Bacc("TRN2", target_bir_lowering=False, num_devices=1)
    aps = {k: nc.dram_tensor(k, a.shape, mybir.dt.from_np(a.dtype), kind="ExternalInput").ap()
           for k, a in arrays.items()}
    out = nc.dram_tensor("out", [NP, D], F32, kind="ExternalOutput").ap()
    build(nc, aps["x"], aps["src_t"], aps["dst_t"], aps["dst_r"], aps["ea_t"], aps["ident_d"], aps["iota_d"],
          {k: aps[f"w_{k}"] for k in weights}, {k: aps[f"v_{k}"] for k in vectors}, out)
    result = run_bass_kernel_spmd(nc, [arrays], core_ids=[0])
    return result.results[0]["out"][:N_NODES]
```
